# Optimizing a Trainium2 kernel written in Bass

```python
import numpy as np
import jax
import jax.numpy as jnp

def _softmax(x, axis=-1):
    return jax.nn.softmax(x, axis=axis)

def _gelu(x):
    return jax.nn.gelu(x, approximate=True)

def _silu(x):
    return jax.nn.silu(x)

def _sigmoid(x):
    return jax.nn.sigmoid(x)

def _layernorm(x, axis=-1, eps=1e-05):
    m = jnp.mean(x, axis=axis, keepdims=True)
    v = jnp.var(x, axis=axis, keepdims=True)
    return (x - m) / jnp.sqrt(v + eps)

def _scatter_add(tgt, idx, src, axis=0):
    return tgt.at[idx].add(src)

def _segment_sum(src, seg, n):
    return jax.ops.segment_sum(src, seg, n)
kernel_name = 'mk_seq_preln_d2_jaxref_r8_ff4f67'

def setup_inputs(seed: int=0):
    np.random.seed(seed)
    _w = jnp.asarray

    def _L0_attn_setup():
        import jax, jax.numpy as jnp
        import numpy as np
        H = 8
        N = 16
        K = 4
        R = 8
        key = jax.random.key(seed)
        B, L, C = (4, 512, 128)
        Dh = C // H
        Di = 2 * Dh
        ks = jax.random.split(key, 8)

        def s(k, shp, fan):
            return jax.random.normal(k, shp, jnp.float32) / np.sqrt(fan)
        x = jax.random.normal(ks[0], (B, L, C), jnp.float32)
        in_proj_w = s(ks[1], (H, 2 * Di, Dh), Dh)
        conv_w = s(ks[2], (H, Di, K), K)
        conv_b = jnp.zeros((H, Di), jnp.float32)
        x_proj_w = s(ks[3], (H, R + 2 * N, Di), Di)
        dt_proj_w = s(ks[4], (H, Di, R), R)
        dt = jnp.exp(jax.random.uniform(ks[5], (H, Di)) * (np.log(0.1) - np.log(0.001)) + np.log(0.001))
        dt_proj_b = dt + jnp.log(-jnp.expm1(-dt))
        A_log = jnp.log(jnp.broadcast_to(jnp.arange(1, N + 1, dtype=jnp.float32), (H, Di, N)))
        D = jnp.ones((H, Di), jnp.float32)
        out_proj_w = s(ks[6], (H, Dh, Di), Di)
        return {'x': x, 'in_proj_w': in_proj_w, 'conv_w': conv_w, 'conv_b': conv_b, 'x_proj_w': x_proj_w, 'dt_proj_w': dt_proj_w, 'dt_proj_b': dt_proj_b, 'A_log': A_log, 'D': D, 'out_proj_w': out_proj_w}
    _L0_attn_in = _L0_attn_setup()

    def _L0_ffn_setup():
        import jax, jax.numpy as jnp
        import numpy as np
        CAPACITY_FACTOR = 1.25
        key = jax.random.key(seed)
        ks = jax.random.split(key, 6)
        B, S, H, E = (4, 512, 128, 8)
        scale = 1.0 / np.sqrt(H)
        return {'tokens': jax.random.normal(ks[0], (B, S, H), dtype=jnp.float32), 'gate_w': jax.random.normal(ks[1], (E, H), dtype=jnp.float32) * scale, 'w1': jax.random.normal(ks[2], (E, H, H), dtype=jnp.float32) * scale, 'b1': jax.random.normal(ks[3], (E, H), dtype=jnp.float32) * 0.01, 'w2': jax.random.normal(ks[4], (E, H, H), dtype=jnp.float32) * scale, 'b2': jax.random.normal(ks[5], (E, H), dtype=jnp.float32) * 0.01}
    _L0_ffn_in = _L0_ffn_setup()

    def _L1_attn_setup():
        import jax, jax.numpy as jnp
        import numpy as np
        D_MODEL = 128
        N_HEADS = 16
        SEQ = 64
        key = jax.random.key(seed)
        ks = jax.random.split(key, 12)
        B = 16
        x = jax.random.normal(ks[0], (B, SEQ, D_MODEL), dtype=jnp.float32)
        c = jax.random.normal(ks[1], (B, SEQ, 8), dtype=jnp.float32)
        s = 1.0 / np.sqrt(D_MODEL)
        Wq = jax.random.normal(ks[2], (D_MODEL, D_MODEL), dtype=jnp.float32) * s
        bq = jnp.zeros((D_MODEL,), dtype=jnp.float32)
        Wk = jax.random.normal(ks[3], (D_MODEL, D_MODEL), dtype=jnp.float32) * s
        bk = jnp.zeros((D_MODEL,), dtype=jnp.float32)
        Wv = jax.random.normal(ks[4], (D_MODEL, D_MODEL), dtype=jnp.float32) * s
        bv = jnp.zeros((D_MODEL,), dtype=jnp.float32)
        Wo = jax.random.normal(ks[5], (D_MODEL, D_MODEL), dtype=jnp.float32) * s
        bo = jnp.zeros((D_MODEL,), dtype=jnp.float32)
        rel_table = jax.random.normal(ks[6], (2 * SEQ - 1, N_HEADS), dtype=jnp.float32) * 0.02
        return {'x': x, 'c': c, 'Wq': Wq, 'bq': bq, 'Wk': Wk, 'bk': bk, 'Wv': Wv, 'bv': bv, 'Wo': Wo, 'bo': bo, 'rel_table': rel_table}
    _L1_attn_in = _L1_attn_setup()

    def _L1_ffn_setup():
        import jax, jax.numpy as jnp
        import numpy as np
        DIM = 128
        DEPTH = 6
        HEADS = 16
        DIM_HEAD = 64
        WINDOW = 32
        INNER = HEADS * DIM_HEAD
        DIM_INNER = int(DIM * 4 * 2 / 3)
        QK_SCALE = 8.0

        def shift_tokens(t):
            a, s = jnp.split(t, 2, -1)
            s = jnp.pad(s, ((0, 0), (1, 0), (0, 0)))[:, :-1]
            return jnp.concatenate([a, s], -1)

        def l2norm(t):
            return t / jnp.maximum(jnp.linalg.norm(t, axis=-1, keepdims=True), 1e-12)

        def rotate_half(x):
            x1, x2 = jnp.split(x, 2, -1)
            return jnp.concatenate([-x2, x1], -1)

        def rotary_tables(n):
            half = jnp.arange(0, DIM_HEAD, 2, dtype=jnp.float32)
            inv_freq = 1.0 / 10000.0 ** (half / DIM_HEAD)
            t = jnp.arange(n, dtype=jnp.float32)
            freqs = t[:, None] * inv_freq[None, :]
            freqs = jnp.concatenate([freqs, freqs], -1)
            base_scale = (half + 0.4 * DIM_HEAD) / (1.4 * DIM_HEAD)
            power = (t - n // 2) / (WINDOW // 2)
            scale = base_scale[None, :] ** power[:, None]
            scale = jnp.concatenate([scale, scale], -1)
            return (freqs, scale)

        def local_attention(q, k, v):
            b, h, n, d = q.shape
            w = WINDOW
            nw = n // w
            bq = q.reshape(b, h, nw, w, d)
            bk = k.reshape(b, h, nw, w, d)
            bv = v.reshape(b, h, nw, w, d)

            def look(t):
                p = jnp.pad(t, ((0, 0), (0, 0), (1, 0), (0, 0), (0, 0)))
                return jnp.concatenate([p[:, :, :nw], p[:, :, 1:]], axis=3)
            bk2, bv2 = (look(bk), look(bv))
            seq = jnp.arange(n).reshape(nw, w)
            seq_p = jnp.pad(seq, ((1, 0), (0, 0)), constant_values=-1)
            jt = jnp.concatenate([seq_p[:nw], seq_p[1:]], axis=1)
            it = seq[:, :, None]
            jb = jt[:, None, :]
            mask = (it < jb) | (it > jb + w) | (jb == -1)
            sim = jnp.einsum('bhwie,bhwje->bhwij', bq, bk2) * QK_SCALE
            sim = jnp.where(mask, -jnp.finfo(sim.dtype).max, sim)
            attn = jax.nn.softmax(sim, -1)
            out = jnp.einsum('bhwij,bhwje->bhwie', attn, bv2)
            return out.reshape(b, h, n, d)

        def attn_layer(x, Wqkv, qs, ksc, Wo):
            b, n, _ = x.shape
            qkv = x @ Wqkv
            q, k, v = jnp.split(qkv, 3, -1)
            sh = lambda t: t.reshape(b, n, HEADS, DIM_HEAD).transpose(0, 2, 1, 3)
            q, k, v = (sh(q), sh(k), sh(v))
            q = l2norm(q) * qs
            k = l2norm(k) * ksc
            freqs, scale = rotary_tables(n)
            cos, sin = (jnp.cos(freqs), jnp.sin(freqs))
            q = q * cos * scale + rotate_half(q) * sin * scale
            inv = 1.0 / scale
            k = k * cos * inv + rotate_half(k) * sin * inv
            out = local_attention(q, k, v)
            out = out.transpose(0, 2, 1, 3).reshape(b, n, INNER)
            return out @ Wo

        def ffn_layer(x, g, bln, W1, b1, W2, b2):
            mu = x.mean(-1, keepdims=True)
            var = ((x - mu) ** 2).mean(-1, keepdims=True)
            xn = (x - mu) / jnp.sqrt(var + 1e-05) * g + bln
            hg = xn @ W1 + b1
            a, gate = jnp.split(hg, 2, -1)
            return a * jax.nn.gelu(gate, approximate=False) @ W2 + b2
        key = jax.random.key(seed)
        ks = jax.random.split(key, 8)
        B, N = (2, 256)
        init = lambda k, shape: jax.random.normal(k, shape, jnp.float32) * 0.02
        return {'x': jax.random.normal(ks[0], (B, N, DIM), jnp.float32), 'Wqkv': init(ks[1], (DEPTH, DIM, 3 * INNER)), 'q_scale': jnp.ones((DEPTH, DIM_HEAD), jnp.float32), 'k_scale': jnp.ones((DEPTH, DIM_HEAD), jnp.float32), 'Wo': init(ks[2], (DEPTH, INNER, DIM)), 'ln_g': jnp.ones((DEPTH, DIM), jnp.float32), 'ln_b': jnp.zeros((DEPTH, DIM), jnp.float32), 'W1': init(ks[3], (DEPTH, DIM, 2 * DIM_INNER)), 'b1': jnp.zeros((DEPTH, 2 * DIM_INNER), jnp.float32), 'W2': init(ks[4], (DEPTH, DIM_INNER, DIM)), 'b2': jnp.zeros((DEPTH, DIM), jnp.float32)}
    _L1_ffn_in = _L1_ffn_setup()
    _d = {'L0_attn_x': _L0_attn_in['x'], 'L0_attn_in_proj_w': _L0_attn_in['in_proj_w'], 'L0_attn_conv_w': _L0_attn_in['conv_w'], 'L0_attn_conv_b': _L0_attn_in['conv_b'], 'L0_attn_x_proj_w': _L0_attn_in['x_proj_w'], 'L0_attn_dt_proj_w': _L0_attn_in['dt_proj_w'], 'L0_attn_dt_proj_b': _L0_attn_in['dt_proj_b'], 'L0_attn_A_log': _L0_attn_in['A_log'], 'L0_attn_D': _L0_attn_in['D'], 'L0_attn_out_proj_w': _L0_attn_in['out_proj_w'], 'L0_ffn_gate_w': _L0_ffn_in['gate_w'], 'L0_ffn_w1': _L0_ffn_in['w1'], 'L0_ffn_b1': _L0_ffn_in['b1'], 'L0_ffn_w2': _L0_ffn_in['w2'], 'L0_ffn_b2': _L0_ffn_in['b2'], 'L1_attn_c': _L1_attn_in['c'], 'L1_attn_Wq': _L1_attn_in['Wq'], 'L1_attn_bq': _L1_attn_in['bq'], 'L1_attn_Wk': _L1_attn_in['Wk'], 'L1_attn_bk': _L1_attn_in['bk'], 'L1_attn_Wv': _L1_attn_in['Wv'], 'L1_attn_bv': _L1_attn_in['bv'], 'L1_attn_Wo': _L1_attn_in['Wo'], 'L1_attn_bo': _L1_attn_in['bo'], 'L1_attn_rel_table': _L1_attn_in['rel_table'], 'L1_ffn_Wqkv': _L1_ffn_in['Wqkv'], 'L1_ffn_q_scale': _L1_ffn_in['q_scale'], 'L1_ffn_k_scale': _L1_ffn_in['k_scale'], 'L1_ffn_Wo': _L1_ffn_in['Wo'], 'L1_ffn_ln_g': _L1_ffn_in['ln_g'], 'L1_ffn_ln_b': _L1_ffn_in['ln_b'], 'L1_ffn_W1': _L1_ffn_in['W1'], 'L1_ffn_b1': _L1_ffn_in['b1'], 'L1_ffn_W2': _L1_ffn_in['W2'], 'L1_ffn_b2': _L1_ffn_in['b2']}
    _x0 = _d['L0_attn_x']
    _d['L0_attn_x'] = jax.random.normal(jax.random.fold_in(jax.random.key(seed), 1), (16, 256, 128), dtype=_x0.dtype)
    del _x0
    return _d

def reference(L0_attn_x, L0_attn_in_proj_w, L0_attn_conv_w, L0_attn_conv_b, L0_attn_x_proj_w, L0_attn_dt_proj_w, L0_attn_dt_proj_b, L0_attn_A_log, L0_attn_D, L0_attn_out_proj_w, L0_ffn_gate_w, L0_ffn_w1, L0_ffn_b1, L0_ffn_w2, L0_ffn_b2, L1_attn_c, L1_attn_Wq, L1_attn_bq, L1_attn_Wk, L1_attn_bk, L1_attn_Wv, L1_attn_bv, L1_attn_Wo, L1_attn_bo, L1_attn_rel_table, L1_ffn_Wqkv, L1_ffn_q_scale, L1_ffn_k_scale, L1_ffn_Wo, L1_ffn_ln_g, L1_ffn_ln_b, L1_ffn_W1, L1_ffn_b1, L1_ffn_W2, L1_ffn_b2):

    def _L0_attn_ref(x, in_proj_w, conv_w, conv_b, x_proj_w, dt_proj_w, dt_proj_b, A_log, D, out_proj_w):
        import jax, jax.numpy as jnp
        import numpy as np
        H = 8
        N = 16
        K = 4
        R = 8
        B, L, C = x.shape
        Dh = C // H
        Di = 2 * Dh
        xh = jnp.transpose(x.reshape(B, L, H, Dh), (2, 0, 1, 3))
        xz = jnp.einsum('hbld,hed->hble', xh, in_proj_w)
        u, z = (xz[..., :Di], xz[..., Di:])
        up = jnp.pad(u, ((0, 0), (0, 0), (K - 1, 0), (0, 0)))
        uc = conv_b[:, None, None, :]
        for k in range(K):
            uc = uc + up[:, :, k:k + L, :] * conv_w[:, :, k][:, None, None, :]
        uc = jax.nn.silu(uc)
        dbl = jnp.einsum('hbld,hed->hble', uc, x_proj_w)
        dt, Bm, Cm = (dbl[..., :R], dbl[..., R:R + N], dbl[..., R + N:])
        delta = jax.nn.softplus(jnp.einsum('hblr,hdr->hbld', dt, dt_proj_w) + dt_proj_b[:, None, None, :])
        A = -jnp.exp(A_log)
        d_t = jnp.moveaxis(delta, 2, 0)
        b_t = jnp.moveaxis(Bm, 2, 0)
        c_t = jnp.moveaxis(Cm, 2, 0)
        u_t = jnp.moveaxis(uc, 2, 0)
        h0 = jnp.zeros((H, B, Di, N), x.dtype)

        def step(h, inp):
            d, b, c, uu = inp
            dA = jnp.exp(d[..., None] * A[:, None, :, :])
            h = dA * h + (d * uu)[..., None] * b[:, :, None, :]
            y = jnp.sum(h * c[:, :, None, :], axis=-1)
            return (h, y)
        _, ys = jax.lax.scan(step, h0, (d_t, b_t, c_t, u_t))
        y = jnp.moveaxis(ys, 0, 2) + uc * D[:, None, None, :]
        y = y * jax.nn.silu(z)
        out = jnp.einsum('hbld,hod->hblo', y, out_proj_w)
        return jnp.transpose(out, (1, 2, 0, 3)).reshape(B, L, C)

    def _L0_ffn_ref(tokens, gate_w, w1, b1, w2, b2):
        import jax, jax.numpy as jnp
        import numpy as np
        CAPACITY_FACTOR = 1.25
        B, S, H = tokens.shape
        E = gate_w.shape[0]
        N = B * S
        cap = int(CAPACITY_FACTOR * N / E)
        x = tokens.reshape(N, H)
        probs = jax.nn.softmax(x @ gate_w.T, axis=-1)
        top2_w, top2_idx = jax.lax.top_k(probs, 2)
        a_e = top2_idx.reshape(-1)
        a_w = top2_w.reshape(-1)
        tok_id = jnp.arange(2 * N) // 2
        counts = jnp.bincount(a_e, length=E)
        keep = counts <= cap
        valid = keep[a_e]
        onehot = jax.nn.one_hot(a_e, E, dtype=jnp.int32)
        pos = jnp.take_along_axis(jnp.cumsum(onehot, axis=0) - 1, a_e[:, None], axis=1)[:, 0]
        p = jnp.where(valid, jnp.minimum(pos, cap - 1), cap)
        x_a = x[tok_id]
        buf = jnp.zeros((E, cap + 1, H), dtype=x.dtype).at[a_e, p].set(x_a)
        h = jax.nn.silu(jnp.einsum('ech,efh->ecf', buf, w1) + b1[:, None, :])
        y = jnp.einsum('ecf,egf->ecg', h, w2) + b2[:, None, :]
        contrib = y[a_e, p] * (a_w * valid.astype(x.dtype))[:, None]
        out = contrib.reshape(N, 2, H).sum(axis=1)
        return out.reshape(B, S, H)

    def _L1_attn_ref(x, c, Wq, bq, Wk, bk, Wv, bv, Wo, bo, rel_table):
        import jax, jax.numpy as jnp
        import numpy as np
        D_MODEL = 128
        N_HEADS = 16
        SEQ = 64
        B, S, D = x.shape
        H = N_HEADS
        dk = D // H
        scale = 1.0 / np.sqrt(dk)
        q = (x @ Wq + bq).reshape(B, S, H, dk)
        k = (x @ Wk + bk).reshape(B, S, H, dk)
        v = (x @ Wv + bv).reshape(B, S, H, dk)
        scores = jnp.einsum('bihd,bjhd->bhij', q, k) * scale
        rel_index = jnp.arange(S)[:, None] + jnp.arange(S - 1, -1, -1)[None, :]
        bias = rel_table[rel_index]
        scores = scores + jnp.transpose(bias, (2, 0, 1))[None]
        probs = jax.nn.softmax(scores, axis=-1)
        out = jnp.einsum('bhij,bjhd->bihd', probs, v).reshape(B, S, D)
        return out @ Wo + bo

    def _L1_ffn_ref(x, Wqkv, q_scale, k_scale, Wo, ln_g, ln_b, W1, b1, W2, b2):
        import jax, jax.numpy as jnp
        import numpy as np
        DIM = 128
        DEPTH = 6
        HEADS = 16
        DIM_HEAD = 64
        WINDOW = 32
        INNER = HEADS * DIM_HEAD
        DIM_INNER = int(DIM * 4 * 2 / 3)
        QK_SCALE = 8.0

        def shift_tokens(t):
            a, s = jnp.split(t, 2, -1)
            s = jnp.pad(s, ((0, 0), (1, 0), (0, 0)))[:, :-1]
            return jnp.concatenate([a, s], -1)

        def l2norm(t):
            return t / jnp.maximum(jnp.linalg.norm(t, axis=-1, keepdims=True), 1e-12)

        def rotate_half(x):
            x1, x2 = jnp.split(x, 2, -1)
            return jnp.concatenate([-x2, x1], -1)

        def rotary_tables(n):
            half = jnp.arange(0, DIM_HEAD, 2, dtype=jnp.float32)
            inv_freq = 1.0 / 10000.0 ** (half / DIM_HEAD)
            t = jnp.arange(n, dtype=jnp.float32)
            freqs = t[:, None] * inv_freq[None, :]
            freqs = jnp.concatenate([freqs, freqs], -1)
            base_scale = (half + 0.4 * DIM_HEAD) / (1.4 * DIM_HEAD)
            power = (t - n // 2) / (WINDOW // 2)
            scale = base_scale[None, :] ** power[:, None]
            scale = jnp.concatenate([scale, scale], -1)
            return (freqs, scale)

        def local_attention(q, k, v):
            b, h, n, d = q.shape
            w = WINDOW
            nw = n // w
            bq = q.reshape(b, h, nw, w, d)
            bk = k.reshape(b, h, nw, w, d)
            bv = v.reshape(b, h, nw, w, d)

            def look(t):
                p = jnp.pad(t, ((0, 0), (0, 0), (1, 0), (0, 0), (0, 0)))
                return jnp.concatenate([p[:, :, :nw], p[:, :, 1:]], axis=3)
            bk2, bv2 = (look(bk), look(bv))
            seq = jnp.arange(n).reshape(nw, w)
            seq_p = jnp.pad(seq, ((1, 0), (0, 0)), constant_values=-1)
            jt = jnp.concatenate([seq_p[:nw], seq_p[1:]], axis=1)
            it = seq[:, :, None]
            jb = jt[:, None, :]
            mask = (it < jb) | (it > jb + w) | (jb == -1)
            sim = jnp.einsum('bhwie,bhwje->bhwij', bq, bk2) * QK_SCALE
            sim = jnp.where(mask, -jnp.finfo(sim.dtype).max, sim)
            attn = jax.nn.softmax(sim, -1)
            out = jnp.einsum('bhwij,bhwje->bhwie', attn, bv2)
            return out.reshape(b, h, n, d)

        def attn_layer(x, Wqkv, qs, ksc, Wo):
            b, n, _ = x.shape
            qkv = x @ Wqkv
            q, k, v = jnp.split(qkv, 3, -1)
            sh = lambda t: t.reshape(b, n, HEADS, DIM_HEAD).transpose(0, 2, 1, 3)
            q, k, v = (sh(q), sh(k), sh(v))
            q = l2norm(q) * qs
            k = l2norm(k) * ksc
            freqs, scale = rotary_tables(n)
            cos, sin = (jnp.cos(freqs), jnp.sin(freqs))
            q = q * cos * scale + rotate_half(q) * sin * scale
            inv = 1.0 / scale
            k = k * cos * inv + rotate_half(k) * sin * inv
            out = local_attention(q, k, v)
            out = out.transpose(0, 2, 1, 3).reshape(b, n, INNER)
            return out @ Wo

        def ffn_layer(x, g, bln, W1, b1, W2, b2):
            mu = x.mean(-1, keepdims=True)
            var = ((x - mu) ** 2).mean(-1, keepdims=True)
            xn = (x - mu) / jnp.sqrt(var + 1e-05) * g + bln
            hg = xn @ W1 + b1
            a, gate = jnp.split(hg, 2, -1)
            return a * jax.nn.gelu(gate, approximate=False) @ W2 + b2
        for i in range(DEPTH):
            x = attn_layer(shift_tokens(x), Wqkv[i], q_scale[i], k_scale[i], Wo[i]) + x
            x = ffn_layer(shift_tokens(x), ln_g[i], ln_b[i], W1[i], b1[i], W2[i], b2[i]) + x
        return x
    x = L0_attn_x
    x = x + _L0_attn_ref(_layernorm(x, axis=-1), L0_attn_in_proj_w, L0_attn_conv_w, L0_attn_conv_b, L0_attn_x_proj_w, L0_attn_dt_proj_w, L0_attn_dt_proj_b, L0_attn_A_log, L0_attn_D, L0_attn_out_proj_w)
    x = x + _L0_ffn_ref(_layernorm(x, axis=-1), L0_ffn_gate_w, L0_ffn_w1, L0_ffn_b1, L0_ffn_w2, L0_ffn_b2)
    x = x + _L1_attn_ref(_layernorm(x, axis=-1), L1_attn_c, L1_attn_Wq, L1_attn_bq, L1_attn_Wk, L1_attn_bk, L1_attn_Wv, L1_attn_bv, L1_attn_Wo, L1_attn_bo, L1_attn_rel_table)
    x = x + _L1_ffn_ref(_layernorm(x, axis=-1), L1_ffn_Wqkv, L1_ffn_q_scale, L1_ffn_k_scale, L1_ffn_Wo, L1_ffn_ln_g, L1_ffn_ln_b, L1_ffn_W1, L1_ffn_b1, L1_ffn_W2, L1_ffn_b2)
    return x

_drawn_inputs = setup_inputs


def setup_inputs(seed=0):
    import zlib

    import numpy as np

    out = dict(_drawn_inputs(seed))
    spreads = {'L0_attn_conv_b': (0.0, 0.1),
     'L0_attn_D': (1.0, 0.2),
     'L1_attn_bq': (0.0, 0.646),
     'L1_attn_bk': (0.0, 2.0),
     'L1_attn_bv': (0.0, 0.1),
     'L1_attn_bo': (0.0, 0.1),
     'L1_ffn_q_scale': (1.0, 0.6),
     'L1_ffn_k_scale': (1.0, 0.6),
     'L1_ffn_ln_g': (1.0, 0.6),
     'L1_ffn_ln_b': (0.0, 0.8),
     'L1_ffn_b1': (0.0, 0.8),
     'L1_ffn_b2': (0.0, 0.1)}
    factors = {'L1_attn_rel_table': 47.37, 'L1_ffn_W1': 3.797, 'L1_ffn_W2': 3.723}
    for name, (base, spread) in spreads.items():
        noise = np.random.default_rng([zlib.crc32(name.encode()), seed]).standard_normal(out[name].shape)
        drawn = base * np.exp(spread * noise) if base else spread * noise
        out[name] = jnp.asarray(drawn.astype(out[name].dtype))
    for name, factor in factors.items():
        out[name] = (out[name] * factor).astype(out[name].dtype)
    return out
```

```python
import concourse.bass as bass
from concourse import mybir
from contextlib import ExitStack

F32 = mybir.dt.float32
BF16 = mybir.dt.bfloat16
ALU = mybir.AluOpType
ACT = mybir.ActivationFunctionType
AX_X = mybir.AxisListType.X

P = 128
SEQS = 16
SEQ = 256
TILES = SEQS * SEQ // P
TPS = SEQ // P
EPS = 1e-5


def need(eng, sem, value):
    if isinstance(value, int) and value <= 0:
        return
    eng.wait_ge(sem, value)


class Semaphores:

    def __init__(self, nc, prefix):
        self.nc, self.prefix, self.all = nc, prefix, []

    def __call__(self, name):
        self.all.append(self.nc.alloc_semaphore(self.prefix + name))
        return self.all[-1]

    def clear(self):
        self.nc.clear_and_free_semaphores(self.all)
        self.nc.all_engine_barrier()


class Chain:

    def __init__(self, eng, sem):
        self.eng, self.sem, self.base, self.k, self.i, self.per = eng, sem, 0, 0, 0, 0

    def turn(self, i, per):
        if self.k and self.per == 0:
            self.base += self.k
        if self.per:
            assert self.k == self.per, (self.k, self.per)
        self.i, self.per, self.k = i, per, 0

    def end(self, turns):
        if self.per:
            assert self.k == self.per, (self.k, self.per)
        self.base += turns * self.per
        self.i, self.per, self.k = 0, 0, 0

    def now(self):
        return self.base + self.i * self.per + self.k

    def step(self, ins):
        ins.then_inc(self.sem, 1)
        self.k += 1

    def wait(self):
        self.eng.wait_ge(self.sem, self.now())

    def link(self, ins):
        self.step(ins)
        self.wait()


def identity(nc, ctx, name="ident"):
    ident = ctx.enter_context(nc.sbuf_tensor(name, [P, P], F32))
    zeroed = ctx.enter_context(nc.semaphore(name + "_zeroed"))
    with nc.Block() as block:
        @block.gpsimd
        def _(pool):
            nc.gpsimd.memset(ident[:, :], 0.0).then_inc(zeroed, 1)
            pool.wait_ge(zeroed, 1)
            nc.gpsimd.affine_select(out=ident[:, :], in_=ident[:, :], compare_op=ALU.not_equal, fill=1.0,
                                    base=0, pattern=[[-1, P]], channel_multiplier=1).then_inc(zeroed, 1)
            pool.wait_ge(zeroed, 2)
    return ident


def layernorm_stats(nc, X, mean, rstd, tag):
    with ExitStack() as ctx:
        def sb(name, shape):
            return ctx.enter_context(nc.sbuf_tensor(f"{name}_{tag}", shape, F32))

        stats = sb("stats", [P, TILES, 6])
        spread = sb("spread", [P, TILES])
        var = sb("var", [P, TILES])
        half = sb("half", [P, TILES])
        sem = Semaphores(nc, tag + "_")
        stats_done, ln_steps, var_ready, half_set = sem("stats_done"), sem("ln_steps"), sem("var_ready"), sem("half_set")
        with nc.Block() as block:
            @block.vector
            def _(dve):
                with dve.Fori(0, TILES) as t:
                    nc.vector.bn_stats(stats[:, bass.ds(t, 1), :], X[:, bass.ds(t, 1), :]).then_inc(stats_done, 1)
                dve.wait_ge(stats_done, TILES)
                c = Chain(dve, ln_steps)
                me, qe, mo, qo = (stats[:, :, k] for k in (1, 2, 4, 5))
                nc.vector.tensor_tensor(mean[:, :], me, mo, ALU.add).then_inc(ln_steps, 1)
                nc.vector.tensor_tensor(spread[:, :], me, mo, ALU.subtract).then_inc(ln_steps, 1)
                nc.vector.tensor_tensor(var[:, :], qe, qo, ALU.add).then_inc(ln_steps, 1)
                c.k = 3
                c.wait()
                c.step(nc.vector.tensor_scalar(mean[:, :], mean[:, :], 0.5, None, ALU.mult))
                c.step(nc.vector.tensor_tensor(spread[:, :], spread[:, :], spread[:, :], ALU.mult))
                c.link(nc.vector.tensor_scalar(var[:, :], var[:, :], 1.0 / P, EPS, ALU.mult, ALU.add))
                c.wait()
                nc.vector.scalar_tensor_tensor(out=var[:, :], in0=spread[:, :], scalar=0.25, in1=var[:, :],
                                               op0=ALU.mult, op1=ALU.add).then_inc(var_ready, 1)
                dve.wait_ge(var_ready, 1)

            @block.gpsimd
            def _(pool):
                nc.gpsimd.memset(half[:, :], -0.5).then_inc(half_set, 1)
                pool.wait_ge(half_set, 1)
                pool.wait_ge(var_ready, 1)
                nc.gpsimd.tensor_tensor(rstd[:, :], var[:, :], half[:, :], ALU.pow).then_inc(half_set, 1)
                pool.wait_ge(half_set, 2)
        sem.clear()


def selective_scan(nc, X, ident, in_w, conv_w, conv_b, xp_w, dt_w, dt_b, a_log, d_skip, out_w):
    H, DH, DI, N, K, R = 8, 16, 32, 16, 4, 8
    G, HG = 2, 4
    TOK = SEQS * SEQ
    NC_ = 4
    CHUNKS = N // NC_
    W = NC_ * SEQ
    with ExitStack() as ctx:
        def sb(name, shape):
            return ctx.enter_context(nc.sbuf_tensor("m_" + name, shape, F32))

        sem = Semaphores(nc, "m_")

        mean, rstd = sb("mean", [P, TILES]), sb("rstd", [P, TILES])
        layernorm_stats(nc, X, mean, rstd, "m")
        Wu = sb("Wu", [P, G, P])
        Wz = sb("Wz", [P, G, P])
        xpw = sb("xpw", [P, G, R + 2 * N])
        Wdx = sb("Wdx", [P, G, HG * R])
        WBC = sb("WBC", [P, G, 2 * N, P])
        Wdt = sb("Wdt", [R * HG, G, P])
        Wo = sb("Wo", [P, G, HG * DH])
        convw, convb, dtb, dsk = sb("convw", [P, G, K]), sb("convb", [P, G]), sb("dtb", [P, G]), sb("dsk", [P, G])
        A = sb("A", [P, G, N])
        UC = sb("UC", [P, G, TOK])
        ZS = sb("ZS", [P, G, TOK])
        DELTA = sb("DELTA", [P, G, TOK])
        zeroed, loaded, a_ready = sem("zeroed"), sem("loaded"), sem("a_ready")
        a_ready_n, placed = sem("a_negated"), sem("placed")
        LOADS = 16 * (6 + 4 * H)
        with nc.Block() as block:
            @block.vector
            def _(dve):
                for w in (Wu[:, :, :], Wz[:, :, :], Wdt[:, :, :], Wo[:, :, :], Wdx[:, :, :], WBC[:, :, :, :]):
                    nc.vector.memset(w, 0.0).then_inc(zeroed, 1)
                dve.wait_ge(zeroed, 6)
                dve.wait_ge(loaded, LOADS)
                for h in range(H):
                    g, hh = divmod(h, HG)
                    rows = slice(DI * hh, DI * hh + DI)
                    nc.vector.tensor_copy(Wdx[rows, g, R * hh:R * hh + R], xpw[rows, g, 0:R]).then_inc(placed, 1)
                    nc.vector.tensor_copy(WBC[rows, g, :, rows], xpw[rows, g, R:].unsqueeze(2).to_broadcast(
                        [DI, 2 * N, DI])).then_inc(placed, 1)
                dve.wait_ge(placed, 2 * H)
                dve.wait_ge(a_ready, 1)
                nc.vector.tensor_scalar(A[:, :, :], A[:, :, :], -1.0, None, ALU.mult).then_inc(a_ready_n, 1)
                dve.wait_ge(a_ready_n, 1)

            @block.sync
            def _(sp):
                n = 0
                for dst, src in ((convw[:, :, :], conv_w.rearrange("(g h) d k -> (h d) g k", g=G)),
                                 (A[:, :, :], a_log.rearrange("(g h) d n -> (h d) g n", g=G)),
                                 (xpw[:, :, :], xp_w.rearrange("(g h) d e -> (h d) g e", g=G))):
                    sp.dma_start(dst, src).then_inc(loaded, 16)
                    n += 1
                for dst, src in ((convb, conv_b), (dtb, dt_b), (dsk, d_skip)):
                    with nc.allow_non_contiguous_dma(reason="small"):
                        sp.dma_start(dst[:, :], src.rearrange("(g h) d -> (h d) g", g=G)).then_inc(loaded, 16)
                    n += 1
                sp.wait_ge(zeroed, 6)
                for h in range(H):
                    g, hh = divmod(h, HG)
                    rows, cols = slice(DH * h, DH * h + DH), slice(DI * hh, DI * hh + DI)
                    for dst, src in ((Wu[rows, g, cols], in_w[h, :, 0:DI]), (Wz[rows, g, cols], in_w[h, :, DI:2 * DI]),
                                     (Wdt[R * hh:R * hh + R, g, cols], dt_w[h]),
                                     (Wo[cols, g, DH * hh:DH * hh + DH], out_w[h])):
                        with nc.allow_non_contiguous_dma(reason="small"):
                            sp.dma_start(dst, src).then_inc(loaded, 16)
                        n += 1
                assert 16 * n == LOADS
                sp.wait_ge(loaded, LOADS)

            @block.scalar
            def _(act):
                act.wait_ge(loaded, LOADS)
                nc.scalar.activation(A[:, :, :], A[:, :, :], ACT.Exp).then_inc(a_ready, 1)

        with ExitStack() as inner:
            def isb(name, shape):
                return inner.enter_context(nc.sbuf_tensor("m1_" + name, shape, F32))

            def ips(name, cols):
                return inner.enter_context(nc.psum_tensor("m1_" + name, [P, cols], F32))

            xn = isb("xn", [P, TPS, P])
            xnT = isb("xnT", [P, SEQ])
            up = isb("up", [P, G, K - 1 + SEQ])
            cv = isb("cv", [P, G, SEQ])
            dts = isb("dts", [R * HG, G, SEQ])
            ps_x, ps_u, ps_z = ips("ps_x", SEQ), ips("ps_u", G * SEQ), ips("ps_z", G * SEQ)
            ps_d, ps_e = ips("ps_d", G * SEQ), ips("ps_e", G * SEQ)
            normed, turned, xnt_ready = sem("normed"), sem("turned"), sem("xnt_ready")
            projected, u_ready, z_used, conv_steps = sem("projected"), sem("u_ready"), sem("z_used"), sem("conv_steps")
            conv_ready, uc_ready, dt_made, dt_ready = sem("conv_ready"), sem("uc_ready"), sem("dt_made"), sem("dt_ready")
            raw_made, raw_ready, pads = sem("raw_made"), sem("raw_ready"), sem("pads")
            with nc.Block() as block:
                @block.vector
                def _(dve):
                    nc.vector.memset(up[:, :, 0:K - 1], 0.0).then_inc(pads, 1)
                    dve.wait_ge(pads, 1)
                    c = Chain(dve, conv_steps)

                    def turn(b):
                        c.turn(b, K - 1)
                        need(dve, turned, b)
                        for t in range(TPS):
                            at = bass.ds(b * TPS + t, 1)
                            nc.vector.tensor_scalar(xn[:, t, :], X[:, at, :].rearrange("p a c -> p (a c)"),
                                                    mean[:, at], rstd[:, at],
                                                    ALU.subtract, ALU.mult).then_inc(normed, 1)
                        dve.wait_ge(u_ready, b + 1)
                        need(dve, uc_ready, b)
                        for k in reversed(range(K)):
                            for g in range(G):
                                tap = up[:, g, k:k + SEQ]
                                if k == K - 1:
                                    ins = nc.vector.tensor_scalar(cv[:, g, :], tap, convw[:, g, k:k + 1],
                                                                  convb[:, g:g + 1], ALU.mult, ALU.add)
                                else:
                                    ins = nc.vector.scalar_tensor_tensor(out=cv[:, g, :], in0=tap,
                                                                         scalar=convw[:, g, k:k + 1],
                                                                         in1=cv[:, g, :], op0=ALU.mult, op1=ALU.add)
                            if k:
                                c.link(ins)
                            else:
                                ins.then_inc(conv_ready, 1)

                    turn(0)
                    with dve.Fori(1, SEQS) as b:
                        turn(b)

                @block.tensor
                def _(pe):
                    def turn(b):
                        pe.wait_ge(normed, TPS * b + TPS)
                        need(pe, xnt_ready, b)
                        for t in range(TPS):
                            ins = nc.tensor.transpose(ps_x[:, t * P:t * P + P], xn[:, t, :], ident[:, :])
                        ins.then_inc(turned, 1)
                        pe.wait_ge(xnt_ready, b + 1)
                        need(pe, u_ready, b)
                        need(pe, z_used, b)
                        for dst, w in ((ps_u, Wu), (ps_z, Wz)):
                            for g in range(G):
                                ins = nc.tensor.matmul(dst[:, g * SEQ:g * SEQ + SEQ], w[:, g, :], xnT[:, :],
                                                       start=True, stop=True)
                        ins.then_inc(projected, 1)
                        pe.wait_ge(uc_ready, b + 1)
                        need(pe, dt_ready, b)
                        for g in range(G):
                            ins = nc.tensor.matmul(ps_d[0:R * HG, g * SEQ:g * SEQ + SEQ],
                                                   Wdx[:, g, :],
                                                   UC[:, g, bass.ds(b * SEQ, SEQ)], start=True, stop=True)
                        ins.then_inc(dt_made, 1)
                        pe.wait_ge(dt_ready, b + 1)
                        need(pe, raw_ready, b)
                        for g in range(G):
                            ins = nc.tensor.matmul(ps_e[:, g * SEQ:g * SEQ + SEQ], Wdt[:, g, :], dts[:, g, :],
                                                   start=True, stop=True)
                        ins.then_inc(raw_made, 1)

                    turn(0)
                    with pe.Fori(1, SEQS) as b:
                        turn(b)

                @block.scalar
                def _(act):
                    def turn(b):
                        at = bass.ds(b * SEQ, SEQ)
                        act.wait_ge(turned, b + 1)
                        need(act, projected, b)
                        nc.scalar.copy(xnT[:, :], ps_x[:, :]).then_inc(xnt_ready, 1)
                        act.wait_ge(projected, b + 1)
                        need(act, conv_ready, b)
                        if isinstance(b, int) and b == 0:
                            act.wait_ge(pads, 1)
                        nc.scalar.copy(up[:, :, K - 1:], ps_u[:, :].rearrange("p (g l) -> p g l", g=G)).then_inc(u_ready, 1)
                        nc.scalar.activation(ZS[:, :, at], ps_z[:, :].rearrange("p (g l) -> p g l", g=G),
                                             ACT.Silu).then_inc(z_used, 1)
                        act.wait_ge(conv_ready, b + 1)
                        nc.scalar.activation(UC[:, :, at], cv[:, :, :], ACT.Silu).then_inc(uc_ready, 1)
                        act.wait_ge(dt_made, b + 1)
                        need(act, raw_made, b)
                        nc.scalar.copy(dts[:, :, :], ps_d[0:R * HG, :].rearrange("p (g l) -> p g l", g=G)).then_inc(dt_ready, 1)
                        act.wait_ge(raw_made, b + 1)
                        for g in range(G):
                            ins = nc.scalar.activation(DELTA[:, g, at], ps_e[:, g * SEQ:g * SEQ + SEQ],
                                                       ACT.Identity, bias=dtb[:, g:g + 1])
                        ins.then_inc(raw_ready, 1)

                    turn(0)
                    with act.Fori(1, SEQS) as b:
                        turn(b)

        with ExitStack() as inner:
            PIECE = 2048
            PIECES = G * TOK // PIECE
            tail = [inner.enter_context(nc.sbuf_tensor(f"m2_tail{i}", [P, PIECE], F32)) for i in range(2)]
            flat = DELTA[:, :, :].rearrange("p g t -> p (g t)")
            abs_done, exp_done, ln_ready, sp_done = sem("abs_done"), sem("exp_done"), sem("ln_ready"), sem("sp_done")
            with nc.Block() as block:
                @block.scalar
                def _(act):
                    for i in range(PIECES):
                        at, v = slice(i * PIECE, (i + 1) * PIECE), tail[i % 2][:, :]
                        need(act, sp_done, i - 1)
                        nc.scalar.activation(v, flat[:, at], ACT.Abs).then_inc(abs_done, 1)
                        act.wait_ge(abs_done, i + 1)
                        nc.scalar.activation(v, v, ACT.Exp, scale=-1.0).then_inc(exp_done, 1)
                        act.wait_ge(exp_done, i + 1)
                        nc.scalar.activation(v, v, ACT.Ln, bias=1.0).then_inc(ln_ready, 1)

                @block.vector
                def _(dve):
                    for i in range(PIECES):
                        at, v = slice(i * PIECE, (i + 1) * PIECE), tail[i % 2][:, :]
                        dve.wait_ge(ln_ready, i + 1)
                        nc.vector.scalar_tensor_tensor(out=flat[:, at], in0=flat[:, at], scalar=0.0, in1=v,
                                                       op0=ALU.max, op1=ALU.add).then_inc(sp_done, 1)

        with ExitStack() as inner:
            def isb(name, shape):
                return inner.enter_context(nc.sbuf_tensor("m3_" + name, shape, F32))

            def ips(name, cols):
                return inner.enter_context(nc.psum_tensor("m3_" + name, [P, cols], F32))

            UNITS = G * CHUNKS
            POOL = 2
            dA = [isb(f"dA{i}", [P, NC_, SEQ]) for i in range(2)]
            dBu = isb("dBu", [P, NC_, SEQ])
            hs = isb("hs", [P, NC_, SEQ])
            hc = [isb(f"hc{i}", [P, NC_, SEQ]) for i in range(2)]
            du = isb("du", [P, SEQ])
            part = isb("part", [P, 2, SEQ])
            ysum = isb("ysum", [P, G, SEQ])
            yT = isb("yT", [P, G, SEQ])
            ps_B = [ips(f"ps_B{i}", W) for i in range(2)]
            ps_C = ips("ps_C", W)
            ps_o = ips("ps_o", TPS * P)
            dA_zero, B_ready, C_ready, dA_ready = sem("dA_zero"), sem("B_ready"), sem("C_ready"), sem("dA_ready")
            du_ready, dBu_done, scan_done, hc_ready = sem("du_ready"), sem("dBu_done"), sem("scan_done"), sem("hc_ready")
            pool_steps, y_partial, y_ready = sem("pool_steps"), sem("y_partial"), sem("y_ready")
            alone = sem("alone")
            y_steps, out_made, x_added = sem("y_steps"), sem("out_made"), sem("x_added")

            with nc.Block() as block:
                @block.tensor
                def _(pe):
                    def out_proj(b):
                        pe.wait_ge(y_ready, G * b + G)
                        need(pe, x_added, b)
                        for t in range(TPS):
                            for g in range(G):
                                o = t * P + g * HG * DH
                                ins = nc.tensor.matmul(ps_o[:, o:o + HG * DH], yT[:, g, t * P:t * P + P], Wo[:, g, :],
                                                       start=True, stop=True)
                        ins.then_inc(out_made, 1)

                    def turn(b, first):
                        seq = bass.ds(b * SEQ, SEQ)
                        for u in range(UNITS):
                            g, c = divmod(u, CHUNKS)
                            n = UNITS * b + u
                            need(pe, dBu_done, n - 1)
                            for ps, column, done in ((ps_B[u % 2], 0, B_ready), (ps_C, N, C_ready)):
                                if done is C_ready:
                                    need(pe, hc_ready, n)
                                for j in range(NC_):
                                    ins = nc.tensor.matmul(ps[:, j * SEQ:j * SEQ + SEQ],
                                                           WBC[:, g, column + NC_ * c + j, :], UC[:, g, seq],
                                                           start=True, stop=True)
                                ins.then_inc(done, 1)
                            if u == 1 and not first:
                                out_proj(b - 1)

                    turn(0, True)
                    turn(1, False)
                    with pe.Fori(2, SEQS) as b:
                        turn(b, False)
                    out_proj(SEQS - 1)

                @block.scalar
                def _(act):
                    act.wait_ge(dA_zero, 2)

                    def turn(b):
                        rest = bass.ds(b * SEQ + 1, SEQ - 1)
                        for u in range(UNITS):
                            g, c = divmod(u, CHUNKS)
                            need(act, scan_done, UNITS * b + u - 1)
                            act.sem_inc(alone, 1)
                            for j in range(NC_):
                                s = NC_ * c + j
                                ins = nc.scalar.activation(dA[u % 2][:, j, 1:], DELTA[:, g, rest], ACT.Exp,
                                                           scale=A[:, g, s:s + 1])
                            ins.then_inc(dA_ready, 1)

                    turn(0)
                    with act.Fori(1, SEQS) as b:
                        turn(b)

                @block.vector
                def _(dve):
                    for i in range(2):
                        nc.vector.memset(dA[i][:, :, 0:1], 0.0).then_inc(dA_zero, 1)
                    dve.wait_ge(dA_zero, 2)
                    c2 = Chain(dve, y_steps)

                    def gate(b, g):
                        seq = bass.ds(b * SEQ, SEQ)
                        dve.wait_ge(y_partial, (CHUNKS - 1) * (G * b + g + 1))
                        need(dve, out_made, b)
                        c2.link(nc.vector.scalar_tensor_tensor(out=yT[:, g, :], in0=UC[:, g, seq], scalar=dsk[:, g:g + 1],
                                                               in1=ysum[:, g, :], op0=ALU.mult, op1=ALU.add))
                        nc.vector.tensor_tensor(yT[:, g, :], yT[:, g, :], ZS[:, g, seq], ALU.mult).then_inc(y_ready, 1)

                    def add_out(b):
                        dve.wait_ge(out_made, b + 1)
                        tiles = bass.ds(b * TPS, TPS)
                        nc.vector.tensor_tensor(X[:, tiles, :], X[:, tiles, :],
                                                ps_o[:, :].rearrange("p (t c) -> p t c", t=TPS), ALU.add).then_inc(x_added, 1)

                    def turn(b, first):
                        seq = bass.ds(b * SEQ, SEQ)
                        for u in range(UNITS):
                            g, c = divmod(u, CHUNKS)
                            n = UNITS * b + u
                            if c == 0:
                                need(dve, dBu_done, n)
                                nc.vector.tensor_tensor(du[:, :], DELTA[:, g, seq], UC[:, g, seq], ALU.mult).then_inc(du_ready, 1)
                                dve.wait_ge(du_ready, G * b + g + 1)
                            dve.wait_ge(B_ready, n + 1)
                            need(dve, scan_done, n)
                            nc.vector.tensor_tensor(dBu[:, :, :], ps_B[u % 2][:, :].rearrange("p (j l) -> p j l", j=NC_),
                                                    du[:, :].unsqueeze(1).to_broadcast([P, NC_, SEQ]),
                                                    ALU.mult).then_inc(dBu_done, 1)
                            dve.wait_ge(dBu_done, n + 1)
                            dve.wait_ge(dA_ready, n + 1)
                            need(dve, hc_ready, n)
                            nc.vector.tensor_tensor_scan(hs[:, :, :].rearrange("p j l -> p (j l)"),
                                                         dA[u % 2][:, :, :].rearrange("p j l -> p (j l)"),
                                                         dBu[:, :, :].rearrange("p j l -> p (j l)"), 0.0,
                                                         ALU.mult, ALU.add).then_inc(scan_done, 1)
                            dve.wait_ge(scan_done, n + 1)
                            dve.wait_ge(C_ready, n + 1)
                            need(dve, pool_steps, POOL * (n - 1))
                            nc.vector.tensor_tensor(hc[u % 2][:, :, :], ps_C[:, :].rearrange("p (j l) -> p j l", j=NC_),
                                                    hs[:, :, :], ALU.mult).then_inc(hc_ready, 1)
                            if u == CHUNKS:
                                gate(b, 0)
                            if u == 0 and not first:
                                gate(b - 1, 1)
                            if u == 2 and not first:
                                add_out(b - 1)

                    c2.turn(0, 1)
                    turn(0, True)
                    c2.end(1)
                    c2.turn(0, 2)
                    turn(1, False)
                    c2.end(1)
                    with dve.Fori(2, SEQS) as b:
                        c2.turn(b - 2, 2)
                        turn(b, False)
                    c2.end(SEQS - 2)
                    gate(SEQS - 1, 1)
                    add_out(SEQS - 1)
                    dve.wait_ge(x_added, SEQS)

                @block.gpsimd
                def _(pool):
                    def turn(b):
                        for u in range(UNITS):
                            g, c = divmod(u, CHUNKS)
                            n = UNITS * b + u
                            pool.wait_ge(hc_ready, n + 1)
                            if c == 0:
                                need(pool, y_ready, G * (b - 1) + g + 1 if not isinstance(b, int) or b else 0)
                            v = hc[u % 2]
                            nc.gpsimd.tensor_tensor(part[:, :, :], v[:, 0:2, :], v[:, 2:4, :], ALU.add).then_inc(pool_steps, 1)
                            pool.wait_ge(pool_steps, POOL * n + 1)
                            if c == 0:
                                nc.gpsimd.tensor_tensor(ysum[:, g, :], part[:, 0, :], part[:, 1, :], ALU.add).then_inc(pool_steps, 1)
                                pool.wait_ge(pool_steps, POOL * n + 2)
                            else:
                                nc.gpsimd.tensor_tensor(part[:, 0, :], part[:, 0, :], part[:, 1, :], ALU.add).then_inc(pool_steps, 1)
                                pool.wait_ge(pool_steps, POOL * n + 2)
                                ins = nc.gpsimd.tensor_tensor(ysum[:, g, :], ysum[:, g, :], part[:, 0, :], ALU.add)
                                ins.then_inc(y_partial, 1)
                                pool.wait_ge(y_partial, (CHUNKS - 1) * (G * b + g) + c)

                    turn(0)
                    with pool.Fori(1, SEQS) as b:
                        turn(b)
        sem.clear()


def expert_layer(nc, X, ident, gate_w, w1, b1, w2, b2):
    E = 8
    CAP = int(1.25 * SEQS * SEQ / E)
    TG = 4
    GROUPS = TILES // TG
    with ExitStack() as ctx:
        def sb(name, shape):
            return ctx.enter_context(nc.sbuf_tensor("e_" + name, shape, F32))

        def ps(name, cols):
            return ctx.enter_context(nc.psum_tensor("e_" + name, [P, cols], F32))

        sem = Semaphores(nc, "e_")

        mean, rstd = sb("mean", [P, TILES]), sb("rstd", [P, TILES])
        layernorm_stats(nc, X, mean, rstd, "e")
        W1, W2 = sb("W1", [P, E, P]), sb("W2", [P, E, P])
        B1, B2, Wg = sb("B1", [P, E]), sb("B2", [E, P]), sb("Wg", [P, E])
        XT = sb("XT", [P, SEQS, SEQ])
        xn = sb("xn", [P, TPS, P])
        xw = sb("xw", [P, SEQ])
        L = sb("L", [P, TILES, E])
        top, total = sb("top", [P, TILES]), sb("total", [P, TILES])
        above, level = sb("above", [P, TILES, E, E]), sb("level", [P, TILES, E, E])
        earlier = sb("earlier", [P, E, E])
        rank = sb("rank", [P, TILES, E])
        counts, keep, ones = sb("counts", [P, E]), sb("keep", [P, E]), sb("ones", [P, P])
        gw = sb("gw", [P, TG, E])
        gT = sb("gT", [E, TG * P])
        h = [sb(f"h{i}", [P, TG * P]) for i in range(2)]
        ps_x, ps_l, ps_c = ps("ps_x", 512), ps("ps_l", 512), ps("ps_c", 512)
        ps_h = [ps(f"ps_h{i}", 512) for i in range(2)]
        ps_y = [ps(f"ps_y{i}", 512) for i in range(2)]
        ps_b = ps("ps_b", 512)
        loaded, normed, turned, xw_ready, xt_ready = (sem(s) for s in ("loaded", "normed", "turned", "xw_ready", "xt_ready"))
        logits_made, logits_ready, pick, exp_done = (sem(s) for s in ("logits_made", "logits_ready", "pick", "exp_done"))
        counted, summed, consts = sem("counted"), sem("summed"), sem("consts")
        h_made, h_ready, y_made, y_added = sem("h_made"), sem("h_ready"), sem("y_made"), sem("y_added")
        gt_made, gt_ready, bias_made, bias_added = sem("gt_made"), sem("gt_ready"), sem("bias_made"), sem("bias_added")
        weighted, gw_ready = sem("weighted"), sem("gw_ready")

        with nc.Block() as block:
            @block.sync
            def _(sp):
                for dst, src in ((W1[:, :, :], w1.rearrange("e h f -> h e f")), (W2[:, :, :], w2.rearrange("e f g -> f e g")),
                                 (B1[:, :], b1), (B2[:, :], b2), (Wg[:, :], gate_w)):
                    sp.dma_start(dst, src).then_inc(loaded, 16)

            @block.gpsimd
            def _(pool):
                nc.gpsimd.memset(ones[:, :], 1.0).then_inc(consts, 1)
                nc.gpsimd.memset(earlier[:, :, :], 0.0).then_inc(consts, 1)
                pool.wait_ge(consts, 2)
                for e in range(1, E):
                    nc.gpsimd.memset(earlier[:, e, 0:e], 1.0).then_inc(consts, 1)

                def turn(b):
                    pool.wait_ge(xw_ready, b + 1)
                    nc.gpsimd.tensor_copy(XT[:, bass.ds(b, 1), :].rearrange("p a l -> p (a l)"), xw[:, :]).then_inc(xt_ready, 1)

                with pool.Fori(0, SEQS) as b:
                    turn(b)
                pool.wait_ge(weighted, 1)

                def group(r):
                    need(pool, gt_made, r)
                    nc.gpsimd.tensor_copy(gw[:, :, :], L[:, bass.ds(r * TG, TG), :]).then_inc(gw_ready, 1)

                group(0)
                with pool.Fori(1, GROUPS) as r:
                    group(r)

            @block.vector
            def _(dve):
                def turn(b):
                    need(dve, turned, b)
                    for t in range(TPS):
                        at = bass.ds(b * TPS + t, 1)
                        nc.vector.tensor_scalar(xn[:, t, :], X[:, at, :].rearrange("p a c -> p (a c)"),
                                                mean[:, at], rstd[:, at], ALU.subtract, ALU.mult).then_inc(normed, 1)
                    dve.wait_ge(logits_made, b + 1)
                    nc.vector.tensor_copy(L[:, bass.ds(b * TPS, TPS), :],
                                          ps_l[:, 0:TPS * E].rearrange("p (t e) -> p t e", t=TPS)).then_inc(logits_ready, 1)

                turn(0)
                with dve.Fori(1, SEQS) as b:
                    turn(b)
                dve.wait_ge(logits_ready, SEQS)
                dve.wait_ge(consts, 2 + E - 1)
                c = Chain(dve, pick)
                per_token = lambda v: v[:, :].unsqueeze(2).to_broadcast([P, TILES, E])
                c.link(nc.vector.tensor_reduce(top[:, :], L[:, :, :], AX_X, ALU.max))
                c.link(nc.vector.tensor_tensor(L[:, :, :], L[:, :, :], per_token(top), ALU.subtract))
                dve.wait_ge(exp_done, 1)
                c.link(nc.vector.tensor_reduce(total[:, :], L[:, :, :], AX_X, ALU.add))
                c.link(nc.vector.reciprocal(total[:, :], total[:, :]))
                c.link(nc.vector.tensor_tensor(L[:, :, :], L[:, :, :], per_token(total), ALU.mult))
                mine = L[:, :, :].unsqueeze(3).to_broadcast([P, TILES, E, E])
                other = L[:, :, :].unsqueeze(2).to_broadcast([P, TILES, E, E])
                c.step(nc.vector.tensor_tensor(above[:, :, :, :], other, mine, ALU.is_gt))
                c.link(nc.vector.tensor_tensor(level[:, :, :, :], other, mine, ALU.is_equal))
                c.link(nc.vector.tensor_tensor(
                    level[:, :, :, :].rearrange("p t e f -> p t (e f)"), level[:, :, :, :].rearrange("p t e f -> p t (e f)"),
                    earlier[:, :, :].rearrange("p e f -> p (e f)").unsqueeze(1).to_broadcast([P, TILES, E * E]), ALU.mult))
                c.link(nc.vector.tensor_tensor(above[:, :, :, :], above[:, :, :, :], level[:, :, :, :], ALU.add))
                c.link(nc.vector.tensor_reduce(rank[:, :, :], above[:, :, :, :], AX_X, ALU.add))
                c.link(nc.vector.tensor_scalar(rank[:, :, :], rank[:, :, :], 1.5, None, ALU.is_lt))
                nc.vector.tensor_reduce(counts[:, :], rank[:, :, :].rearrange("p t e -> p e t"), AX_X,
                                        ALU.add).then_inc(counted, 1)
                c.link(nc.vector.tensor_tensor(L[:, :, :], L[:, :, :], rank[:, :, :], ALU.mult))
                dve.wait_ge(summed, 1)
                c.link(nc.vector.tensor_scalar(keep[:, :], ps_c[:, 0:E], CAP + 0.5, None, ALU.is_lt))
                nc.vector.tensor_tensor(L[:, :, :], L[:, :, :], keep[:, :].unsqueeze(1).to_broadcast([P, TILES, E]),
                                        ALU.mult).then_inc(weighted, 1)
                dve.wait_ge(weighted, 1)

                def experts(r):
                    for e in range(E):
                        n = E * r + e
                        dve.wait_ge(y_made, n + 1)
                        if e:
                            dve.wait_ge(y_added, TG * n)
                        else:
                            need(dve, bias_added, r)
                        for t in range(TG):
                            row = X[:, bass.ds(r * TG + t, 1), :].rearrange("p a c -> p (a c)")
                            weight = L[:, bass.ds(r * TG + t, 1), e]
                            nc.vector.scalar_tensor_tensor(out=row, in0=ps_y[e % 2][:, t * P:t * P + P], scalar=weight,
                                                           in1=row, op0=ALU.mult, op1=ALU.add).then_inc(y_added, 1)
                    dve.wait_ge(bias_made, r + 1)
                    dve.wait_ge(y_added, TG * (E * r + E))
                    rows = X[:, bass.ds(r * TG, TG), :]
                    nc.vector.tensor_tensor(rows, rows, ps_b[:, :].rearrange("p (t c) -> p t c", t=TG),
                                            ALU.add).then_inc(bias_added, 1)

                experts(0)
                with dve.Fori(1, GROUPS) as r:
                    experts(r)
                dve.wait_ge(bias_added, GROUPS)

            @block.scalar
            def _(act):
                def turn(b):
                    act.wait_ge(turned, b + 1)
                    need(act, logits_made, b)
                    need(act, xt_ready, b)
                    nc.scalar.copy(xw[:, :], ps_x[:, 0:SEQ]).then_inc(xw_ready, 1)

                turn(0)
                with act.Fori(1, SEQS) as b:
                    turn(b)
                act.wait_ge(pick, 2)
                nc.scalar.activation(L[:, :, :], L[:, :, :], ACT.Exp).then_inc(exp_done, 1)
                act.wait_ge(loaded, 16 * 5)

                def experts(r):
                    for e in range(E):
                        n = E * r + e
                        act.wait_ge(h_made, n + 1)
                        need(act, y_made, n - 1)
                        nc.scalar.activation(h[e % 2][:, :], ps_h[e % 2][:, :], ACT.Silu, bias=B1[:, e:e + 1]).then_inc(h_ready, 1)
                    act.wait_ge(gt_made, r + 1)
                    need(act, bias_made, r)
                    nc.scalar.copy(gT[:, :], ps_x[0:E, :]).then_inc(gt_ready, 1)

                experts(0)
                with act.Fori(1, GROUPS) as r:
                    experts(r)

            @block.tensor
            def _(pe):
                pe.wait_ge(loaded, 16 * 5)

                def turn(b):
                    pe.wait_ge(normed, TPS * b + TPS)
                    need(pe, xw_ready, b)
                    for t in range(TPS):
                        ins = nc.tensor.transpose(ps_x[:, t * P:t * P + P], xn[:, t, :], ident[:, :])
                    ins.then_inc(turned, 1)
                    pe.wait_ge(xw_ready, b + 1)
                    need(pe, logits_ready, b)
                    for t in range(TPS):
                        ins = nc.tensor.matmul(ps_l[:, t * E:t * E + E], xw[:, t * P:t * P + P], Wg[:, :],
                                               start=True, stop=True)
                    ins.then_inc(logits_made, 1)

                turn(0)
                with pe.Fori(1, SEQS) as b:
                    turn(b)
                pe.wait_ge(counted, 1)
                nc.tensor.matmul(ps_c[:, 0:E], ones[:, :], counts[:, :], start=True, stop=True).then_inc(summed, 1)
                pe.wait_ge(xt_ready, SEQS)
                pe.wait_ge(weighted, 1)

                def first(r, e):
                    n = E * r + e
                    need(pe, h_ready, n - 1)
                    nc.tensor.matmul(ps_h[e % 2][:, :], W1[:, e, :],
                                     XT[:, bass.ds(r * (TG // TPS), TG // TPS), :].rearrange("p a l -> p (a l)"),
                                     start=True, stop=True).then_inc(h_made, 1)

                def second(r, e):
                    n = E * r + e
                    pe.wait_ge(h_ready, n + 1)
                    need(pe, y_added, TG * (n - 1))
                    for t in range(TG):
                        ins = nc.tensor.matmul(ps_y[e % 2][:, t * P:t * P + P], h[e % 2][:, t * P:t * P + P], W2[:, e, :],
                                               start=True, stop=True)
                    ins.then_inc(y_made, 1)

                def experts(r):
                    first(r, 0)
                    for e in range(E):
                        if e + 1 < E:
                            first(r, e + 1)
                        second(r, e)
                    pe.wait_ge(gw_ready, r + 1)
                    need(pe, gt_ready, r)
                    for t in range(TG):
                        ins = nc.tensor.transpose(ps_x[0:E, t * P:t * P + P],
                                                  gw[:, t, :], ident[:, :])
                    ins.then_inc(gt_made, 1)
                    pe.wait_ge(gt_ready, r + 1)
                    need(pe, bias_added, r)
                    for t in range(TG):
                        ins = nc.tensor.matmul(ps_b[:, t * P:t * P + P], gT[:, t * P:t * P + P], B2[:, :],
                                               start=True, stop=True)
                    ins.then_inc(bias_made, 1)

                experts(0)
                with pe.Fori(1, GROUPS) as r:
                    experts(r)
        sem.clear()


def full_attention(nc, X, ident, w_q, b_q, w_k, b_k, w_v, b_v, w_o, b_o, table):
    H, D = 16, 8
    SCALE = float(D) ** -0.5
    SPREAD = P + D
    SPAN = 2 * SEQ - 1
    with ExitStack() as ctx:
        def sb(name, shape):
            return ctx.enter_context(nc.sbuf_tensor("a_" + name, shape, F32))

        def ps(name, cols=512):
            return ctx.enter_context(nc.psum_tensor("a_" + name, [P, cols], F32))

        sem = Semaphores(nc, "a_")

        mean, rstd = sb("mean", [P, TILES]), sb("rstd", [P, TILES])
        layernorm_stats(nc, X, mean, rstd, "a")
        W = sb("W", [P, 4, P])
        bq, bk = sb("bq", [P, 1]), sb("bk", [P, 1])
        bv, bo = sb("bv", [P, P]), sb("bo", [P, P])
        hmask = sb("hmask", [P, H])
        near = sb("near", [P, H, SEQ])
        far = sb("far", [P, H])
        xn, xT, xTr = sb("xn", [P, TPS, P]), sb("xT", [P, SEQ]), sb("xTr", [P, SEQ])
        qT = sb("qT", [P, SEQ])
        kT = [sb(f"kT{i}", [P, SEQ]) for i in range(2)]
        qz = [sb(f"qz{i}", [P, H, SEQ]) for i in range(2)]
        Vz = [sb(f"Vz{i}", [P, TPS, H * SPREAD]) for i in range(2)]
        nmax = [sb(f"nmax{i}", [P, TPS]) for i in range(2)]
        den = [sb(f"den{i}", [P, TPS]) for i in range(2)]
        prob = [sb(f"prob{i}", [P, TPS, SEQ]) for i in range(2)]
        probT = [sb(f"probT{i}", [P, TPS, SEQ]) for i in range(2)]
        oT = sb("oT", [P, SEQ])
        ps_x, ps_q, ps_v, ps_o = ps("ps_x"), ps("ps_q"), ps("ps_v"), ps("ps_o")
        ps_s = [ps(f"ps_s{i}") for i in range(2)]
        ps_t = [ps(f"ps_t{i}") for i in range(2)]
        loaded, masks, zeroed = sem("loaded"), sem("masks"), sem("zeroed")
        normed, turned, xt_ready, xtr_ready = sem("normed"), sem("turned"), sem("xt_ready"), sem("xtr_ready")
        qkv_made, q_ready, k_ready, qz_ready, v_ready = (sem(s) for s in ("qkv_made", "q_ready", "k_ready", "qz_ready", "v_ready"))
        scored, biased, maxed, nmax_ready, exp_done = (sem(s) for s in ("scored", "biased", "maxed", "nmax_ready", "exp_done"))
        inverted, prob_ready, prob_turned, probT_ready, pv_done = (
            sem(s) for s in ("inverted", "prob_ready", "prob_turned", "probT_ready", "pv_done"))
        oT_ready, out_made, out_added, x_ready = (sem(s) for s in ("oT_ready", "out_made", "out_added", "x_ready"))
        LOADS = 16 * 10

        def sequences(eng, turn, start, tail):
            start()
            turn(0, 0, True, False)
            turn(1, 1, False, False)
            with eng.Fori(0, SEQS // 2 - 2) as pair:
                turn(2 * pair + 2, 0, False, False)
                turn(2 * pair + 3, 1, False, False)
            turn(SEQS - 2, 0, False, False)
            turn(SEQS - 1, 1, False, True)
            tail()

        with nc.Block() as block:
            @block.sync
            def _(sp):
                for i, w in enumerate((w_q, w_k, w_v, w_o)):
                    sp.dma_start(W[:, i, :], w).then_inc(loaded, 16)
                for dst, src in ((bq, b_q), (bk, b_k)):
                    sp.dma_start(dst[:, :], src.rearrange("(c a) -> c a", a=1)).then_inc(loaded, 16)
                for dst, src in ((bv, b_v), (bo, b_o)):
                    sp.dma_start(dst[:, :], src.rearrange("(a c) -> a c", a=1).to_broadcast([P, P])).then_inc(loaded, 16)
                sp.dma_start(near[:, :, :], bass.AP(tensor=table.tensor, offset=0, ap=[[1, P], [SPAN, H], [1, SEQ]])
                             ).then_inc(loaded, 16)
                with nc.allow_non_contiguous_dma(reason="small"):
                    sp.dma_start(far[:, :], bass.AP(tensor=table.tensor, offset=SPAN - 1, ap=[[0, P], [SPAN, H]])
                                 ).then_inc(loaded, 16)

            @block.gpsimd
            def _(pool):
                for v in Vz:
                    nc.gpsimd.memset(v[:, :, :], 0.0).then_inc(zeroed, 1)

            @block.vector
            def _(dve):
                def norm(b):
                    need(dve, turned, b)
                    for t in range(TPS):
                        at = bass.ds(b * TPS + t, 1)
                        nc.vector.tensor_scalar(xn[:, t, :], X[:, at, :].rearrange("p a c -> p (a c)"),
                                                mean[:, at], rstd[:, at], ALU.subtract, ALU.mult).then_inc(normed, 1)

                def reverse(b):
                    dve.wait_ge(xt_ready, b + 1)
                    need(dve, qkv_made, b)
                    nc.vector.tensor_copy(xTr[:, :], xT[:, ::-1]).then_inc(xtr_ready, 1)

                def values(b, s):
                    dve.wait_ge(qkv_made, b + 1)
                    if isinstance(b, int) and b < 2:
                        dve.wait_ge(zeroed, 2)
                    need(dve, pv_done, H * (b - 1))
                    for t in range(TPS):
                        nc.vector.tensor_tensor(
                            Vz[s][:, t, :].rearrange("p (h k) -> p h k", h=H)[:, :, 0:D],
                            ps_v[:, t * P:t * P + P].rearrange("p (h d) -> p h d", h=H),
                            bv[:, :].rearrange("p (h d) -> p h d", h=H), ALU.add).then_inc(v_ready, 1)

                def queries(b, s, heads):
                    dve.wait_ge(q_ready, b + 1)
                    need(dve, scored, H * (b - 1))
                    for h in heads:
                        nc.vector.tensor_scalar(qz[s][:, h, :], qT[:, :], hmask[:, h:h + 1], SCALE,
                                                ALU.mult, ALU.mult).then_inc(qz_ready, 1)

                def shift(b, h):
                    n, i = H * b + h, h % 2
                    dve.wait_ge(scored, n + 1)
                    nc.vector.tensor_tensor(ps_s[i][:, 0:SEQ], ps_s[i][:, 0:SEQ], near[:, h, :], ALU.add).then_inc(biased, 1)
                    dve.wait_ge(biased, n + 1)
                    need(dve, exp_done, n - 1)
                    nc.vector.tensor_reduce(nmax[i][:, :], ps_s[i][:, :].rearrange("p (t k) -> p t k", t=TPS), AX_X,
                                            ALU.max, negate=True).then_inc(maxed, 1)
                    dve.wait_ge(maxed, n + 1)
                    nc.vector.scalar_tensor_tensor(out=nmax[i][:, 1:2], in0=nmax[i][:, 1:2], scalar=far[:, h:h + 1],
                                                   in1=far[:, h:h + 1], op0=ALU.subtract, op1=ALU.add).then_inc(nmax_ready, 1)

                def scale(b, h):
                    n, i = H * b + h, h % 2
                    dve.wait_ge(exp_done, n + 1)
                    nc.vector.reciprocal(den[i][:, :], den[i][:, :]).then_inc(inverted, 1)
                    dve.wait_ge(inverted, n + 1)
                    for t in range(TPS):
                        ins = nc.vector.tensor_scalar(prob[i][:, t, :], prob[i][:, t, :], den[i][:, t:t + 1], None, ALU.mult)
                    ins.then_inc(prob_ready, 1)

                def add_out(b):
                    dve.wait_ge(out_made, b + 1)
                    rows = X[:, bass.ds(b * TPS, TPS), :]
                    nc.vector.tensor_tensor(rows, rows, ps_x[:, SEQ:2 * SEQ].rearrange("p (t c) -> p t c", t=TPS),
                                            ALU.add).then_inc(out_added, 1)
                    dve.wait_ge(out_added, b + 1)
                    nc.vector.tensor_tensor(rows, rows, bo[:, :].unsqueeze(1).to_broadcast([P, TPS, P]),
                                            ALU.add).then_inc(x_ready, 1)

                def start():
                    nc.vector.tensor_reduce(hmask[:, :], ident[:, :].rearrange("p (h d) -> p h d", h=H), AX_X,
                                            ALU.add).then_inc(masks, 1)
                    dve.wait_ge(masks, 1)
                    dve.wait_ge(loaded, LOADS)
                    norm(0)
                    reverse(0)
                    values(0, 0)
                    queries(0, 0, range(H))

                def turn(b, s, first, last):
                    for h in range(H):
                        shift(b, h)
                        if h:
                            scale(b, h - 1)
                        elif not first:
                            scale(b - 1, H - 1)
                        if h == 5 and not first:
                            add_out(b - 1)
                        if not last:
                            if h == 1:
                                norm(b + 1)
                            if h == 3:
                                reverse(b + 1)
                            if h == 7:
                                values(b + 1, 1 - s)
                            if h >= 8:
                                queries(b + 1, 1 - s, range(2 * h - 16, 2 * h - 14))

                def tail():
                    scale(SEQS - 1, H - 1)
                    add_out(SEQS - 1)
                    dve.wait_ge(x_ready, SEQS)

                sequences(dve, turn, start, tail)

            @block.scalar
            def _(act):
                def channels(b):
                    act.wait_ge(turned, b + 1)
                    need(act, qkv_made, b)
                    need(act, xtr_ready, b)
                    nc.scalar.copy(xT[:, :], ps_x[:, 0:SEQ]).then_inc(xt_ready, 1)

                def keys(b, s):
                    act.wait_ge(qkv_made, b + 1)
                    need(act, qz_ready, H * b)
                    nc.scalar.activation(qT[:, :], ps_q[:, 0:SEQ], ACT.Identity, bias=bq[:, :]).then_inc(q_ready, 1)
                    need(act, scored, H * (b - 1))
                    nc.scalar.activation(kT[s][:, :], ps_q[:, SEQ:2 * SEQ], ACT.Identity, bias=bk[:, :]).then_inc(k_ready, 1)

                def expo(b, h):
                    n, i = H * b + h, h % 2
                    act.wait_ge(nmax_ready, n + 1)
                    need(act, prob_turned, n - 1)
                    need(act, prob_ready, n - 1)
                    for t in range(TPS):
                        ins = nc.scalar.activation(prob[i][:, t, :], ps_s[i][:, t * SEQ:t * SEQ + SEQ], ACT.Exp,
                                                   bias=nmax[i][:, t:t + 1], accum_out=den[i][:, t:t + 1])
                    ins.then_inc(exp_done, 1)

                def evacuate(b, h):
                    n, i = H * b + h, h % 2
                    act.wait_ge(prob_turned, n + 1)
                    need(act, pv_done, n - 1)
                    nc.scalar.copy(probT[i][:, :, :], ps_t[i][:, :].rearrange("p (k q) -> p k q", k=TPS)).then_inc(probT_ready, 1)

                def outputs(b):
                    act.wait_ge(pv_done, H * b + H)
                    need(act, out_made, b)
                    nc.scalar.copy(oT[:, :], ps_o[:, 0:SEQ]).then_inc(oT_ready, 1)

                def start():
                    act.wait_ge(loaded, LOADS)
                    channels(0)
                    keys(0, 0)

                def turn(b, s, first, last):
                    for h in range(H):
                        expo(b, h)
                        if h >= 2:
                            evacuate(b, h - 2)
                        elif not first:
                            evacuate(b - 1, H - 2 + h)
                        if h == 2 and not first:
                            outputs(b - 1)
                        if not last:
                            if h == 3:
                                channels(b + 1)
                            if h == 6:
                                keys(b + 1, 1 - s)

                def tail():
                    evacuate(SEQS - 1, H - 2)
                    evacuate(SEQS - 1, H - 1)
                    outputs(SEQS - 1)

                sequences(act, turn, start, tail)

            @block.tensor
            def _(pe):
                def transpose_x(b):
                    pe.wait_ge(normed, TPS * b + TPS)
                    need(pe, xt_ready, b)
                    need(pe, out_added, b - 2)
                    for t in range(TPS):
                        ins = nc.tensor.transpose(ps_x[:, t * P:t * P + P], xn[:, t, :], ident[:, :])
                    ins.then_inc(turned, 1)

                def project(b):
                    pe.wait_ge(xt_ready, b + 1)
                    pe.wait_ge(xtr_ready, b + 1)
                    need(pe, k_ready, b)
                    need(pe, v_ready, TPS * b)
                    nc.tensor.matmul(ps_q[:, 0:SEQ], W[:, 0, :], xT[:, :], start=True, stop=True)
                    nc.tensor.matmul(ps_q[:, SEQ:2 * SEQ], W[:, 1, :], xTr[:, :], start=True, stop=True)
                    for t in range(TPS):
                        ins = nc.tensor.matmul(ps_v[:, t * P:t * P + P], xTr[:, t * P:t * P + P], W[:, 2, :],
                                               start=True, stop=True)
                    ins.then_inc(qkv_made, 1)

                def score(b, s, h):
                    n, i = H * b + h, h % 2
                    pe.wait_ge(qz_ready, n + 1)
                    if h == 0:
                        pe.wait_ge(k_ready, b + 1)
                    need(pe, exp_done, n - 1)
                    for t in range(TPS):
                        ins = nc.tensor.matmul(ps_s[i][:, t * SEQ:t * SEQ + SEQ], qz[s][:, h, t * P:t * P + P], kT[s][:, :],
                                               start=True, stop=True)
                    ins.then_inc(scored, 1)

                def turn_probs(b, h):
                    n, i = H * b + h, h % 2
                    pe.wait_ge(prob_ready, n + 1)
                    need(pe, probT_ready, n - 1)
                    for k in range(TPS):
                        for t in range(TPS):
                            ins = nc.tensor.transpose(ps_t[i][:, k * SEQ + t * P:k * SEQ + t * P + P],
                                                      prob[i][:, t, k * P:k * P + P], ident[:, :])
                    ins.then_inc(prob_turned, 1)

                def weigh(b, s, h):
                    n, i = H * b + h, h % 2
                    pe.wait_ge(probT_ready, n + 1)
                    if h == 0:
                        pe.wait_ge(v_ready, TPS * b + TPS)
                        need(pe, oT_ready, b)
                    for k in range(TPS):
                        ins = nc.tensor.matmul(ps_o[:, 0:SEQ], Vz[s][:, k, h * P:h * P + P], probT[i][:, k, :],
                                               start=(h == 0 and k == 0), stop=(h == H - 1 and k == TPS - 1))
                    ins.then_inc(pv_done, 1)

                def out_proj(b, turned_too):
                    pe.wait_ge(oT_ready, b + 1)
                    pe.wait_ge(xt_ready, turned_too)
                    need(pe, out_added, b)
                    for t in range(TPS):
                        ins = nc.tensor.matmul(ps_x[:, SEQ + t * P:SEQ + t * P + P], oT[:, t * P:t * P + P], W[:, 3, :],
                                               start=True, stop=True)
                    ins.then_inc(out_made, 1)

                def start():
                    pe.wait_ge(loaded, LOADS)
                    transpose_x(0)
                    project(0)

                def turn(b, s, first, last):
                    for h in range(H):
                        score(b, s, h)
                        if h >= 1:
                            turn_probs(b, h - 1)
                        elif not first:
                            turn_probs(b - 1, H - 1)
                        if h >= 2:
                            weigh(b, s, h - 2)
                        elif not first:
                            weigh(b - 1, 1 - s, H - 2 + h)
                        if h == 4 and not first:
                            out_proj(b - 1, SEQS if last else b + 2)
                        if not last:
                            if h == 2:
                                transpose_x(b + 1)
                            if h == 5:
                                project(b + 1)

                def tail():
                    turn_probs(SEQS - 1, H - 1)
                    weigh(SEQS - 1, 1, H - 2)
                    weigh(SEQS - 1, 1, H - 1)
                    out_proj(SEQS - 1, SEQS)

                sequences(pe, turn, start, tail)
        sem.clear()


def local_layers(nc, X, ident, w_qkv, q_scale, k_scale, w_o, ln_g, ln_b, w_1, b_1, w_2, b_2, rotary, masks):
    LAYERS, H, D, WIN = 6, 16, 64, 32
    INNER = H * D
    FF = w_2.shape[1]
    ITEMS = LAYERS * SEQS
    PAIRS = H // 2
    CH = 512
    HC = CH // D
    GH, HG = 4, H // 4
    K1 = P + WIN
    FK = [P, P, FF - 2 * P]
    with ExitStack() as ctx:
        def sb(name, shape, dt=F32):
            return ctx.enter_context(nc.sbuf_tensor("l_" + name, shape, dt))

        def ps(name, cols=512):
            return ctx.enter_context(nc.psum_tensor("l_" + name, [P, cols], F32))

        sem = Semaphores(nc, "l_")

        Wqkv = sb("Wqkv", [P, 3 * INNER])
        Wo = sb("Wo", [P, 2, PAIRS, P])
        W1 = sb("W1", [P, 2, 2 * FF])
        W2 = sb("W2", [P, 2, 3, P])
        b1 = sb("b1", [P, 2, 2 * FF])
        b2 = sb("b2", [P, 2, P])
        gain, offset = sb("gain", [P, LAYERS]), sb("offset", [P, LAYERS])
        own = [sb(f"own{x}", [P, LAYERS, TPS, D]) for x in "qk"]
        cross = [sb(f"cross{x}", [P, LAYERS, TPS, D]) for x in "qk"]
        mask0, mask1 = sb("mask0", [P, P], BF16), sb("mask1", [P, K1], BF16)
        identb = sb("identb", [P, P], BF16)
        xs, sT = sb("xs", [P, TPS, P]), sb("sT", [P, SEQ])
        sq = [sb(f"sq{i}", [P, CH]) for i in range(2)]
        t1 = [sb(f"t1_{i}", [P, CH]) for i in range(2)]
        t2 = [sb(f"t2_{i}", [P, CH]) for i in range(2)]
        n2, clampd, rn = sb("n2", [P, TPS, 2 * H]), sb("clampd", [P, TPS, 2 * H]), sb("rn", [P, TPS, 2 * H])
        half = sb("half", [P, 2 * H])
        qk = sb("qk", [P, 4, CH])
        qz = [sb(f"qz{i}", [P, PAIRS, 2, SEQ]) for i in range(2)]
        kT = [sb(f"kT{i}", [P, PAIRS, SEQ]) for i in range(2)]
        V = [sb(f"V{i}", [P, TPS, INNER]) for i in range(2)]
        sc8 = [sb(f"sc8_{i}", [P, TPS, H]) for i in range(2)]
        nmax = [sb(f"nmax{i}", [P, TPS, HG]) for i in range(2)]
        nbias = [sb(f"nbias{i}", [P, TPS, HG]) for i in range(2)]
        den = [sb(f"den{i}", [P, TPS, HG]) for i in range(2)]
        P0 = [sb(f"P0_{i}", [P, HG, P]) for i in range(2)]
        P1 = [sb(f"P1_{i}", [P, HG, K1]) for i in range(2)]
        PT0 = [sb(f"PT0_{i}", [P, HG, K1]) for i in range(2)]
        PT1 = [sb(f"PT1_{i}", [P, HG, P]) for i in range(2)]
        oT = sb("oT", [P, PAIRS, SEQ])
        xf, stats, mv = sb("xf", [P, TPS, P]), sb("stats", [P, TPS, 6]), sb("mv", [P, TPS, 2])
        var, rstd = sb("var", [P, TPS]), sb("rstd", [P, TPS])
        xn, xnT = sb("xn", [P, TPS, P]), sb("xnT", [P, SEQ])
        gate, gated, lin = sb("gate", [P, FF]), sb("gated", [P, FF]), sb("lin", [P, FF])
        hid = sb("hid", [P, TPS, FF])
        hT = sb("hT", [P, TPS, 3, P])
        ps_w = [ps(f"ps_w{i}") for i in range(2)]
        ps_t, ps_p, ps_o = ps("ps_t"), ps("ps_p"), ps("ps_o")
        ps_s0, ps_s1, ps_s2 = ps("ps_s0"), ps("ps_s1"), ps("ps_s2")

        names = ("setup consts zeroed scales_in qscales wqkv_in later_in shifted turned sT_ready qkv_made sq_done rot_done n2_made clamped "
                 "powed roped scaled qk_turned qkT_ready sc_ready v_ready scored maxed nm_ready exp_done inverted "
                 "norm_done bt_done pt_turned pt_ready pv_done ot_ready wo_made x_attn shifted2 bn_done var_ready "
                 "rstd_ready xn_ready ft_made xnT_ready fw_made gate_ready gelu_done lin_ready h_ready ht_made "
                 "hT_ready w2_made ffn_part x_ffn aggr_done small_done").split()
        S = {n: sem(n) for n in names}
        (setup, consts, zeroed, scales_in, qscales, wqkv_in, later_in, shifted, turned, sT_ready, qkv_made, sq_done, rot_done, n2_made,
         clamped, powed, roped, scaled, qk_turned, qkT_ready, sc_ready, v_ready, scored, maxed, nm_ready, exp_done,
         inverted, norm_done, bt_done, pt_turned, pt_ready, pv_done, ot_ready, wo_made, x_attn, shifted2, bn_done,
         var_ready, rstd_ready, xn_ready, ft_made, xnT_ready, fw_made, gate_ready, gelu_done, lin_ready, h_ready,
         ht_made, hT_ready, w2_made, ffn_part, x_ffn, aggr_done, small_done) = (S[n] for n in names)
        sp_alone, dve_alone = sem("sp_alone"), sem("dve_alone")
        LATER = 16 * 6
        SHIFT = 16 * 3
        MISC = 16 * 10

        with ExitStack() as inner:
            base = inner.enter_context(nc.sbuf_tensor("l_base", [P, TPS, 4, D], F32))
            scale = inner.enter_context(nc.sbuf_tensor("l_scale", [P, 2, LAYERS, D], F32))
            maskf = inner.enter_context(nc.sbuf_tensor("l_maskf", [P, P + K1], F32))
            with nc.Block() as block:
                @block.sync
                def _(sp):
                    n = 0
                    for dst, src in (
                            (base[:, :, :, :], rotary.rearrange("(t p) k e -> p t k e", p=P)),
                            (scale[:, 0, :, :], q_scale.rearrange("(a l) e -> a l e", a=1).to_broadcast([P, LAYERS, D])),
                            (scale[:, 1, :, :], k_scale.rearrange("(a l) e -> a l e", a=1).to_broadcast([P, LAYERS, D])),
                            (maskf[:, :], masks)):
                        sp.dma_start(dst, src).then_inc(setup, 16)
                        n += 1
                    with nc.allow_non_contiguous_dma(reason="small"):
                        sp.dma_start(gain[:, :], ln_g.rearrange("l c -> c l")).then_inc(setup, 16)
                        sp.dma_start(offset[:, :], ln_b.rearrange("l c -> c l")).then_inc(setup, 16)
                    sp.wait_ge(setup, 16 * (n + 2))

                @block.vector
                def _(dve):
                    dve.wait_ge(setup, 16 * 6)
                    for x in range(2):
                        for t in range(TPS):
                            fac = lambda k: base[:, t, 2 * x + k, :].unsqueeze(1).to_broadcast([P, LAYERS, D])
                            nc.vector.tensor_tensor(own[x][:, :, t, :], scale[:, x, :, :], fac(0), ALU.mult).then_inc(qscales, 1)
                            for hf in range(2):
                                lo, hi = slice(hf * D // 2, (hf + 1) * D // 2), slice((1 - hf) * D // 2, (2 - hf) * D // 2)
                                nc.vector.tensor_tensor(cross[x][:, :, t, lo], scale[:, x, :, hi], fac(1)[:, :, lo],
                                                        ALU.mult).then_inc(qscales, 1)
                    nc.vector.tensor_copy(mask0[:, :], maskf[:, 0:P]).then_inc(qscales, 1)
                    nc.vector.tensor_copy(mask1[:, :], maskf[:, P:]).then_inc(qscales, 1)
                    nc.vector.tensor_copy(identb[:, :], ident[:, :]).then_inc(qscales, 1)
                    nc.vector.memset(xs[0:1, 0, D:], 0.0).then_inc(qscales, 1)
                    nc.vector.memset(xf[0:1, 0, D:], 0.0).then_inc(qscales, 1)
                    dve.wait_ge(qscales, 6 * TPS + 5)

                @block.gpsimd
                def _(pool):
                    nc.gpsimd.memset(half[:, :], -0.5).then_inc(zeroed, 1)
                    for i in range(2):
                        nc.gpsimd.memset(qz[i][:, :, :, :], 0.0).then_inc(zeroed, 1)
                        nc.gpsimd.memset(PT0[i][:, :, :], 0.0).then_inc(zeroed, 1)
                    pool.wait_ge(zeroed, 5)

        def items(eng, turn):
            turn(0, 0, True, False, False)
            turn(1, 1, True, True, False)
            turn(2, 0, True, True, True)
            turn(3, 1, True, True, True)
            with eng.Fori(0, ITEMS // 2 - 2) as pair:
                turn(2 * pair + 4, 0, True, True, True)
                turn(2 * pair + 5, 1, True, True, True)
            turn(ITEMS, 0, False, True, True)
            turn(ITEMS + 1, 1, False, False, True)

        with nc.Block() as block:
            @block.sync
            def _(sp):
                def load_qkv(l):
                    need(sp, qkv_made, 12 * SEQS * l)
                    sp.dma_start(Wqkv[:, :], w_qkv[bass.ds(l, 1), :, :].rearrange("a c n -> c (a n)")).then_inc(wqkv_in, 16)

                def load_later(l):
                    need(sp, x_ffn, SEQS * (l - 1))
                    sp.sem_inc(sp_alone, 1)
                    h = bass.ds(l % 2, 1)
                    at = bass.ds(l, 1)
                    sp.dma_start(Wo[:, h, :, :].rearrange("p a j n -> p (a j) n"),
                                 w_o[at, :, :].rearrange("a (j p) n -> p (a j) n", p=P)).then_inc(later_in, 16)
                    sp.dma_start(W1[:, h, :].rearrange("p a n -> p (a n)"),
                                 w_1[at, :, :].rearrange("a c n -> c (a n)")).then_inc(later_in, 16)
                    sp.dma_start(W2[:, h, 0:2, :].rearrange("p a k n -> p (a k) n"),
                                 w_2[at, 0:2 * P, :].rearrange("a (k p) n -> p (a k) n", p=P)).then_inc(later_in, 16)
                    sp.dma_start(W2[0:FK[2], h, 2, :].rearrange("p a n -> p (a n)"),
                                 w_2[at, 2 * P:FF, :].rearrange("a p n -> p (a n)")).then_inc(later_in, 16)
                    sp.dma_start(b1[:, h, :].rearrange("p a n -> p (a n)"),
                                 b_1[at, :].to_broadcast([P, 2 * FF])).then_inc(later_in, 16)
                    sp.dma_start(b2[:, h, :].rearrange("p a n -> p (a n)"),
                                 b_2[at, :].to_broadcast([P, P])).then_inc(later_in, 16)

                def shift(dst, b, done):
                    t = bass.ds(b * TPS, TPS)
                    sp.dma_start(dst[:, :, 0:D], X[:, t, 0:D]).then_inc(done, 16)
                    sp.dma_start(dst[1:P, :, D:], X[0:P - 1, t, D:]).then_inc(done, 16)
                    sp.dma_start(dst[0:1, 1, D:], X[P - 1:P, bass.ds(b * TPS, 1), D:].rearrange("p a c -> p (a c)")
                                 ).then_inc(done, 16)

                def item(i, b, ahead, first=False):
                    if not first:
                        sp.wait_ge(x_ffn, i - SEQS + 1)
                        sp.sem_inc(sp_alone, 1)
                    need(sp, turned, i)
                    shift(xs, b, shifted)
                    if ahead:
                        later(i - 2, (b + SEQS - 2) % SEQS)

                def later(f, b):
                    sp.wait_ge(x_attn, f + 1)
                    sp.sem_inc(sp_alone, 1)
                    need(sp, xn_ready, f)
                    shift(xf, b, shifted2)

                load_qkv(0)
                load_later(0)
                item(0, 0, False, True)
                item(1, 1, False, True)
                item(2, 2, True, True)
                item(3, 3, True, True)
                load_later(1)
                with sp.Fori(4, SEQS) as b:
                    item(b, b, True, True)
                with sp.Fori(1, LAYERS - 1) as l:
                    load_qkv(l)
                    with sp.Fori(0, 4) as b:
                        item(l * SEQS + b, b, True)
                    load_later(l + 1)
                    with sp.Fori(4, SEQS) as b:
                        item(l * SEQS + b, b, True)
                load_qkv(LAYERS - 1)
                with sp.Fori(0, SEQS) as b:
                    item((LAYERS - 1) * SEQS + b, b, True)
                later(ITEMS - 2, SEQS - 2)
                later(ITEMS - 1, SEQS - 1)

            @block.tensor
            def _(pe):
                def turn(i, s, p1, p2, p3):
                    a, f, o = i - 1, i - 2, 1 - s
                    layer = i // SEQS
                    half_o, half_f = bass.ds((a // SEQS) % 2, 1), bass.ds((f // SEQS) % 2, 1)

                    def scores(g):
                        if not p2:
                            return
                        n = GH * a + g
                        if g == 0:
                            pe.wait_ge(qkT_ready, 8 * a + 8)
                        need(pe, exp_done, n)
                        for ps_, m, heads, width, t in ((ps_s0, mask0, range(HG), P, 0), (ps_s1, mask1, (0, 1), K1, 1),
                                                        (ps_s2, mask1, (2, 3), K1, 1)):
                            k = len(heads)
                            nc.tensor.matmul(ps_[:, 0:k * width], identb[:, :], m[:, :].unsqueeze(1).to_broadcast([P, k, width]),
                                             start=True, stop=False)
                            for x, h in enumerate(heads):
                                pair, odd = divmod(HG * g + h, 2)
                                ins = nc.tensor.matmul(ps_[:, x * width:x * width + width],
                                                       qz[o][:, pair, odd, t * P:t * P + P],
                                                       kT[o][:, pair, t * (P - WIN):t * (P - WIN) + width],
                                                       start=False, stop=(x == k - 1))
                        ins.then_inc(scored, 1)

                    def turn_probs(g, t):
                        if not p2:
                            return
                        n = GH * a + g
                        pe.wait_ge(norm_done, n + 1)
                        need(pe, pt_ready, 2 * n + t)
                        for h in range(HG):
                            src = P1[g % 2][:, h, WIN:K1] if t else P0[g % 2][:, h, :]
                            ins = nc.tensor.transpose(ps_p[:, h * P:h * P + P], src, ident[:, :])
                        ins.then_inc(pt_turned, 1)

                    def weigh(g):
                        if not p2:
                            return
                        n = GH * a + g
                        pe.wait_ge(pt_ready, 2 * n + 2)
                        pe.wait_ge(bt_done, n + 1)
                        if g == 0:
                            pe.wait_ge(v_ready, 4 * a + 4)
                            need(pe, x_attn, a)
                        need(pe, ot_ready, n)
                        if g == GH - 1 and p3:
                            pe.wait_ge(x_ffn, f + 1)
                        for h in range(HG):
                            head = HG * g + h
                            rows, c0 = slice(D * (h % 2), D * (h % 2) + D), (h // 2) * SEQ
                            nc.tensor.matmul(ps_o[rows, c0:c0 + K1], V[o][:, 0, head * D:head * D + D], PT0[g % 2][:, h, :],
                                             start=True, stop=False, skip_group_check=True)
                            ins = nc.tensor.matmul(ps_o[rows, c0 + P:c0 + SEQ], V[o][:, 1, head * D:head * D + D],
                                                   PT1[g % 2][:, h, :], start=False, stop=True, skip_group_check=True)
                        ins.then_inc(pv_done, 1)

                    def out_proj():
                        if not p2:
                            return
                        pe.wait_ge(ot_ready, GH * a + GH)
                        for t in range(TPS):
                            for j in range(PAIRS):
                                ins = nc.tensor.matmul(ps_o[:, t * P:t * P + P], oT[:, j, t * P:t * P + P],
                                                       Wo[:, half_o, j, :].rearrange("p a n -> p (a n)"),
                                                       start=(j == 0), stop=(j == PAIRS - 1))
                        ins.then_inc(wo_made, 1)

                    def turn_x():
                        if not p1:
                            return
                        pe.wait_ge(shifted, SHIFT * (i + 1))
                        need(pe, qkT_ready, 8 * i)
                        if p3:
                            need(pe, hT_ready, 2 * f)
                        for t in range(TPS):
                            ins = nc.tensor.transpose(ps_t[:, t * P:t * P + P], xs[:, t, :], ident[:, :])
                        ins.then_inc(turned, 1)

                    def project(j):
                        if not p1:
                            return
                        t, c = divmod(j, 6)
                        if j == 0:
                            pe.wait_ge(sT_ready, i + 1)
                            pe.wait_ge(wqkv_in, 16 * (layer + 1))
                        if j < 2:
                            need(pe, v_ready, 4 * i)
                        elif j in (6, 7):
                            pe.wait_ge(v_ready, 4 * i + j - 5)
                        else:
                            pe.wait_ge(rot_done, 8 * i + 4 * t + (j - 2) % 6 + 1)
                        if p3 and j in (4, 6):
                            pe.wait_ge(gate_ready, 2 * f + j // 2 - 1)
                        if p3 and j in (5, 7):
                            pe.wait_ge(lin_ready, 2 * f + j // 2 - 1)
                        nc.tensor.matmul(ps_w[j % 2][:, :], sT[:, t * P:t * P + P], Wqkv[:, c * CH:c * CH + CH],
                                         start=True, stop=True).then_inc(qkv_made, 1)

                    def turn_qk(t):
                        if not p1:
                            return
                        for c in range(4):
                            m = 8 * i + 4 * t + c
                            if c < 2:
                                pe.wait_ge(roped, m + 1)
                            else:
                                pe.wait_ge(scaled, 2 * (2 * i + t) + c - 1)
                            if c == 0 and p3:
                                pe.wait_ge(xnT_ready, f + 1) if t == 0 else pe.wait_ge(hT_ready, 2 * f + 1)
                            if c == 0 and t == 0:
                                pe.wait_ge(sT_ready, i + 1)
                            need(pe, qkT_ready, m)
                            for x in range(4):
                                ins = nc.tensor.transpose(ps_t[:, x * P:x * P + P], qk[:, c, x * P:x * P + P], ident[:, :])
                            ins.then_inc(qk_turned, 1)

                    def turn_normed():
                        if not p3:
                            return
                        pe.wait_ge(xn_ready, f + 1)
                        if p1:
                            pe.wait_ge(sT_ready, i + 1)
                        else:
                            pe.wait_ge(qkT_ready, 8 * ITEMS)
                            need(pe, hT_ready, 2 * f)
                        for t in range(TPS):
                            ins = nc.tensor.transpose(ps_t[:, t * P:t * P + P], xn[:, t, :], ident[:, :])
                        ins.then_inc(ft_made, 1)

                    def hidden(t):
                        if not p3:
                            return
                        if t == 0:
                            pe.wait_ge(xnT_ready, f + 1)
                            pe.wait_ge(later_in, LATER * (f // SEQS + 1))
                        for k in range(2):
                            if p1 and t == 0:
                                pe.wait_ge(rot_done, 8 * i + 3 + k)
                            if p1 and t == 1:
                                pe.wait_ge(v_ready, 4 * i + 1 + k)
                            if not p1:
                                pe.wait_ge(v_ready, 4 * ITEMS)
                            need(pe, lin_ready if k else gate_ready, 2 * f + t)
                            c0 = FF * (1 - k)
                            nc.tensor.matmul(ps_w[k][:, 0:FF], xnT[:, t * P:t * P + P],
                                             W1[:, half_f, c0:c0 + FF].rearrange("p a n -> p (a n)"),
                                             start=True, stop=True).then_inc(fw_made, 1)

                    def turn_hidden(t):
                        if not p3:
                            return
                        pe.wait_ge(h_ready, 2 * f + t + 1)
                        if p1:
                            pe.wait_ge(qkT_ready, 8 * i + 4 * t + 4)
                        else:
                            pe.wait_ge(xnT_ready, f + 1)
                            need(pe, hT_ready, 2 * f + t)
                        for k, rows in enumerate(FK):
                            ins = nc.tensor.transpose(ps_t[0:rows, k * P:k * P + P], hid[:, t, k * P:k * P + rows], ident[:, :])
                        ins.then_inc(ht_made, 1)

                    def ff_out():
                        if not p3:
                            return
                        pe.wait_ge(hT_ready, 2 * f + 2)
                        if p2:
                            pe.wait_ge(ot_ready, GH * a + GH - 1)
                        else:
                            pe.wait_ge(x_attn, ITEMS)
                        for t in range(TPS):
                            for k, rows in enumerate(FK):
                                ins = nc.tensor.matmul(ps_o[:, t * P:t * P + P], hT[0:rows, t, k, :],
                                                       W2[0:rows, half_f, k, :].rearrange("p a n -> p (a n)"),
                                                       start=(k == 0), stop=(k == 2))
                        ins.then_inc(w2_made, 1)

                    scores(0)
                    turn_x()
                    for j in range(4):
                        project(j)
                    turn_normed()
                    scores(1)
                    turn_probs(0, 0)
                    hidden(0)
                    turn_probs(0, 1)
                    project(4)
                    project(5)
                    weigh(0)
                    hidden(1)
                    turn_qk(0)
                    scores(2)
                    turn_probs(1, 0)
                    project(6)
                    project(7)
                    turn_probs(1, 1)
                    project(8)
                    project(9)
                    weigh(1)
                    turn_hidden(0)
                    scores(3)
                    turn_probs(2, 0)
                    project(10)
                    turn_probs(2, 1)
                    project(11)
                    turn_qk(1)
                    weigh(2)
                    turn_hidden(1)
                    turn_probs(3, 0)
                    ff_out()
                    turn_probs(3, 1)
                    weigh(3)
                    if p2:
                        pe.wait_ge(later_in, LATER * (a // SEQS + 1))
                    out_proj()

                items(pe, turn)

            @block.scalar
            def _(act):
                def turn(i, s, p1, p2, p3):
                    a, f, o = i - 1, i - 2, 1 - s

                    def expo(g):
                        if not p2:
                            return
                        n, k = GH * a + g, g % 2
                        act.wait_ge(nm_ready, n + 1)
                        need(act, pt_turned, 2 * n - 2)
                        need(act, bt_done, n - 1)
                        for t in range(TPS):
                            for h in range(HG):
                                if t == 0:
                                    src, dst = ps_s0[:, h * P:h * P + P], P0[k][:, h, :]
                                else:
                                    x = (h % 2) * K1
                                    src, dst = (ps_s2 if h >= 2 else ps_s1)[:, x:x + K1], P1[k][:, h, :]
                                ins = nc.scalar.activation(dst, src, ACT.Exp, bias=nbias[k][:, t, h:h + 1],
                                                           scale=sc8[o][:, t, HG * g + h:HG * g + h + 1],
                                                           accum_out=den[k][:, t, h:h + 1])
                        ins.then_inc(exp_done, 1)

                    def outputs(g):
                        if not p2:
                            return
                        n = GH * a + g
                        act.wait_ge(pv_done, n + 1)
                        if g == 0:
                            need(act, wo_made, a)
                        nc.scalar.copy(oT[:, 2 * g:2 * g + 2, :], ps_o[:, :].rearrange("p (j q) -> p j q", j=2)).then_inc(ot_ready, 1)

                    def channels():
                        if not p1:
                            return
                        act.wait_ge(turned, i + 1)
                        need(act, qkv_made, 12 * i)
                        nc.scalar.copy(sT[:, :], ps_t[:, 0:SEQ]).then_inc(sT_ready, 1)

                    def squares(j):
                        if not p1:
                            return
                        t, c = divmod(j, 6)
                        m = 8 * i + 4 * t + c
                        act.wait_ge(qkv_made, 12 * i + j + 1)
                        need(act, n2_made, m - 1)
                        nc.scalar.activation(sq[c % 2][:, :], ps_w[j % 2][:, :], ACT.Square).then_inc(sq_done, 1)

                    def values(j):
                        if not p1:
                            return
                        t, c = divmod(j, 6)
                        act.wait_ge(qkv_made, 12 * i + j + 1)
                        need(act, pv_done, GH * (i - 1))
                        nc.scalar.copy(V[s][:, t, (c - 4) * CH:(c - 3) * CH], ps_w[j % 2][:, :]).then_inc(v_ready, 1)

                    def keep_qk(t):
                        if not p1:
                            return
                        for c in range(4):
                            m = 8 * i + 4 * t + c
                            act.wait_ge(qk_turned, m + 1)
                            if c == 0:
                                need(act, scored, GH * (i - 1))
                            src = ps_t[:, :].rearrange("p (j q) -> p j q", j=4)
                            pairs, cols = slice(4 * (c % 2), 4 * (c % 2) + 4), slice(t * P, t * P + P)
                            if c < 2:
                                nc.scalar.copy(qz[s][0:D, pairs, 0, cols], src[0:D])
                                ins = nc.scalar.copy(qz[s][D:P, pairs, 1, cols], src[D:P])
                            else:
                                ins = nc.scalar.copy(kT[s][:, pairs, cols], src)
                            ins.then_inc(qkT_ready, 1)

                    def ff_input():
                        if not p3:
                            return
                        act.wait_ge(ft_made, f + 1)
                        need(act, fw_made, 4 * f)
                        l = bass.ds(f // SEQS, 1)
                        nc.scalar.activation(xnT[:, :], ps_t[:, 0:SEQ], ACT.Identity, bias=offset[:, l], scale=gain[:, l]
                                             ).then_inc(xnT_ready, 1)

                    def gelu(t):
                        if not p3:
                            return
                        act.wait_ge(gate_ready, 2 * f + t + 1)
                        need(act, h_ready, 2 * f + t)
                        nc.scalar.activation(gated[:, :], gate[:, :], ACT.Gelu).then_inc(gelu_done, 1)

                    expo(0)
                    channels()
                    for j in range(4):
                        squares(j)
                    ff_input()
                    expo(1)
                    gelu(0)
                    values(4)
                    values(5)
                    outputs(0)
                    gelu(1)
                    keep_qk(0)
                    expo(2)
                    for j in range(6, 10):
                        squares(j)
                    outputs(1)
                    expo(3)
                    values(10)
                    values(11)
                    keep_qk(1)
                    outputs(2)
                    outputs(3)

                items(act, turn)

            @block.vector
            def _(dve):
                def turn(i, s, p1, p2, p3):
                    a, f, o = i - 1, i - 2, 1 - s
                    layer = bass.ds(min(i // SEQS, LAYERS - 1) if isinstance(i, int) else i // SEQS, 1)

                    def maxima(g):
                        if not p2:
                            return
                        n, k = GH * a + g, g % 2
                        dve.wait_ge(scored, n + 1)
                        need(dve, exp_done, n - 1)
                        for out, src in ((nmax[k][:, 0, :], ps_s0[:, :].rearrange("p (h k) -> p h k", h=HG)),
                                         (nmax[k][:, 1, 0:2], ps_s1[:, 0:2 * K1].rearrange("p (h k) -> p h k", h=2)),
                                         (nmax[k][:, 1, 2:4], ps_s2[:, 0:2 * K1].rearrange("p (h k) -> p h k", h=2))):
                            ins = nc.vector.tensor_reduce(out, src, AX_X, ALU.max, negate=True)
                        ins.then_inc(maxed, 1)
                        dve.wait_ge(maxed, n + 1)
                        if g == 0:
                            dve.wait_ge(sc_ready, 2 * a + 2)
                        nc.vector.tensor_tensor(nbias[k][:, :, :], nmax[k][:, :, :], sc8[o][:, :, HG * g:HG * g + HG],
                                                ALU.mult).then_inc(nm_ready, 1)

                    def normalise(g):
                        if not p2:
                            return
                        n, k = GH * a + g, g % 2
                        dve.wait_ge(exp_done, n + 1)
                        nc.vector.reciprocal(den[k][:, :, :], den[k][:, :, :]).then_inc(inverted, 1)
                        dve.wait_ge(inverted, n + 1)
                        nc.vector.tensor_tensor(P0[k][:, :, :], P0[k][:, :, :],
                                                den[k][:, 0, :].unsqueeze(2).to_broadcast([P, HG, P]), ALU.mult)
                        nc.vector.tensor_tensor(P1[k][:, :, :], P1[k][:, :, :],
                                                den[k][:, 1, :].unsqueeze(2).to_broadcast([P, HG, K1]), ALU.mult
                                                ).then_inc(norm_done, 1)
                        dve.wait_ge(norm_done, n + 1)
                        need(dve, pv_done, n - 1)
                        nc.vector.transpose(PT0[k][P - WIN:P, :, P:K1], P1[k][0:WIN, :, 0:WIN]).then_inc(bt_done, 1)

                    def keep_probs(g, t):
                        if not p2:
                            return
                        n, k = GH * a + g, g % 2
                        dve.wait_ge(pt_turned, 2 * n + t + 1)
                        dst = PT1[k][:, :, :] if t else PT0[k][:, :, 0:P]
                        nc.vector.tensor_copy(dst, ps_p[:, :].rearrange("p (h q) -> p h q", h=HG)).then_inc(pt_ready, 1)

                    def add_attention():
                        if not p2:
                            return
                        dve.wait_ge(wo_made, a + 1)
                        rows = X[:, bass.ds((a % SEQS) * TPS, TPS), :]
                        nc.vector.tensor_tensor(rows, rows, ps_o[:, 0:SEQ].rearrange("p (t c) -> p t c", t=TPS),
                                                ALU.add).then_inc(x_attn, 1)

                    def rotate(j):
                        if not p1:
                            return
                        t, c = divmod(j, 6)
                        m, x = 8 * i + 4 * t + c, c // 2
                        k = c % 2
                        dve.wait_ge(sq_done, m + 1)
                        need(dve, roped, m - 1)
                        src = ps_w[j % 2][:, :].rearrange("p (h a e) -> p h a e", h=HC, a=2)
                        table = lambda v: v[x][:, layer, t, :].to_broadcast([P, HC, D])
                        nc.vector.tensor_tensor(t1[k][:, :].rearrange("p (h e) -> p h e", h=HC),
                                                ps_w[j % 2][:, :].rearrange("p (h e) -> p h e", h=HC), table(own), ALU.mult)
                        nc.vector.tensor_tensor(t2[k][:, :].rearrange("p (h a e) -> p h a e", h=HC, a=2), src[:, :, ::-1, :],
                                                table(cross).rearrange("p h (a e) -> p h a e", a=2), ALU.mult
                                                ).then_inc(rot_done, 1)
                        if c == 0:
                            need(dve, clamped, 2 * i + t)
                        nc.vector.tensor_reduce(n2[:, t, HC * c:HC * c + HC], sq[k][:, :].rearrange("p (h e) -> p h e", h=HC),
                                                AX_X, ALU.add).then_inc(n2_made, 1)
                        if c == 3:
                            dve.wait_ge(n2_made, m + 1)
                            need(dve, powed, 2 * i + t - 1)
                            nc.vector.tensor_scalar(clampd[:, t, :], n2[:, t, :], 1e-24, None, ALU.max).then_inc(clamped, 1)

                    def q_factor(t):
                        if not p1:
                            return
                        dve.wait_ge(powed, 2 * i + t + 1)
                        need(dve, exp_done, GH * (i - 1))
                        nc.vector.tensor_scalar(sc8[s][:, t, :], rn[:, t, 0:H], 8.0, None, ALU.mult).then_inc(sc_ready, 1)

                    def ff_stats():
                        if not p3:
                            return
                        dve.wait_ge(shifted2, SHIFT * (f + 1))
                        for t in range(TPS):
                            nc.vector.bn_stats(stats[:, t, :], xf[:, t, :]).then_inc(bn_done, 1)
                        dve.wait_ge(bn_done, TPS * (f + 1))
                        dve.sem_inc(dve_alone, 1)
                        for t in range(TPS):
                            nc.vector.bn_aggr(mv[:, t, :], stats[:, t, :]).then_inc(aggr_done, 1)
                        dve.wait_ge(aggr_done, TPS * (f + 1))
                        nc.vector.tensor_scalar(var[:, :], mv[:, :, 1], EPS, None, ALU.add).then_inc(var_ready, 1)

                    def ff_norm():
                        if not p3:
                            return
                        dve.wait_ge(rstd_ready, f + 1)
                        need(dve, ft_made, f)
                        for t in range(TPS):
                            ins = nc.vector.tensor_scalar(xn[:, t, :], xf[:, t, :], mv[:, t, 0:1], rstd[:, t:t + 1],
                                                          ALU.subtract, ALU.mult)
                        ins.then_inc(xn_ready, 1)

                    def bias_1(t):
                        if not p3:
                            return
                        n, hf = 2 * f + t, bass.ds((f // SEQS) % 2, 1)
                        if t == 0:
                            dve.wait_ge(later_in, LATER * (f // SEQS + 1))
                        dve.wait_ge(fw_made, 2 * n + 1)
                        need(dve, gelu_done, n)
                        bias = lambda c0: b1[:, hf, c0:c0 + FF].rearrange("p a n -> p (a n)")
                        nc.vector.tensor_tensor(gate[:, :], ps_w[0][:, 0:FF], bias(FF), ALU.add).then_inc(gate_ready, 1)
                        dve.wait_ge(fw_made, 2 * n + 2)
                        need(dve, h_ready, n)
                        nc.vector.tensor_tensor(lin[:, :], ps_w[1][:, 0:FF], bias(0), ALU.add).then_inc(lin_ready, 1)

                    def multiply(t):
                        if not p3:
                            return
                        n = 2 * f + t
                        dve.wait_ge(gelu_done, n + 1)
                        dve.wait_ge(lin_ready, n + 1)
                        need(dve, ht_made, n - 1)
                        nc.vector.tensor_tensor(hid[:, t, :], lin[:, :], gated[:, :], ALU.mult).then_inc(h_ready, 1)

                    def keep_hidden(t):
                        if not p3:
                            return
                        n = 2 * f + t
                        dve.wait_ge(ht_made, n + 1)
                        need(dve, w2_made, f)
                        nc.vector.tensor_copy(hT[:, t, 0:2, :], ps_t[:, 0:2 * P].rearrange("p (k q) -> p k q", k=2))
                        nc.vector.tensor_copy(hT[0:FK[2], t, 2, :], ps_t[0:FK[2], 2 * P:3 * P]).then_inc(hT_ready, 1)

                    def add_ff():
                        if not p3:
                            return
                        dve.wait_ge(w2_made, f + 1)
                        rows = X[:, bass.ds((f % SEQS) * TPS, TPS), :]
                        nc.vector.tensor_tensor(rows, rows, ps_o[:, 0:SEQ].rearrange("p (t c) -> p t c", t=TPS),
                                                ALU.add).then_inc(ffn_part, 1)
                        dve.wait_ge(ffn_part, f + 1)
                        nc.vector.tensor_tensor(rows, rows, b2[:, bass.ds((f // SEQS) % 2, 1), :].to_broadcast([P, TPS, P]),
                                                ALU.add).then_inc(x_ffn, 1)

                    maxima(0)
                    rotate(0)
                    rotate(1)
                    ff_stats()
                    rotate(2)
                    ff_norm()
                    rotate(3)
                    normalise(0)
                    maxima(1)
                    keep_probs(0, 0)
                    bias_1(0)
                    multiply(0)
                    keep_probs(0, 1)
                    q_factor(0)
                    bias_1(1)
                    multiply(1)
                    normalise(1)
                    maxima(2)
                    keep_probs(1, 0)
                    rotate(6)
                    rotate(7)
                    keep_probs(1, 1)
                    rotate(8)
                    rotate(9)
                    keep_hidden(0)
                    normalise(2)
                    maxima(3)
                    keep_probs(2, 0)
                    keep_probs(2, 1)
                    q_factor(1)
                    keep_hidden(1)
                    normalise(3)
                    keep_probs(3, 0)
                    add_ff()
                    keep_probs(3, 1)
                    add_attention()

                items(dve, turn)
                dve.wait_ge(x_ffn, ITEMS)

            @block.gpsimd
            def _(pool):
                def turn(i, s, p1, p2, p3):
                    f = i - 2

                    def add(j):
                        if not p1:
                            return
                        t, c = divmod(j, 6)
                        m, k = 8 * i + 4 * t + c, c % 2
                        pool.wait_ge(rot_done, m + 1)
                        need(pool, qk_turned, m - 3)
                        nc.gpsimd.tensor_tensor(qk[:, c, :], t1[k][:, :], t2[k][:, :], ALU.add).then_inc(roped, 1)

                    def norms(t):
                        if not p1:
                            return
                        n = 2 * i + t
                        pool.wait_ge(clamped, n + 1)
                        need(pool, sc_ready, n - 1)
                        need(pool, scaled, 2 * n - 2)
                        nc.gpsimd.tensor_tensor(rn[:, t, :], clampd[:, t, :], half[:, :], ALU.pow).then_inc(powed, 1)
                        pool.wait_ge(powed, n + 1)
                        pool.wait_ge(roped, 4 * n + 4)
                        for c in (2, 3):
                            v = qk[:, c, :].rearrange("p (h e) -> p h e", h=HC)
                            nc.gpsimd.tensor_tensor(v, v, rn[:, t, HC * c:HC * c + HC].unsqueeze(2).to_broadcast([P, HC, D]),
                                                    ALU.mult).then_inc(scaled, 1)

                    def ff_rstd():
                        if not p3:
                            return
                        pool.wait_ge(var_ready, f + 1)
                        need(pool, xn_ready, f)
                        nc.gpsimd.tensor_tensor(rstd[:, :], var[:, :], half[:, 0:TPS], ALU.pow).then_inc(rstd_ready, 1)

                    add(0)
                    add(1)
                    ff_rstd()
                    add(2)
                    add(3)
                    norms(0)
                    for j in range(6, 10):
                        add(j)
                    norms(1)

                items(pool, turn)
        sem.clear()


def normalise_all(nc, X, store):
    with ExitStack() as ctx:
        mean = ctx.enter_context(nc.sbuf_tensor("n_mean", [P, TILES], F32))
        rstd = ctx.enter_context(nc.sbuf_tensor("n_rstd", [P, TILES], F32))
        stored = ctx.enter_context(nc.semaphore("n_stored"))
        normed = ctx.enter_context(nc.semaphore("n_normed"))
        layernorm_stats(nc, X, mean, rstd, "n")
        with nc.Block() as block:
            @block.sync
            def _(sp):
                sp.dma_start(store, X[:, :, :]).then_inc(stored, 16)

            @block.vector
            def _(dve):
                dve.wait_ge(stored, 16)
                with dve.Fori(0, TILES) as t:
                    row = X[:, bass.ds(t, 1), :].rearrange("p a c -> p (a c)")
                    nc.vector.tensor_scalar(row, row, mean[:, bass.ds(t, 1)], rstd[:, bass.ds(t, 1)],
                                            ALU.subtract, ALU.mult).then_inc(normed, 1)
                dve.wait_ge(normed, TILES)


def add_and_store(nc, X, store, out):
    PARTS = 4
    N = TILES // PARTS
    with ExitStack() as ctx:
        held = ctx.enter_context(nc.sbuf_tensor("f_held", [P, TILES, P], F32))
        back = [ctx.enter_context(nc.semaphore(f"f_back{i}")) for i in range(PARTS)]
        added = ctx.enter_context(nc.semaphore("f_added"))
        written = ctx.enter_context(nc.semaphore("f_written"))
        with nc.Block() as block:
            @block.sync
            def _(sp):
                for i in range(PARTS):
                    at = slice(i * N, i * N + N)
                    sp.dma_start(held[:, at, :], store[:, at, :]).then_inc(back[i], 16)
                for i in range(PARTS):
                    at = slice(i * N, i * N + N)
                    sp.wait_ge(added, i + 1)
                    sp.dma_start(out[:, at, :], X[:, at, :]).then_inc(written, 16)
                sp.wait_ge(written, 16 * PARTS)

            @block.vector
            def _(dve):
                for i in range(PARTS):
                    at = slice(i * N, i * N + N)
                    dve.wait_ge(back[i], 16)
                    nc.vector.tensor_tensor(X[:, at, :], X[:, at, :], held[:, at, :], ALU.add).then_inc(added, 1)


def mamba_moe_attention_local(nc, a):
    tiles = lambda v: v.rearrange("s (t p) c -> p (s t) c", p=P)
    with ExitStack() as ctx:
        X = ctx.enter_context(nc.sbuf_tensor("X", [P, TILES, P], F32))
        store = nc.dram_tensor("store", [P, TILES, P], F32).ap()
        x_in = ctx.enter_context(nc.semaphore("x_in"))
        ident = identity(nc, ctx)
        with nc.Block() as block:
            @block.sync
            def _(sp):
                sp.dma_start(X[:, :, :], tiles(a["x"])).then_inc(x_in, 16)
                sp.wait_ge(x_in, 16)
        selective_scan(nc, X, ident, a["in_w"], a["conv_w"], a["conv_b"], a["xp_w"], a["dt_w"], a["dt_b"],
                       a["a_log"], a["d_skip"], a["out_w"])
        expert_layer(nc, X, ident, a["gate_w"], a["e_w1"], a["e_b1"], a["e_w2"], a["e_b2"])
        full_attention(nc, X, ident, a["w_q"], a["b_q"], a["w_k"], a["b_k"], a["w_v"], a["b_v"], a["w_o"], a["b_o"],
                       a["table"])
        normalise_all(nc, X, store)
        local_layers(nc, X, ident, a["w_qkv"], a["q_scale"], a["k_scale"], a["l_wo"], a["ln_g"], a["ln_b"],
                     a["l_w1"], a["l_b1"], a["l_w2"], a["l_b2"], a["rotary"], a["masks"])
        add_and_store(nc, X, store, tiles(a["out"]))


def _rotary():
    import numpy as np
    dim, window, f = 64, 32, np.float32
    half = np.arange(0, dim, 2, dtype=f)
    inv_freq = (f(1.0) / f(10000.0) ** (half / f(dim))).astype(f)
    t = np.arange(SEQ, dtype=f)
    freqs = t[:, None] * inv_freq[None, :]
    freqs = np.concatenate([freqs, freqs], -1)
    base = (half + f(0.4 * dim)) / f(1.4 * dim)
    scale = base[None, :] ** ((t - SEQ // 2) / f(window // 2))[:, None]
    scale = np.concatenate([scale, scale], -1)
    sign = np.concatenate([-np.ones(dim // 2, f), np.ones(dim // 2, f)])
    cos, sin = np.cos(freqs), np.sin(freqs) * sign
    return np.stack([cos * scale, sin * scale, cos / scale, sin / scale], 1).astype(f)


def _masks():
    import numpy as np
    window, out = 32, []
    for tile, keys in ((0, np.arange(P)), (1, np.arange(P - window, 2 * P))):
        q, k = np.arange(P)[:, None] + P * tile, keys[None, :]
        sees = (k <= q) & (k >= q - window) & (k // window >= q // window - 1)
        out.append(np.where(sees, 0.0, -1e30))
    return np.concatenate(out, 1).astype(np.float32)


def kernel(**inputs):
    import numpy as _np
    import concourse.bacc as _bacc
    from concourse import mybir as _mybir
    from concourse.bass_utils import run_bass_kernel_spmd as _run

    given = {k: _np.asarray(v) for k, v in inputs.items()}
    turned = lambda name, *order: given[name].transpose(order)
    table = given["L1_attn_rel_table"]
    far = _np.broadcast_to(table[-1:], (2 * SEQ - 1 - table.shape[0], table.shape[1]))
    data = {
        "x": given["L0_attn_x"],
        "in_w": turned("L0_attn_in_proj_w", 0, 2, 1), "conv_w": given["L0_attn_conv_w"],
        "conv_b": given["L0_attn_conv_b"], "xp_w": turned("L0_attn_x_proj_w", 0, 2, 1),
        "dt_w": turned("L0_attn_dt_proj_w", 0, 2, 1), "dt_b": given["L0_attn_dt_proj_b"],
        "a_log": given["L0_attn_A_log"], "d_skip": given["L0_attn_D"], "out_w": turned("L0_attn_out_proj_w", 0, 2, 1),
        "gate_w": turned("L0_ffn_gate_w", 1, 0), "e_w1": turned("L0_ffn_w1", 0, 2, 1),
        "e_b1": turned("L0_ffn_b1", 1, 0), "e_w2": turned("L0_ffn_w2", 0, 2, 1), "e_b2": given["L0_ffn_b2"],
        "w_q": given["L1_attn_Wq"], "b_q": given["L1_attn_bq"], "w_k": given["L1_attn_Wk"], "b_k": given["L1_attn_bk"],
        "w_v": given["L1_attn_Wv"], "b_v": given["L1_attn_bv"], "w_o": given["L1_attn_Wo"], "b_o": given["L1_attn_bo"],
        "table": _np.concatenate([table, far], 0).T,
        "w_qkv": given["L1_ffn_Wqkv"], "q_scale": given["L1_ffn_q_scale"], "k_scale": given["L1_ffn_k_scale"],
        "l_wo": given["L1_ffn_Wo"], "ln_g": given["L1_ffn_ln_g"], "ln_b": given["L1_ffn_ln_b"],
        "l_w1": given["L1_ffn_W1"], "l_b1": given["L1_ffn_b1"], "l_w2": given["L1_ffn_W2"], "l_b2": given["L1_ffn_b2"],
        "rotary": _rotary(), "masks": _masks(),
    }
    nc = _bacc.Bacc("TRN2", target_bir_lowering=False, num_devices=1)
    arrays, tensors = {}, {}
    for name, v in data.items():
        v = _np.ascontiguousarray(v)
        arrays[f"in_{name}_dram"] = v
        tensors[name] = nc.dram_tensor(f"in_{name}_dram", v.shape, _mybir.dt.from_np(v.dtype), kind="ExternalInput").ap()
    tensors["out"] = nc.dram_tensor("out_0_dram", (SEQS, SEQ, P), F32, kind="ExternalOutput").ap()
    mamba_moe_attention_local(nc, tensors)
    r = _run(nc, [arrays], core_ids=[0])
    return r.results[0]["out_0_dram"]
```

```python
import concourse.bass as bass
from concourse import mybir
from contextlib import ExitStack

F32 = mybir.dt.float32
BF16 = mybir.dt.bfloat16
ALU = mybir.AluOpType
ACT = mybir.ActivationFunctionType
AX_X = mybir.AxisListType.X

P = 128
SEQS = 16
SEQ = 256
TILES = SEQS * SEQ // P
TPS = SEQ // P
EPS = 1e-5


def need(eng, sem, value):
    if isinstance(value, int) and value <= 0:
        return
    eng.wait_ge(sem, value)


class Semaphores:

    def __init__(self, nc, prefix):
        self.nc, self.prefix, self.all = nc, prefix, []

    def __call__(self, name):
        self.all.append(self.nc.alloc_semaphore(self.prefix + name))
        return self.all[-1]

    def clear(self):
        self.nc.clear_and_free_semaphores(self.all)
        self.nc.all_engine_barrier()


class Chain:

    def __init__(self, eng, sem):
        self.eng, self.sem, self.base, self.k, self.i, self.per = eng, sem, 0, 0, 0, 0

    def turn(self, i, per):
        if self.k and self.per == 0:
            self.base += self.k
        if self.per:
            assert self.k == self.per, (self.k, self.per)
        self.i, self.per, self.k = i, per, 0

    def end(self, turns):
        if self.per:
            assert self.k == self.per, (self.k, self.per)
        self.base += turns * self.per
        self.i, self.per, self.k = 0, 0, 0

    def now(self):
        return self.base + self.i * self.per + self.k

    def step(self, ins):
        ins.then_inc(self.sem, 1)
        self.k += 1

    def wait(self):
        self.eng.wait_ge(self.sem, self.now())

    def link(self, ins):
        self.step(ins)
        self.wait()


def identity(nc, ctx, name="ident"):
    ident = ctx.enter_context(nc.sbuf_tensor(name, [P, P], F32))
    zeroed = ctx.enter_context(nc.semaphore(name + "_zeroed"))
    with nc.Block() as block:
        @block.gpsimd
        def _(pool):
            nc.gpsimd.memset(ident[:, :], 0.0).then_inc(zeroed, 1)
            pool.wait_ge(zeroed, 1)
            nc.gpsimd.affine_select(out=ident[:, :], in_=ident[:, :], compare_op=ALU.not_equal, fill=1.0,
                                    base=0, pattern=[[-1, P]], channel_multiplier=1).then_inc(zeroed, 1)
            pool.wait_ge(zeroed, 2)
    return ident


def layernorm_stats(nc, X, mean, rstd, tag):
    with ExitStack() as ctx:
        def sb(name, shape):
            return ctx.enter_context(nc.sbuf_tensor(f"{name}_{tag}", shape, F32))

        stats = sb("stats", [P, TILES, 6])
        spread = sb("spread", [P, TILES])
        var = sb("var", [P, TILES])
        half = sb("half", [P, TILES])
        sem = Semaphores(nc, tag + "_")
        stats_done, ln_steps, var_ready, half_set = sem("stats_done"), sem("ln_steps"), sem("var_ready"), sem("half_set")
        with nc.Block() as block:
            @block.vector
            def _(dve):
                with dve.Fori(0, TILES) as t:
                    nc.vector.bn_stats(stats[:, bass.ds(t, 1), :], X[:, bass.ds(t, 1), :]).then_inc(stats_done, 1)
                dve.wait_ge(stats_done, TILES)
                c = Chain(dve, ln_steps)
                me, qe, mo, qo = (stats[:, :, k] for k in (1, 2, 4, 5))
                nc.vector.tensor_tensor(mean[:, :], me, mo, ALU.add).then_inc(ln_steps, 1)
                nc.vector.tensor_tensor(spread[:, :], me, mo, ALU.subtract).then_inc(ln_steps, 1)
                nc.vector.tensor_tensor(var[:, :], qe, qo, ALU.add).then_inc(ln_steps, 1)
                c.k = 3
                c.wait()
                c.step(nc.vector.tensor_scalar(mean[:, :], mean[:, :], 0.5, None, ALU.mult))
                c.step(nc.vector.tensor_tensor(spread[:, :], spread[:, :], spread[:, :], ALU.mult))
                c.link(nc.vector.tensor_scalar(var[:, :], var[:, :], 1.0 / P, EPS, ALU.mult, ALU.add))
                c.wait()
                nc.vector.scalar_tensor_tensor(out=var[:, :], in0=spread[:, :], scalar=0.25, in1=var[:, :],
                                               op0=ALU.mult, op1=ALU.add).then_inc(var_ready, 1)
                dve.wait_ge(var_ready, 1)

            @block.gpsimd
            def _(pool):
                nc.gpsimd.memset(half[:, :], -0.5).then_inc(half_set, 1)
                pool.wait_ge(half_set, 1)
                pool.wait_ge(var_ready, 1)
                nc.gpsimd.tensor_tensor(rstd[:, :], var[:, :], half[:, :], ALU.pow).then_inc(half_set, 1)
                pool.wait_ge(half_set, 2)
        sem.clear()


def selective_scan(nc, X, ident, in_w, conv_w, conv_b, xp_w, dt_w, dt_b, a_log, d_skip, out_w):
    H, DH, DI, N, K, R = 8, 16, 32, 16, 4, 8
    G, HG = 2, 4
    TOK = SEQS * SEQ
    NC_ = 4
    CHUNKS = N // NC_
    W = NC_ * SEQ
    with ExitStack() as ctx:
        def sb(name, shape):
            return ctx.enter_context(nc.sbuf_tensor("m_" + name, shape, F32))

        sem = Semaphores(nc, "m_")

        mean, rstd = sb("mean", [P, TILES]), sb("rstd", [P, TILES])
        layernorm_stats(nc, X, mean, rstd, "m")
        Wu = sb("Wu", [P, G, P])
        Wz = sb("Wz", [P, G, P])
        xpw = sb("xpw", [P, G, R + 2 * N])
        Wdx = sb("Wdx", [P, G, HG * R])
        WBC = sb("WBC", [P, G, 2 * N, P])
        Wdt = sb("Wdt", [R * HG, G, P])
        Wo = sb("Wo", [P, G, HG * DH])
        convw, convb, dtb, dsk = sb("convw", [P, G, K]), sb("convb", [P, G]), sb("dtb", [P, G]), sb("dsk", [P, G])
        A = sb("A", [P, G, N])
        UC = sb("UC", [P, G, TOK])
        ZS = sb("ZS", [P, G, TOK])
        DELTA = sb("DELTA", [P, G, TOK])
        zeroed, loaded, a_ready = sem("zeroed"), sem("loaded"), sem("a_ready")
        a_ready_n, placed = sem("a_negated"), sem("placed")
        LOADS = 16 * (6 + 4 * H)
        with nc.Block() as block:
            @block.vector
            def _(dve):
                for w in (Wu[:, :, :], Wz[:, :, :], Wdt[:, :, :], Wo[:, :, :], Wdx[:, :, :], WBC[:, :, :, :]):
                    nc.vector.memset(w, 0.0).then_inc(zeroed, 1)
                dve.wait_ge(zeroed, 6)
                dve.wait_ge(loaded, LOADS)
                for h in range(H):
                    g, hh = divmod(h, HG)
                    rows = slice(DI * hh, DI * hh + DI)
                    nc.vector.tensor_copy(Wdx[rows, g, R * hh:R * hh + R], xpw[rows, g, 0:R]).then_inc(placed, 1)
                    nc.vector.tensor_copy(WBC[rows, g, :, rows], xpw[rows, g, R:].unsqueeze(2).to_broadcast(
                        [DI, 2 * N, DI])).then_inc(placed, 1)
                dve.wait_ge(placed, 2 * H)
                dve.wait_ge(a_ready, 1)
                nc.vector.tensor_scalar(A[:, :, :], A[:, :, :], -1.0, None, ALU.mult).then_inc(a_ready_n, 1)
                dve.wait_ge(a_ready_n, 1)

            @block.sync
            def _(sp):
                n = 0
                for dst, src in ((convw[:, :, :], conv_w.rearrange("(g h) d k -> (h d) g k", g=G)),
                                 (A[:, :, :], a_log.rearrange("(g h) d n -> (h d) g n", g=G)),
                                 (xpw[:, :, :], xp_w.rearrange("(g h) d e -> (h d) g e", g=G))):
                    sp.dma_start(dst, src).then_inc(loaded, 16)
                    n += 1
                for dst, src in ((convb, conv_b), (dtb, dt_b), (dsk, d_skip)):
                    with nc.allow_non_contiguous_dma(reason="small"):
                        sp.dma_start(dst[:, :], src.rearrange("(g h) d -> (h d) g", g=G)).then_inc(loaded, 16)
                    n += 1
                sp.wait_ge(zeroed, 6)
                for h in range(H):
                    g, hh = divmod(h, HG)
                    rows, cols = slice(DH * h, DH * h + DH), slice(DI * hh, DI * hh + DI)
                    for dst, src in ((Wu[rows, g, cols], in_w[h, :, 0:DI]), (Wz[rows, g, cols], in_w[h, :, DI:2 * DI]),
                                     (Wdt[R * hh:R * hh + R, g, cols], dt_w[h]),
                                     (Wo[cols, g, DH * hh:DH * hh + DH], out_w[h])):
                        with nc.allow_non_contiguous_dma(reason="small"):
                            sp.dma_start(dst, src).then_inc(loaded, 16)
                        n += 1
                assert 16 * n == LOADS
                sp.wait_ge(loaded, LOADS)

            @block.scalar
            def _(act):
                act.wait_ge(loaded, LOADS)
                nc.scalar.activation(A[:, :, :], A[:, :, :], ACT.Exp).then_inc(a_ready, 1)

        with ExitStack() as inner:
            def isb(name, shape):
                return inner.enter_context(nc.sbuf_tensor("m1_" + name, shape, F32))

            def ips(name, cols):
                return inner.enter_context(nc.psum_tensor("m1_" + name, [P, cols], F32))

            xn = isb("xn", [P, TPS, P])
            xnT = isb("xnT", [P, SEQ])
            up = [isb(f"up{i}", [P, G, K - 1 + SEQ]) for i in range(2)]
            cv = [isb(f"cv{i}", [P, G, SEQ]) for i in range(2)]
            dts = isb("dts", [R * HG, G, SEQ])
            ps_x, ps_u, ps_z = ips("ps_x", 2 * SEQ), ips("ps_u", G * SEQ), ips("ps_z", G * SEQ)
            ps_d, ps_e = ips("ps_d", G * SEQ), ips("ps_e", G * SEQ)
            normed, turned, xnt_ready = sem("normed"), sem("turned"), sem("xnt_ready")
            projected, u_ready, z_used, conv_steps = sem("projected"), sem("u_ready"), sem("z_used"), sem("conv_steps")
            conv_ready, uc_ready, dt_made, dt_ready = sem("conv_ready"), sem("uc_ready"), sem("dt_made"), sem("dt_ready")
            raw_made, raw_ready, pads = sem("raw_made"), sem("raw_ready"), sem("pads")

            def sequences(eng, turn):
                turn(0, 0, True, False)
                turn(1, 1, False, False)
                with eng.Fori(0, SEQS // 2 - 2) as pair:
                    turn(2 * pair + 2, 0, False, False)
                    turn(2 * pair + 3, 1, False, False)
                turn(SEQS - 2, 0, False, False)
                turn(SEQS - 1, 1, False, True)

            with nc.Block() as block:
                @block.vector
                def _(dve):
                    for u in up:
                        nc.vector.memset(u[:, :, 0:K - 1], 0.0).then_inc(pads, 1)
                    dve.wait_ge(pads, 2)

                    def norm(b):
                        need(dve, turned, b)
                        for t in range(TPS):
                            at = bass.ds(b * TPS + t, 1)
                            nc.vector.tensor_scalar(xn[:, t, :], X[:, at, :].rearrange("p a c -> p (a c)"),
                                                    mean[:, at], rstd[:, at],
                                                    ALU.subtract, ALU.mult).then_inc(normed, 1)

                    def convolve(b, s):
                        dve.wait_ge(u_ready, b + 1)
                        need(dve, uc_ready, b - 1)
                        for k in reversed(range(K)):
                            for g in range(G):
                                tap = up[s][:, g, k:k + SEQ]
                                if k == K - 1:
                                    ins = nc.vector.tensor_scalar(cv[s][:, g, :], tap, convw[:, g, k:k + 1],
                                                                  convb[:, g:g + 1], ALU.mult, ALU.add)
                                else:
                                    ins = nc.vector.scalar_tensor_tensor(out=cv[s][:, g, :], in0=tap,
                                                                         scalar=convw[:, g, k:k + 1],
                                                                         in1=cv[s][:, g, :], op0=ALU.mult, op1=ALU.add)
                            if k:
                                ins.then_inc(conv_steps, 1)
                                dve.wait_ge(conv_steps, (K - 1) * b + K - k)
                            else:
                                ins.then_inc(conv_ready, 1)

                    def turn(b, s, first, last):
                        if not last:
                            norm(b + 1)
                        convolve(b, s)

                    norm(0)
                    sequences(dve, turn)

                @block.tensor
                def _(pe):
                    def transpose_x(b):
                        pe.wait_ge(normed, TPS * b + TPS)
                        need(pe, xnt_ready, b)
                        for t in range(TPS):
                            ins = nc.tensor.transpose(ps_x[:, t * P:t * P + P], xn[:, t, :], ident[:, :])
                        ins.then_inc(turned, 1)

                    def project(b):
                        pe.wait_ge(xnt_ready, b + 1)
                        need(pe, u_ready, b)
                        need(pe, z_used, b)
                        for dst, w in ((ps_u, Wu), (ps_z, Wz)):
                            for g in range(G):
                                ins = nc.tensor.matmul(dst[:, g * SEQ:g * SEQ + SEQ], w[:, g, :], xnT[:, :],
                                                       start=True, stop=True)
                        ins.then_inc(projected, 1)

                    def make_dt(b):
                        pe.wait_ge(uc_ready, b + 1)
                        need(pe, dt_ready, b)
                        for g in range(G):
                            ins = nc.tensor.matmul(ps_d[0:R * HG, g * SEQ:g * SEQ + SEQ], Wdx[:, g, :],
                                                   UC[:, g, bass.ds(b * SEQ, SEQ)], start=True, stop=True)
                        ins.then_inc(dt_made, 1)

                    def make_raw(b):
                        pe.wait_ge(dt_ready, b + 1)
                        need(pe, raw_ready, b)
                        for g in range(G):
                            ins = nc.tensor.matmul(ps_e[:, g * SEQ:g * SEQ + SEQ], Wdt[:, g, :], dts[:, g, :],
                                                   start=True, stop=True)
                        ins.then_inc(raw_made, 1)

                    def turn(b, s, first, last):
                        if not last:
                            transpose_x(b + 1)
                        if not first:
                            make_dt(b - 1)
                        if not last:
                            project(b + 1)
                        if not first:
                            make_raw(b - 1)

                    transpose_x(0)
                    project(0)
                    sequences(pe, turn)
                    make_dt(SEQS - 1)
                    make_raw(SEQS - 1)

                @block.scalar
                def _(act):
                    act.wait_ge(pads, 2)

                    def channels(b):
                        act.wait_ge(turned, b + 1)
                        need(act, projected, b)
                        nc.scalar.copy(xnT[:, :], ps_x[:, 0:SEQ]).then_inc(xnt_ready, 1)

                    def keep_u(b, s):
                        act.wait_ge(projected, b + 1)
                        need(act, conv_ready, b - 1)
                        nc.scalar.copy(up[s][:, :, K - 1:], ps_u[:, :].rearrange("p (g l) -> p g l", g=G)).then_inc(u_ready, 1)

                    def keep_z(b):
                        nc.scalar.activation(ZS[:, :, bass.ds(b * SEQ, SEQ)], ps_z[:, :].rearrange("p (g l) -> p g l", g=G),
                                             ACT.Silu).then_inc(z_used, 1)

                    def silu_u(b, s):
                        act.wait_ge(conv_ready, b + 1)
                        nc.scalar.activation(UC[:, :, bass.ds(b * SEQ, SEQ)], cv[s][:, :, :], ACT.Silu).then_inc(uc_ready, 1)

                    def keep_dt(b):
                        act.wait_ge(dt_made, b + 1)
                        need(act, raw_made, b)
                        nc.scalar.copy(dts[:, :, :], ps_d[0:R * HG, :].rearrange("p (g l) -> p g l", g=G)).then_inc(dt_ready, 1)

                    def keep_raw(b):
                        act.wait_ge(raw_made, b + 1)
                        for g in range(G):
                            ins = nc.scalar.activation(DELTA[:, g, bass.ds(b * SEQ, SEQ)], ps_e[:, g * SEQ:g * SEQ + SEQ],
                                                       ACT.Identity, bias=dtb[:, g:g + 1])
                        ins.then_inc(raw_ready, 1)

                    def turn(b, s, first, last):
                        if not last:
                            channels(b + 1)
                        if not first:
                            keep_dt(b - 1)
                        if not last:
                            keep_u(b + 1, 1 - s)
                            keep_z(b + 1)
                        if not first:
                            keep_raw(b - 1)
                        silu_u(b, s)

                    channels(0)
                    keep_u(0, 0)
                    keep_z(0)
                    sequences(act, turn)
                    keep_dt(SEQS - 1)
                    keep_raw(SEQS - 1)

        with ExitStack() as inner:
            PIECE = 2048
            PIECES = G * TOK // PIECE
            tail = [inner.enter_context(nc.sbuf_tensor(f"m2_tail{i}", [P, PIECE], F32)) for i in range(2)]
            flat = DELTA[:, :, :].rearrange("p g t -> p (g t)")
            abs_done, exp_done, ln_ready, sp_done = sem("abs_done"), sem("exp_done"), sem("ln_ready"), sem("sp_done")
            with nc.Block() as block:
                @block.scalar
                def _(act):
                    for i in range(PIECES):
                        at, v = slice(i * PIECE, (i + 1) * PIECE), tail[i % 2][:, :]
                        need(act, sp_done, i - 1)
                        nc.scalar.activation(v, flat[:, at], ACT.Abs).then_inc(abs_done, 1)
                        act.wait_ge(abs_done, i + 1)
                        nc.scalar.activation(v, v, ACT.Exp, scale=-1.0).then_inc(exp_done, 1)
                        act.wait_ge(exp_done, i + 1)
                        nc.scalar.activation(v, v, ACT.Ln, bias=1.0).then_inc(ln_ready, 1)

                @block.vector
                def _(dve):
                    for i in range(PIECES):
                        at, v = slice(i * PIECE, (i + 1) * PIECE), tail[i % 2][:, :]
                        dve.wait_ge(ln_ready, i + 1)
                        nc.vector.scalar_tensor_tensor(out=flat[:, at], in0=flat[:, at], scalar=0.0, in1=v,
                                                       op0=ALU.max, op1=ALU.add).then_inc(sp_done, 1)

        with ExitStack() as inner:
            def isb(name, shape):
                return inner.enter_context(nc.sbuf_tensor("m3_" + name, shape, F32))

            def ips(name, cols):
                return inner.enter_context(nc.psum_tensor("m3_" + name, [P, cols], F32))

            UNITS = G * CHUNKS
            POOL = 2
            dA = [isb(f"dA{i}", [P, NC_, SEQ]) for i in range(2)]
            dBu = isb("dBu", [P, NC_, SEQ])
            hs = isb("hs", [P, NC_, SEQ])
            hc = [isb(f"hc{i}", [P, NC_, SEQ]) for i in range(2)]
            du = isb("du", [P, SEQ])
            part = isb("part", [P, 2, SEQ])
            ysum = isb("ysum", [P, G, SEQ])
            yT = isb("yT", [P, G, SEQ])
            ps_B = [ips(f"ps_B{i}", W) for i in range(2)]
            ps_C = ips("ps_C", W)
            ps_o = ips("ps_o", TPS * P)
            dA_zero, B_ready, C_ready, dA_ready = sem("dA_zero"), sem("B_ready"), sem("C_ready"), sem("dA_ready")
            du_ready, dBu_done, scan_done, hc_ready = sem("du_ready"), sem("dBu_done"), sem("scan_done"), sem("hc_ready")
            pool_steps, y_partial, y_ready = sem("pool_steps"), sem("y_partial"), sem("y_ready")
            alone = sem("alone")
            y_steps, out_made, x_added = sem("y_steps"), sem("out_made"), sem("x_added")

            with nc.Block() as block:
                @block.tensor
                def _(pe):
                    def out_proj(b):
                        pe.wait_ge(y_ready, G * b + G)
                        need(pe, x_added, b)
                        for t in range(TPS):
                            for g in range(G):
                                o = t * P + g * HG * DH
                                ins = nc.tensor.matmul(ps_o[:, o:o + HG * DH], yT[:, g, t * P:t * P + P], Wo[:, g, :],
                                                       start=True, stop=True)
                        ins.then_inc(out_made, 1)

                    def turn(b, first):
                        seq = bass.ds(b * SEQ, SEQ)
                        for u in range(UNITS):
                            g, c = divmod(u, CHUNKS)
                            n = UNITS * b + u
                            need(pe, dBu_done, n - 1)
                            for ps, column, done in ((ps_B[u % 2], 0, B_ready), (ps_C, N, C_ready)):
                                if done is C_ready:
                                    need(pe, hc_ready, n)
                                for j in range(NC_):
                                    ins = nc.tensor.matmul(ps[:, j * SEQ:j * SEQ + SEQ],
                                                           WBC[:, g, column + NC_ * c + j, :], UC[:, g, seq],
                                                           start=True, stop=True)
                                ins.then_inc(done, 1)
                            if u == 1 and not first:
                                out_proj(b - 1)

                    turn(0, True)
                    turn(1, False)
                    with pe.Fori(2, SEQS) as b:
                        turn(b, False)
                    out_proj(SEQS - 1)

                @block.scalar
                def _(act):
                    act.wait_ge(dA_zero, 2)

                    def turn(b):
                        rest = bass.ds(b * SEQ + 1, SEQ - 1)
                        for u in range(UNITS):
                            g, c = divmod(u, CHUNKS)
                            need(act, scan_done, UNITS * b + u - 1)
                            act.sem_inc(alone, 1)
                            for j in range(NC_):
                                s = NC_ * c + j
                                ins = nc.scalar.activation(dA[u % 2][:, j, 1:], DELTA[:, g, rest], ACT.Exp,
                                                           scale=A[:, g, s:s + 1])
                            ins.then_inc(dA_ready, 1)

                    turn(0)
                    with act.Fori(1, SEQS) as b:
                        turn(b)

                @block.vector
                def _(dve):
                    for i in range(2):
                        nc.vector.memset(dA[i][:, :, 0:1], 0.0).then_inc(dA_zero, 1)
                    dve.wait_ge(dA_zero, 2)
                    c2 = Chain(dve, y_steps)

                    def gate(b, g):
                        seq = bass.ds(b * SEQ, SEQ)
                        dve.wait_ge(y_partial, (CHUNKS - 1) * (G * b + g + 1))
                        need(dve, out_made, b)
                        c2.link(nc.vector.scalar_tensor_tensor(out=yT[:, g, :], in0=UC[:, g, seq], scalar=dsk[:, g:g + 1],
                                                               in1=ysum[:, g, :], op0=ALU.mult, op1=ALU.add))
                        nc.vector.tensor_tensor(yT[:, g, :], yT[:, g, :], ZS[:, g, seq], ALU.mult).then_inc(y_ready, 1)

                    def add_out(b):
                        dve.wait_ge(out_made, b + 1)
                        tiles = bass.ds(b * TPS, TPS)
                        nc.vector.tensor_tensor(X[:, tiles, :], X[:, tiles, :],
                                                ps_o[:, :].rearrange("p (t c) -> p t c", t=TPS), ALU.add).then_inc(x_added, 1)

                    def turn(b, first):
                        seq = bass.ds(b * SEQ, SEQ)
                        for u in range(UNITS):
                            g, c = divmod(u, CHUNKS)
                            n = UNITS * b + u
                            if c == 0:
                                need(dve, dBu_done, n)
                                nc.vector.tensor_tensor(du[:, :], DELTA[:, g, seq], UC[:, g, seq], ALU.mult).then_inc(du_ready, 1)
                                dve.wait_ge(du_ready, G * b + g + 1)
                            dve.wait_ge(B_ready, n + 1)
                            need(dve, scan_done, n)
                            nc.vector.tensor_tensor(dBu[:, :, :], ps_B[u % 2][:, :].rearrange("p (j l) -> p j l", j=NC_),
                                                    du[:, :].unsqueeze(1).to_broadcast([P, NC_, SEQ]),
                                                    ALU.mult).then_inc(dBu_done, 1)
                            dve.wait_ge(dBu_done, n + 1)
                            dve.wait_ge(dA_ready, n + 1)
                            need(dve, hc_ready, n)
                            nc.vector.tensor_tensor_scan(hs[:, :, :].rearrange("p j l -> p (j l)"),
                                                         dA[u % 2][:, :, :].rearrange("p j l -> p (j l)"),
                                                         dBu[:, :, :].rearrange("p j l -> p (j l)"), 0.0,
                                                         ALU.mult, ALU.add).then_inc(scan_done, 1)
                            dve.wait_ge(scan_done, n + 1)
                            dve.wait_ge(C_ready, n + 1)
                            need(dve, pool_steps, POOL * (n - 1))
                            nc.vector.tensor_tensor(hc[u % 2][:, :, :], ps_C[:, :].rearrange("p (j l) -> p j l", j=NC_),
                                                    hs[:, :, :], ALU.mult).then_inc(hc_ready, 1)
                            if u == CHUNKS:
                                gate(b, 0)
                            if u == 0 and not first:
                                gate(b - 1, 1)
                            if u == 2 and not first:
                                add_out(b - 1)

                    c2.turn(0, 1)
                    turn(0, True)
                    c2.end(1)
                    c2.turn(0, 2)
                    turn(1, False)
                    c2.end(1)
                    with dve.Fori(2, SEQS) as b:
                        c2.turn(b - 2, 2)
                        turn(b, False)
                    c2.end(SEQS - 2)
                    gate(SEQS - 1, 1)
                    add_out(SEQS - 1)
                    dve.wait_ge(x_added, SEQS)

                @block.gpsimd
                def _(pool):
                    def turn(b):
                        for u in range(UNITS):
                            g, c = divmod(u, CHUNKS)
                            n = UNITS * b + u
                            pool.wait_ge(hc_ready, n + 1)
                            if c == 0:
                                need(pool, y_ready, G * (b - 1) + g + 1 if not isinstance(b, int) or b else 0)
                            v = hc[u % 2]
                            nc.gpsimd.tensor_tensor(part[:, :, :], v[:, 0:2, :], v[:, 2:4, :], ALU.add).then_inc(pool_steps, 1)
                            pool.wait_ge(pool_steps, POOL * n + 1)
                            if c == 0:
                                nc.gpsimd.tensor_tensor(ysum[:, g, :], part[:, 0, :], part[:, 1, :], ALU.add).then_inc(pool_steps, 1)
                                pool.wait_ge(pool_steps, POOL * n + 2)
                            else:
                                nc.gpsimd.tensor_tensor(part[:, 0, :], part[:, 0, :], part[:, 1, :], ALU.add).then_inc(pool_steps, 1)
                                pool.wait_ge(pool_steps, POOL * n + 2)
                                ins = nc.gpsimd.tensor_tensor(ysum[:, g, :], ysum[:, g, :], part[:, 0, :], ALU.add)
                                ins.then_inc(y_partial, 1)
                                pool.wait_ge(y_partial, (CHUNKS - 1) * (G * b + g) + c)

                    turn(0)
                    with pool.Fori(1, SEQS) as b:
                        turn(b)
        sem.clear()


def expert_layer(nc, X, ident, gate_w, w1, b1, w2, b2):
    E = 8
    CAP = int(1.25 * SEQS * SEQ / E)
    TG = 4
    GROUPS = TILES // TG
    with ExitStack() as ctx:
        def sb(name, shape):
            return ctx.enter_context(nc.sbuf_tensor("e_" + name, shape, F32))

        def ps(name, cols):
            return ctx.enter_context(nc.psum_tensor("e_" + name, [P, cols], F32))

        sem = Semaphores(nc, "e_")

        mean, rstd = sb("mean", [P, TILES]), sb("rstd", [P, TILES])
        layernorm_stats(nc, X, mean, rstd, "e")
        W1, W2 = sb("W1", [P, E, P]), sb("W2", [P, E, P])
        B1, B2, Wg = sb("B1", [P, E]), sb("B2", [E, P]), sb("Wg", [P, E])
        XT = sb("XT", [P, SEQS, SEQ])
        xn = sb("xn", [P, TPS, P])
        xw = sb("xw", [P, SEQ])
        L = sb("L", [P, TILES, E])
        top, total = sb("top", [P, TILES]), sb("total", [P, TILES])
        above, level = sb("above", [P, TILES, E, E]), sb("level", [P, TILES, E, E])
        earlier = sb("earlier", [P, E, E])
        rank = sb("rank", [P, TILES, E])
        counts, keep, ones = sb("counts", [P, E]), sb("keep", [P, E]), sb("ones", [P, P])
        gw = sb("gw", [P, TG, E])
        gT = sb("gT", [E, TG * P])
        h = [sb(f"h{i}", [P, TG * P]) for i in range(2)]
        ps_x, ps_l, ps_c = ps("ps_x", 512), ps("ps_l", 512), ps("ps_c", 512)
        ps_h = [ps(f"ps_h{i}", 512) for i in range(2)]
        ps_y = [ps(f"ps_y{i}", 512) for i in range(2)]
        ps_b = ps("ps_b", 512)
        loaded, normed, turned, xw_ready, xt_ready = (sem(s) for s in ("loaded", "normed", "turned", "xw_ready", "xt_ready"))
        logits_made, logits_ready, pick, exp_done = (sem(s) for s in ("logits_made", "logits_ready", "pick", "exp_done"))
        counted, summed, consts = sem("counted"), sem("summed"), sem("consts")
        h_made, h_ready, y_made, y_added = sem("h_made"), sem("h_ready"), sem("y_made"), sem("y_added")
        gt_made, gt_ready, bias_made, bias_added = sem("gt_made"), sem("gt_ready"), sem("bias_made"), sem("bias_added")
        weighted, gw_ready = sem("weighted"), sem("gw_ready")

        with nc.Block() as block:
            @block.sync
            def _(sp):
                for dst, src in ((W1[:, :, :], w1.rearrange("e h f -> h e f")), (W2[:, :, :], w2.rearrange("e f g -> f e g")),
                                 (B1[:, :], b1), (B2[:, :], b2), (Wg[:, :], gate_w)):
                    sp.dma_start(dst, src).then_inc(loaded, 16)

            @block.gpsimd
            def _(pool):
                nc.gpsimd.memset(ones[:, :], 1.0).then_inc(consts, 1)
                nc.gpsimd.memset(earlier[:, :, :], 0.0).then_inc(consts, 1)
                pool.wait_ge(consts, 2)
                for e in range(1, E):
                    nc.gpsimd.memset(earlier[:, e, 0:e], 1.0).then_inc(consts, 1)

                def turn(b):
                    pool.wait_ge(xw_ready, b + 1)
                    nc.gpsimd.tensor_copy(XT[:, bass.ds(b, 1), :].rearrange("p a l -> p (a l)"), xw[:, :]).then_inc(xt_ready, 1)

                with pool.Fori(0, SEQS) as b:
                    turn(b)
                pool.wait_ge(weighted, 1)

                def group(r):
                    need(pool, gt_made, r)
                    nc.gpsimd.tensor_copy(gw[:, :, :], L[:, bass.ds(r * TG, TG), :]).then_inc(gw_ready, 1)

                group(0)
                with pool.Fori(1, GROUPS) as r:
                    group(r)

            @block.vector
            def _(dve):
                def turn(b):
                    need(dve, turned, b)
                    for t in range(TPS):
                        at = bass.ds(b * TPS + t, 1)
                        nc.vector.tensor_scalar(xn[:, t, :], X[:, at, :].rearrange("p a c -> p (a c)"),
                                                mean[:, at], rstd[:, at], ALU.subtract, ALU.mult).then_inc(normed, 1)
                    dve.wait_ge(logits_made, b + 1)
                    nc.vector.tensor_copy(L[:, bass.ds(b * TPS, TPS), :],
                                          ps_l[:, 0:TPS * E].rearrange("p (t e) -> p t e", t=TPS)).then_inc(logits_ready, 1)

                turn(0)
                with dve.Fori(1, SEQS) as b:
                    turn(b)
                dve.wait_ge(logits_ready, SEQS)
                dve.wait_ge(consts, 2 + E - 1)
                c = Chain(dve, pick)
                per_token = lambda v: v[:, :].unsqueeze(2).to_broadcast([P, TILES, E])
                c.link(nc.vector.tensor_reduce(top[:, :], L[:, :, :], AX_X, ALU.max))
                c.link(nc.vector.tensor_tensor(L[:, :, :], L[:, :, :], per_token(top), ALU.subtract))
                dve.wait_ge(exp_done, 1)
                c.link(nc.vector.tensor_reduce(total[:, :], L[:, :, :], AX_X, ALU.add))
                c.link(nc.vector.reciprocal(total[:, :], total[:, :]))
                c.link(nc.vector.tensor_tensor(L[:, :, :], L[:, :, :], per_token(total), ALU.mult))
                mine = L[:, :, :].unsqueeze(3).to_broadcast([P, TILES, E, E])
                other = L[:, :, :].unsqueeze(2).to_broadcast([P, TILES, E, E])
                c.step(nc.vector.tensor_tensor(above[:, :, :, :], other, mine, ALU.is_gt))
                c.link(nc.vector.tensor_tensor(level[:, :, :, :], other, mine, ALU.is_equal))
                c.link(nc.vector.tensor_tensor(
                    level[:, :, :, :].rearrange("p t e f -> p t (e f)"), level[:, :, :, :].rearrange("p t e f -> p t (e f)"),
                    earlier[:, :, :].rearrange("p e f -> p (e f)").unsqueeze(1).to_broadcast([P, TILES, E * E]), ALU.mult))
                c.link(nc.vector.tensor_tensor(above[:, :, :, :], above[:, :, :, :], level[:, :, :, :], ALU.add))
                c.link(nc.vector.tensor_reduce(rank[:, :, :], above[:, :, :, :], AX_X, ALU.add))
                c.link(nc.vector.tensor_scalar(rank[:, :, :], rank[:, :, :], 1.5, None, ALU.is_lt))
                nc.vector.tensor_reduce(counts[:, :], rank[:, :, :].rearrange("p t e -> p e t"), AX_X,
                                        ALU.add).then_inc(counted, 1)
                c.link(nc.vector.tensor_tensor(L[:, :, :], L[:, :, :], rank[:, :, :], ALU.mult))
                dve.wait_ge(summed, 1)
                c.link(nc.vector.tensor_scalar(keep[:, :], ps_c[:, 0:E], CAP + 0.5, None, ALU.is_lt))
                nc.vector.tensor_tensor(L[:, :, :], L[:, :, :], keep[:, :].unsqueeze(1).to_broadcast([P, TILES, E]),
                                        ALU.mult).then_inc(weighted, 1)
                dve.wait_ge(weighted, 1)

                def experts(r):
                    for e in range(E):
                        n = E * r + e
                        dve.wait_ge(y_made, n + 1)
                        if e:
                            dve.wait_ge(y_added, TG * n)
                        else:
                            need(dve, bias_added, r)
                        for t in range(TG):
                            row = X[:, bass.ds(r * TG + t, 1), :].rearrange("p a c -> p (a c)")
                            weight = L[:, bass.ds(r * TG + t, 1), e]
                            nc.vector.scalar_tensor_tensor(out=row, in0=ps_y[e % 2][:, t * P:t * P + P], scalar=weight,
                                                           in1=row, op0=ALU.mult, op1=ALU.add).then_inc(y_added, 1)
                    dve.wait_ge(bias_made, r + 1)
                    dve.wait_ge(y_added, TG * (E * r + E))
                    rows = X[:, bass.ds(r * TG, TG), :]
                    nc.vector.tensor_tensor(rows, rows, ps_b[:, :].rearrange("p (t c) -> p t c", t=TG),
                                            ALU.add).then_inc(bias_added, 1)

                experts(0)
                with dve.Fori(1, GROUPS) as r:
                    experts(r)
                dve.wait_ge(bias_added, GROUPS)

            @block.scalar
            def _(act):
                def turn(b):
                    act.wait_ge(turned, b + 1)
                    need(act, logits_made, b)
                    need(act, xt_ready, b)
                    nc.scalar.copy(xw[:, :], ps_x[:, 0:SEQ]).then_inc(xw_ready, 1)

                turn(0)
                with act.Fori(1, SEQS) as b:
                    turn(b)
                act.wait_ge(pick, 2)
                nc.scalar.activation(L[:, :, :], L[:, :, :], ACT.Exp).then_inc(exp_done, 1)
                act.wait_ge(loaded, 16 * 5)

                def experts(r):
                    for e in range(E):
                        n = E * r + e
                        act.wait_ge(h_made, n + 1)
                        need(act, y_made, n - 1)
                        nc.scalar.activation(h[e % 2][:, :], ps_h[e % 2][:, :], ACT.Silu, bias=B1[:, e:e + 1]).then_inc(h_ready, 1)
                    act.wait_ge(gt_made, r + 1)
                    need(act, bias_made, r)
                    nc.scalar.copy(gT[:, :], ps_x[0:E, :]).then_inc(gt_ready, 1)

                experts(0)
                with act.Fori(1, GROUPS) as r:
                    experts(r)

            @block.tensor
            def _(pe):
                pe.wait_ge(loaded, 16 * 5)

                def turn(b):
                    pe.wait_ge(normed, TPS * b + TPS)
                    need(pe, xw_ready, b)
                    for t in range(TPS):
                        ins = nc.tensor.transpose(ps_x[:, t * P:t * P + P], xn[:, t, :], ident[:, :])
                    ins.then_inc(turned, 1)
                    pe.wait_ge(xw_ready, b + 1)
                    need(pe, logits_ready, b)
                    for t in range(TPS):
                        ins = nc.tensor.matmul(ps_l[:, t * E:t * E + E], xw[:, t * P:t * P + P], Wg[:, :],
                                               start=True, stop=True)
                    ins.then_inc(logits_made, 1)

                turn(0)
                with pe.Fori(1, SEQS) as b:
                    turn(b)
                pe.wait_ge(counted, 1)
                nc.tensor.matmul(ps_c[:, 0:E], ones[:, :], counts[:, :], start=True, stop=True).then_inc(summed, 1)
                pe.wait_ge(xt_ready, SEQS)
                pe.wait_ge(weighted, 1)

                def first(r, e):
                    n = E * r + e
                    need(pe, h_ready, n - 1)
                    nc.tensor.matmul(ps_h[e % 2][:, :], W1[:, e, :],
                                     XT[:, bass.ds(r * (TG // TPS), TG // TPS), :].rearrange("p a l -> p (a l)"),
                                     start=True, stop=True).then_inc(h_made, 1)

                def second(r, e):
                    n = E * r + e
                    pe.wait_ge(h_ready, n + 1)
                    need(pe, y_added, TG * (n - 1))
                    for t in range(TG):
                        ins = nc.tensor.matmul(ps_y[e % 2][:, t * P:t * P + P], h[e % 2][:, t * P:t * P + P], W2[:, e, :],
                                               start=True, stop=True)
                    ins.then_inc(y_made, 1)

                def experts(r):
                    first(r, 0)
                    for e in range(E):
                        if e + 1 < E:
                            first(r, e + 1)
                        second(r, e)
                    pe.wait_ge(gw_ready, r + 1)
                    need(pe, gt_ready, r)
                    for t in range(TG):
                        ins = nc.tensor.transpose(ps_x[0:E, t * P:t * P + P],
                                                  gw[:, t, :], ident[:, :])
                    ins.then_inc(gt_made, 1)
                    pe.wait_ge(gt_ready, r + 1)
                    need(pe, bias_added, r)
                    for t in range(TG):
                        ins = nc.tensor.matmul(ps_b[:, t * P:t * P + P], gT[:, t * P:t * P + P], B2[:, :],
                                               start=True, stop=True)
                    ins.then_inc(bias_made, 1)

                experts(0)
                with pe.Fori(1, GROUPS) as r:
                    experts(r)
        sem.clear()


def full_attention(nc, X, ident, w_q, b_q, w_k, b_k, w_v, b_v, w_o, b_o, table):
    H, D = 16, 8
    SCALE = float(D) ** -0.5
    SPREAD = P + D
    SPAN = 2 * SEQ - 1
    RING = 4
    AHEAD = 6
    TURN, WEIGH = 2, 3
    with ExitStack() as ctx:
        def sb(name, shape):
            return ctx.enter_context(nc.sbuf_tensor("a_" + name, shape, F32))

        def ps(name, cols=512):
            return ctx.enter_context(nc.psum_tensor("a_" + name, [P, cols], F32))

        sem = Semaphores(nc, "a_")

        mean, rstd = sb("mean", [P, TILES]), sb("rstd", [P, TILES])
        layernorm_stats(nc, X, mean, rstd, "a")
        W = sb("W", [P, 4, P])
        bq, bk = sb("bq", [P, 1]), sb("bk", [P, 1])
        bv, bo = sb("bv", [P, P]), sb("bo", [P, P])
        hmask = sb("hmask", [P, H])
        near = sb("near", [P, H, SEQ])
        far = sb("far", [P, H])
        xn, xT, xTr = sb("xn", [P, TPS, P]), sb("xT", [P, SEQ]), sb("xTr", [P, SEQ])
        qT = [sb(f"qT{i}", [P, SEQ]) for i in range(2)]
        kT = [sb(f"kT{i}", [P, SEQ]) for i in range(2)]
        qz = [sb(f"qz{i}", [P, H, SEQ]) for i in range(2)]
        Vz = [sb(f"Vz{i}", [P, TPS, H * SPREAD]) for i in range(2)]
        nmax = [sb(f"nmax{i}", [P, TPS]) for i in range(RING)]
        den = [sb(f"den{i}", [P, TPS]) for i in range(RING)]
        prob = [sb(f"prob{i}", [P, TPS, SEQ]) for i in range(RING)]
        probT = [sb(f"probT{i}", [P, TPS, SEQ]) for i in range(RING)]
        oT = sb("oT", [P, SEQ])
        ps_x, ps_q = ps("ps_x"), ps("ps_q")
        ps_o = [ps(f"ps_o{i}", SEQ) for i in range(2)]
        ps_s = [ps(f"ps_s{i}") for i in range(2)]
        ps_t = [ps(f"ps_t{i}") for i in range(2)]
        loaded, masks, zeroed = sem("loaded"), sem("masks"), sem("zeroed")
        normed, turned, xt_ready, xtr_ready = sem("normed"), sem("turned"), sem("xt_ready"), sem("xtr_ready")
        qkv_made, q_ready, k_ready, qz_ready, v_ready = (sem(s) for s in ("qkv_made", "q_ready", "k_ready", "qz_ready", "v_ready"))
        scored, biased, maxed, nmax_ready, exp_done = (sem(s) for s in ("scored", "biased", "maxed", "nmax_ready", "exp_done"))
        inverted, prob_ready, prob_turned, probT_ready, pv_done = (
            sem(s) for s in ("inverted", "prob_ready", "prob_turned", "probT_ready", "pv_done"))
        oT_ready, out_made, out_added, x_ready = (sem(s) for s in ("oT_ready", "out_made", "out_added", "x_ready"))
        LOADS = 16 * 10

        def sequences(eng, turn, start, tail):
            start()
            turn(0, 0, True, False)
            turn(1, 1, False, False)
            with eng.Fori(0, SEQS // 2 - 2) as pair:
                turn(2 * pair + 2, 0, False, False)
                turn(2 * pair + 3, 1, False, False)
            turn(SEQS - 2, 0, False, False)
            turn(SEQS - 1, 1, False, True)
            tail()

        with nc.Block() as block:
            @block.sync
            def _(sp):
                for i, w in enumerate((w_q, w_k, w_v, w_o)):
                    sp.dma_start(W[:, i, :], w).then_inc(loaded, 16)
                for dst, src in ((bq, b_q), (bk, b_k)):
                    sp.dma_start(dst[:, :], src.rearrange("(c a) -> c a", a=1)).then_inc(loaded, 16)
                for dst, src in ((bv, b_v), (bo, b_o)):
                    sp.dma_start(dst[:, :], src.rearrange("(a c) -> a c", a=1).to_broadcast([P, P])).then_inc(loaded, 16)
                sp.dma_start(near[:, :, :], bass.AP(tensor=table.tensor, offset=0, ap=[[1, P], [SPAN, H], [1, SEQ]])
                             ).then_inc(loaded, 16)
                with nc.allow_non_contiguous_dma(reason="small"):
                    sp.dma_start(far[:, :], bass.AP(tensor=table.tensor, offset=SPAN - 1, ap=[[0, P], [SPAN, H]])
                                 ).then_inc(loaded, 16)

            @block.gpsimd
            def _(pool):
                for v in Vz:
                    nc.gpsimd.memset(v[:, :, :], 0.0).then_inc(zeroed, 1)

            @block.vector
            def _(dve):
                def norm(b):
                    need(dve, turned, b)
                    for t in range(TPS):
                        at = bass.ds(b * TPS + t, 1)
                        nc.vector.tensor_scalar(xn[:, t, :], X[:, at, :].rearrange("p a c -> p (a c)"),
                                                mean[:, at], rstd[:, at], ALU.subtract, ALU.mult).then_inc(normed, 1)

                def reverse(b):
                    dve.wait_ge(xt_ready, b + 1)
                    need(dve, qkv_made, b)
                    nc.vector.tensor_copy(xTr[:, :], xT[:, ::-1]).then_inc(xtr_ready, 1)

                def values(b, s, t):
                    dve.wait_ge(qkv_made, b + 1)
                    if isinstance(b, int) and b < 2:
                        dve.wait_ge(zeroed, 2)
                    need(dve, pv_done, H * (b - 1))
                    nc.vector.tensor_tensor(
                        Vz[s][:, t, :].rearrange("p (h k) -> p h k", h=H)[:, :, 0:D],
                        ps_x[:, SEQ + t * P:SEQ + t * P + P].rearrange("p (h d) -> p h d", h=H),
                        bv[:, :].rearrange("p (h d) -> p h d", h=H), ALU.add).then_inc(v_ready, 1)

                def queries(b, s, heads):
                    dve.wait_ge(q_ready, b + 1)
                    need(dve, scored, H * (b - 1))
                    for h in heads:
                        nc.vector.tensor_scalar(qz[s][:, h, :], qT[s][:, :], hmask[:, h:h + 1], SCALE,
                                                ALU.mult, ALU.mult).then_inc(qz_ready, 1)

                def shift(b, h):
                    n, i, r = H * b + h, h % 2, h % RING
                    dve.wait_ge(scored, n + 1)
                    nc.vector.tensor_tensor(ps_s[i][:, 0:SEQ], ps_s[i][:, 0:SEQ], near[:, h, :], ALU.add).then_inc(biased, 1)
                    dve.wait_ge(biased, n + 1)
                    need(dve, exp_done, n + 1 - RING)
                    nc.vector.tensor_reduce(nmax[r][:, :], ps_s[i][:, :].rearrange("p (t k) -> p t k", t=TPS), AX_X,
                                            ALU.max, negate=True).then_inc(maxed, 1)
                    dve.wait_ge(maxed, n + 1)
                    nc.vector.scalar_tensor_tensor(out=nmax[r][:, 1:2], in0=nmax[r][:, 1:2], scalar=far[:, h:h + 1],
                                                   in1=far[:, h:h + 1], op0=ALU.subtract, op1=ALU.add).then_inc(nmax_ready, 1)

                def scale(b, h):
                    n, r = H * b + h, h % RING
                    dve.wait_ge(exp_done, n + 1)
                    nc.vector.reciprocal(den[r][:, :], den[r][:, :]).then_inc(inverted, 1)
                    dve.wait_ge(inverted, n + 1)
                    for t in range(TPS):
                        ins = nc.vector.tensor_scalar(prob[r][:, t, :], prob[r][:, t, :], den[r][:, t:t + 1], None, ALU.mult)
                    ins.then_inc(prob_ready, 1)

                def add_out(b):
                    dve.wait_ge(out_made, b + 1)
                    rows = X[:, bass.ds(b * TPS, TPS), :]
                    nc.vector.tensor_tensor(rows, rows, ps_x[:, 0:SEQ].rearrange("p (t c) -> p t c", t=TPS),
                                            ALU.add).then_inc(out_added, 1)
                    dve.wait_ge(out_added, b + 1)
                    nc.vector.tensor_tensor(rows, rows, bo[:, :].unsqueeze(1).to_broadcast([P, TPS, P]),
                                            ALU.add).then_inc(x_ready, 1)

                def start():
                    nc.vector.tensor_reduce(hmask[:, :], ident[:, :].rearrange("p (h d) -> p h d", h=H), AX_X,
                                            ALU.add).then_inc(masks, 1)
                    dve.wait_ge(masks, 1)
                    dve.wait_ge(loaded, LOADS)
                    norm(0)
                    reverse(0)
                    for t in range(TPS):
                        values(0, 0, t)
                    queries(0, 0, range(AHEAD))

                def turn(b, s, first, last):
                    for h in range(H):
                        shift(b, h)
                        if h < H - AHEAD:
                            queries(b, s, (h + AHEAD,))
                        elif not last:
                            queries(b + 1, 1 - s, (h + AHEAD - H,))
                        if h:
                            scale(b, h - 1)
                        elif not first:
                            scale(b - 1, H - 1)
                        if h == 5 and not first:
                            add_out(b - 1)
                        if not last:
                            if h == 2:
                                norm(b + 1)
                            if h == 7:
                                reverse(b + 1)
                            if h in (8, 9):
                                values(b + 1, 1 - s, h - 8)

                def tail():
                    scale(SEQS - 1, H - 1)
                    add_out(SEQS - 1)
                    dve.wait_ge(x_ready, SEQS)

                sequences(dve, turn, start, tail)

            @block.scalar
            def _(act):
                def channels(b):
                    act.wait_ge(turned, b + 1)
                    need(act, qkv_made, b)
                    need(act, xtr_ready, b)
                    nc.scalar.copy(xT[:, :], ps_x[:, 0:SEQ]).then_inc(xt_ready, 1)

                def keys(b, s):
                    act.wait_ge(qkv_made, b + 1)
                    need(act, qz_ready, H * (b - 1))
                    nc.scalar.activation(qT[s][:, :], ps_q[:, 0:SEQ], ACT.Identity, bias=bq[:, :]).then_inc(q_ready, 1)
                    need(act, scored, H * (b - 1))
                    nc.scalar.activation(kT[s][:, :], ps_q[:, SEQ:2 * SEQ], ACT.Identity, bias=bk[:, :]).then_inc(k_ready, 1)

                def expo(b, h):
                    n, i, r = H * b + h, h % 2, h % RING
                    act.wait_ge(nmax_ready, n + 1)
                    need(act, prob_turned, n + 1 - RING)
                    for t in range(TPS):
                        ins = nc.scalar.activation(prob[r][:, t, :], ps_s[i][:, t * SEQ:t * SEQ + SEQ], ACT.Exp,
                                                   bias=nmax[r][:, t:t + 1], accum_out=den[r][:, t:t + 1])
                    ins.then_inc(exp_done, 1)

                def evacuate(b, h):
                    n, i, r = H * b + h, h % 2, h % RING
                    act.wait_ge(prob_turned, n + 1)
                    need(act, pv_done, n + 1 - RING)
                    nc.scalar.copy(probT[r][:, :, :], ps_t[i][:, :].rearrange("p (k q) -> p k q", k=TPS)).then_inc(probT_ready, 1)

                def outputs(b, s):
                    act.wait_ge(pv_done, H * b + H)
                    need(act, out_made, b)
                    nc.scalar.copy(oT[:, :], ps_o[s][:, :]).then_inc(oT_ready, 1)

                def start():
                    act.wait_ge(loaded, LOADS)
                    channels(0)
                    keys(0, 0)

                def turn(b, s, first, last):
                    for h in range(H):
                        if h >= TURN:
                            evacuate(b, h - TURN)
                        elif not first:
                            evacuate(b - 1, H - TURN + h)
                        expo(b, h)
                        if h == WEIGH and not first:
                            outputs(b - 1, 1 - s)
                        if not last:
                            if h == 6:
                                channels(b + 1)
                            if h == 8:
                                keys(b + 1, 1 - s)

                def tail():
                    for h in range(H - TURN, H):
                        evacuate(SEQS - 1, h)
                    outputs(SEQS - 1, 1)

                sequences(act, turn, start, tail)

            @block.tensor
            def _(pe):
                def transpose_x(b):
                    pe.wait_ge(normed, TPS * b + TPS)
                    need(pe, xt_ready, b)
                    need(pe, out_added, b - 1)
                    for t in range(TPS):
                        ins = nc.tensor.transpose(ps_x[:, t * P:t * P + P], xn[:, t, :], ident[:, :])
                    ins.then_inc(turned, 1)

                def project(b):
                    pe.wait_ge(xt_ready, b + 1)
                    pe.wait_ge(xtr_ready, b + 1)
                    need(pe, k_ready, b)
                    nc.tensor.matmul(ps_q[:, 0:SEQ], W[:, 0, :], xT[:, :], start=True, stop=True)
                    nc.tensor.matmul(ps_q[:, SEQ:2 * SEQ], W[:, 1, :], xTr[:, :], start=True, stop=True)
                    for t in range(TPS):
                        ins = nc.tensor.matmul(ps_x[:, SEQ + t * P:SEQ + t * P + P], xTr[:, t * P:t * P + P], W[:, 2, :],
                                               start=True, stop=True)
                    ins.then_inc(qkv_made, 1)

                def score(b, s, h):
                    n, i = H * b + h, h % 2
                    pe.wait_ge(qz_ready, n + 1)
                    if h == 0:
                        pe.wait_ge(k_ready, b + 1)
                    need(pe, exp_done, n - 1)
                    for t in range(TPS):
                        ins = nc.tensor.matmul(ps_s[i][:, t * SEQ:t * SEQ + SEQ], qz[s][:, h, t * P:t * P + P], kT[s][:, :],
                                               start=True, stop=True)
                    ins.then_inc(scored, 1)

                def turn_probs(b, h):
                    n, i, r = H * b + h, h % 2, h % RING
                    pe.wait_ge(prob_ready, n + 1)
                    need(pe, probT_ready, n - 1)
                    for k in range(TPS):
                        for t in range(TPS):
                            ins = nc.tensor.transpose(ps_t[i][:, k * SEQ + t * P:k * SEQ + t * P + P],
                                                      prob[r][:, t, k * P:k * P + P], ident[:, :])
                    ins.then_inc(prob_turned, 1)

                def weigh(b, s, h):
                    n, r = H * b + h, h % RING
                    pe.wait_ge(probT_ready, n + 1)
                    if h == 0:
                        pe.wait_ge(v_ready, TPS * b + TPS)
                        need(pe, oT_ready, b - 1)
                    for k in range(TPS):
                        ins = nc.tensor.matmul(ps_o[s][:, :], Vz[s][:, k, h * P:h * P + P], probT[r][:, k, :],
                                               start=(h == 0 and k == 0), stop=(h == H - 1 and k == TPS - 1))
                    ins.then_inc(pv_done, 1)

                def out_proj(b, known):
                    pe.wait_ge(oT_ready, b + 1)
                    pe.wait_ge(v_ready, TPS * known)
                    for t in range(TPS):
                        ins = nc.tensor.matmul(ps_x[:, t * P:t * P + P], oT[:, t * P:t * P + P], W[:, 3, :],
                                               start=True, stop=True)
                    ins.then_inc(out_made, 1)

                def start():
                    pe.wait_ge(loaded, LOADS)
                    transpose_x(0)
                    project(0)

                def turn(b, s, first, last):
                    for h in range(H):
                        score(b, s, h)
                        if h >= TURN:
                            turn_probs(b, h - TURN)
                        elif not first:
                            turn_probs(b - 1, H - TURN + h)
                        if h >= WEIGH:
                            weigh(b, s, h - WEIGH)
                        elif not first:
                            weigh(b - 1, 1 - s, H - WEIGH + h)
                        if h == 4 and not first:
                            out_proj(b - 1, b + 1)
                        if not last:
                            if h == 5:
                                transpose_x(b + 1)
                            if h == 7:
                                project(b + 1)

                def tail():
                    for x in range(WEIGH):
                        if x < TURN:
                            turn_probs(SEQS - 1, H - TURN + x)
                        weigh(SEQS - 1, 1, H - WEIGH + x)
                    out_proj(SEQS - 1, SEQS)

                sequences(pe, turn, start, tail)
        sem.clear()


def local_layers(nc, X, ident, w_qkv, q_scale, k_scale, w_o, ln_g, ln_b, w_1, b_1, w_2, b_2, rotary, masks):
    LAYERS, H, D, WIN = 6, 16, 64, 32
    INNER = H * D
    FF = w_2.shape[1]
    ITEMS = LAYERS * SEQS
    PAIRS = H // 2
    CH = 512
    HC = CH // D
    GH, HG = 4, H // 4
    K1 = P + WIN
    FK = [P, P, FF - 2 * P]
    with ExitStack() as ctx:
        def sb(name, shape, dt=F32):
            return ctx.enter_context(nc.sbuf_tensor("l_" + name, shape, dt))

        def ps(name, cols=512):
            return ctx.enter_context(nc.psum_tensor("l_" + name, [P, cols], F32))

        sem = Semaphores(nc, "l_")

        Wqkv = sb("Wqkv", [P, 3 * INNER])
        Wo = sb("Wo", [P, 2, PAIRS, P])
        W1 = sb("W1", [P, 2, 2 * FF])
        W2 = sb("W2", [P, 2, 3, P])
        b1 = sb("b1", [P, 2, 2 * FF])
        b2 = sb("b2", [P, 2, P])
        gain, offset = sb("gain", [P, LAYERS]), sb("offset", [P, LAYERS])
        own = [sb(f"own{x}", [P, LAYERS, TPS, D]) for x in "qk"]
        cross = [sb(f"cross{x}", [P, LAYERS, TPS, D]) for x in "qk"]
        mask0, mask1 = sb("mask0", [P, P], BF16), sb("mask1", [P, K1], BF16)
        identb = sb("identb", [P, P], BF16)
        xs, sT = sb("xs", [P, TPS, P]), sb("sT", [P, SEQ])
        sq = [sb(f"sq{i}", [P, CH]) for i in range(2)]
        t1 = [sb(f"t1_{i}", [P, CH]) for i in range(2)]
        t2 = [sb(f"t2_{i}", [P, CH]) for i in range(2)]
        n2, clampd, rn = sb("n2", [P, TPS, 2 * H]), sb("clampd", [P, TPS, 2 * H]), sb("rn", [P, TPS, 2 * H])
        half = sb("half", [P, 2 * H])
        qk = sb("qk", [P, 4, CH])
        qz = [sb(f"qz{i}", [P, PAIRS, 2, SEQ]) for i in range(2)]
        kT = [sb(f"kT{i}", [P, PAIRS, SEQ]) for i in range(2)]
        V = [sb(f"V{i}", [P, TPS, INNER]) for i in range(2)]
        sc8 = [sb(f"sc8_{i}", [P, TPS, H]) for i in range(2)]
        nmax = [sb(f"nmax{i}", [P, TPS, HG]) for i in range(2)]
        nbias = [sb(f"nbias{i}", [P, TPS, HG]) for i in range(2)]
        den = [sb(f"den{i}", [P, TPS, HG]) for i in range(2)]
        P0 = [sb(f"P0_{i}", [P, HG, P]) for i in range(2)]
        P1 = [sb(f"P1_{i}", [P, HG, K1]) for i in range(2)]
        PT0 = [sb(f"PT0_{i}", [P, HG, K1]) for i in range(2)]
        PT1 = [sb(f"PT1_{i}", [P, HG, P]) for i in range(2)]
        oT = sb("oT", [P, PAIRS, SEQ])
        xf, stats, mv = sb("xf", [P, TPS, P]), sb("stats", [P, TPS, 6]), sb("mv", [P, TPS, 2])
        var, rstd = sb("var", [P, TPS]), sb("rstd", [P, TPS])
        xn, xnT = sb("xn", [P, TPS, P]), sb("xnT", [P, SEQ])
        gate, gated, lin = sb("gate", [P, FF]), sb("gated", [P, FF]), sb("lin", [P, FF])
        hid = sb("hid", [P, TPS, FF])
        hT = sb("hT", [P, TPS, 3, P])
        ps_w = [ps(f"ps_w{i}") for i in range(2)]
        ps_t, ps_p, ps_o = ps("ps_t"), ps("ps_p"), ps("ps_o")
        ps_s0, ps_s1, ps_s2 = ps("ps_s0"), ps("ps_s1"), ps("ps_s2")

        names = ("setup consts zeroed scales_in qscales wqkv_in later_in shifted turned sT_ready qkv_made sq_done rot_done n2_made clamped "
                 "powed roped scaled qk_turned qkT_ready sc_ready v_ready scored maxed nm_ready exp_done inverted "
                 "norm_done bt_done pt_turned pt_ready pv_done ot_ready wo_made x_attn shifted2 bn_done var_ready "
                 "rstd_ready xn_ready ft_made xnT_ready fw_made gate_ready gelu_done lin_ready h_ready ht_made "
                 "hT_ready w2_made ffn_part x_ffn aggr_done small_done").split()
        S = {n: sem(n) for n in names}
        (setup, consts, zeroed, scales_in, qscales, wqkv_in, later_in, shifted, turned, sT_ready, qkv_made, sq_done, rot_done, n2_made,
         clamped, powed, roped, scaled, qk_turned, qkT_ready, sc_ready, v_ready, scored, maxed, nm_ready, exp_done,
         inverted, norm_done, bt_done, pt_turned, pt_ready, pv_done, ot_ready, wo_made, x_attn, shifted2, bn_done,
         var_ready, rstd_ready, xn_ready, ft_made, xnT_ready, fw_made, gate_ready, gelu_done, lin_ready, h_ready,
         ht_made, hT_ready, w2_made, ffn_part, x_ffn, aggr_done, small_done) = (S[n] for n in names)
        sp_alone, dve_alone = sem("sp_alone"), sem("dve_alone")
        LATER = 16 * 6
        SHIFT = 16 * 3
        MISC = 16 * 10

        with ExitStack() as inner:
            base = inner.enter_context(nc.sbuf_tensor("l_base", [P, TPS, 4, D], F32))
            scale = inner.enter_context(nc.sbuf_tensor("l_scale", [P, 2, LAYERS, D], F32))
            maskf = inner.enter_context(nc.sbuf_tensor("l_maskf", [P, P + K1], F32))
            with nc.Block() as block:
                @block.sync
                def _(sp):
                    n = 0
                    for dst, src in (
                            (base[:, :, :, :], rotary.rearrange("(t p) k e -> p t k e", p=P)),
                            (scale[:, 0, :, :], q_scale.rearrange("(a l) e -> a l e", a=1).to_broadcast([P, LAYERS, D])),
                            (scale[:, 1, :, :], k_scale.rearrange("(a l) e -> a l e", a=1).to_broadcast([P, LAYERS, D])),
                            (maskf[:, :], masks)):
                        sp.dma_start(dst, src).then_inc(setup, 16)
                        n += 1
                    with nc.allow_non_contiguous_dma(reason="small"):
                        sp.dma_start(gain[:, :], ln_g.rearrange("l c -> c l")).then_inc(setup, 16)
                        sp.dma_start(offset[:, :], ln_b.rearrange("l c -> c l")).then_inc(setup, 16)
                    sp.wait_ge(setup, 16 * (n + 2))

                @block.vector
                def _(dve):
                    dve.wait_ge(setup, 16 * 6)
                    for x in range(2):
                        for t in range(TPS):
                            fac = lambda k: base[:, t, 2 * x + k, :].unsqueeze(1).to_broadcast([P, LAYERS, D])
                            nc.vector.tensor_tensor(own[x][:, :, t, :], scale[:, x, :, :], fac(0), ALU.mult).then_inc(qscales, 1)
                            for hf in range(2):
                                lo, hi = slice(hf * D // 2, (hf + 1) * D // 2), slice((1 - hf) * D // 2, (2 - hf) * D // 2)
                                nc.vector.tensor_tensor(cross[x][:, :, t, lo], scale[:, x, :, hi], fac(1)[:, :, lo],
                                                        ALU.mult).then_inc(qscales, 1)
                    nc.vector.tensor_copy(mask0[:, :], maskf[:, 0:P]).then_inc(qscales, 1)
                    nc.vector.tensor_copy(mask1[:, :], maskf[:, P:]).then_inc(qscales, 1)
                    nc.vector.tensor_copy(identb[:, :], ident[:, :]).then_inc(qscales, 1)
                    nc.vector.memset(xs[0:1, 0, D:], 0.0).then_inc(qscales, 1)
                    nc.vector.memset(xf[0:1, 0, D:], 0.0).then_inc(qscales, 1)
                    dve.wait_ge(qscales, 6 * TPS + 5)

                @block.gpsimd
                def _(pool):
                    nc.gpsimd.memset(half[:, :], -0.5).then_inc(zeroed, 1)
                    for i in range(2):
                        nc.gpsimd.memset(qz[i][:, :, :, :], 0.0).then_inc(zeroed, 1)
                        nc.gpsimd.memset(PT0[i][:, :, :], 0.0).then_inc(zeroed, 1)
                    pool.wait_ge(zeroed, 5)

        def items(eng, turn):
            turn(0, 0, True, False, False)
            turn(1, 1, True, True, False)
            turn(2, 0, True, True, True)
            with eng.Fori(0, ITEMS // 2 - 2) as pair:
                turn(2 * pair + 3, 1, True, True, True)
                turn(2 * pair + 4, 0, True, True, True)
            turn(ITEMS - 1, 1, True, True, True, last=True)
            turn(ITEMS, 0, False, True, True)
            turn(ITEMS + 1, 1, False, False, True)

        with nc.Block() as block:
            @block.sync
            def _(sp):
                def load_qkv(l):
                    need(sp, qkv_made, 12 * SEQS * l)
                    sp.dma_start(Wqkv[:, :], w_qkv[bass.ds(l, 1), :, :].rearrange("a c n -> c (a n)")).then_inc(wqkv_in, 16)

                def load_later(l):
                    need(sp, x_ffn, SEQS * (l - 1))
                    sp.sem_inc(sp_alone, 1)
                    h = bass.ds(l % 2, 1)
                    at = bass.ds(l, 1)
                    sp.dma_start(Wo[:, h, :, :].rearrange("p a j n -> p (a j) n"),
                                 w_o[at, :, :].rearrange("a (j p) n -> p (a j) n", p=P)).then_inc(later_in, 16)
                    sp.dma_start(W1[:, h, :].rearrange("p a n -> p (a n)"),
                                 w_1[at, :, :].rearrange("a c n -> c (a n)")).then_inc(later_in, 16)
                    sp.dma_start(W2[:, h, 0:2, :].rearrange("p a k n -> p (a k) n"),
                                 w_2[at, 0:2 * P, :].rearrange("a (k p) n -> p (a k) n", p=P)).then_inc(later_in, 16)
                    sp.dma_start(W2[0:FK[2], h, 2, :].rearrange("p a n -> p (a n)"),
                                 w_2[at, 2 * P:FF, :].rearrange("a p n -> p (a n)")).then_inc(later_in, 16)
                    sp.dma_start(b1[:, h, :].rearrange("p a n -> p (a n)"),
                                 b_1[at, :].to_broadcast([P, 2 * FF])).then_inc(later_in, 16)
                    sp.dma_start(b2[:, h, :].rearrange("p a n -> p (a n)"),
                                 b_2[at, :].to_broadcast([P, P])).then_inc(later_in, 16)

                def shift(dst, b, done):
                    t = bass.ds(b * TPS, TPS)
                    sp.dma_start(dst[:, :, 0:D], X[:, t, 0:D]).then_inc(done, 16)
                    sp.dma_start(dst[1:P, :, D:], X[0:P - 1, t, D:]).then_inc(done, 16)
                    sp.dma_start(dst[0:1, 1, D:], X[P - 1:P, bass.ds(b * TPS, 1), D:].rearrange("p a c -> p (a c)")
                                 ).then_inc(done, 16)

                def item(i, b, ahead, first=False, layer=None):
                    if not first:
                        sp.wait_ge(x_ffn, i - SEQS + 1)
                        sp.sem_inc(sp_alone, 1)
                    need(sp, turned, i)
                    shift(xs, b, shifted)
                    if layer is not None:
                        load_qkv(layer)
                    if ahead:
                        later(i - 2, (b + SEQS - 2) % SEQS)

                def later(f, b):
                    sp.wait_ge(x_attn, f + 1)
                    sp.sem_inc(sp_alone, 1)
                    need(sp, xn_ready, f)
                    shift(xf, b, shifted2)

                load_qkv(0)
                load_later(0)
                item(0, 0, False, True)
                item(1, 1, False, True)
                item(2, 2, True, True)
                item(3, 3, True, True)
                load_later(1)
                with sp.Fori(4, SEQS) as b:
                    item(b, b, True, True)
                with sp.Fori(1, LAYERS - 1) as l:
                    item(l * SEQS, 0, True, layer=l)
                    with sp.Fori(1, 4) as b:
                        item(l * SEQS + b, b, True)
                    load_later(l + 1)
                    with sp.Fori(4, SEQS) as b:
                        item(l * SEQS + b, b, True)
                item((LAYERS - 1) * SEQS, 0, True, layer=LAYERS - 1)
                with sp.Fori(1, SEQS) as b:
                    item((LAYERS - 1) * SEQS + b, b, True)
                later(ITEMS - 2, SEQS - 2)
                later(ITEMS - 1, SEQS - 1)

            @block.tensor
            def _(pe):
                def turn_x(i):
                    pe.wait_ge(shifted, SHIFT * (i + 1))
                    need(pe, qkT_ready, 8 * i)
                    for t in range(TPS):
                        ins = nc.tensor.transpose(ps_t[:, t * P:t * P + P], xs[:, t, :], ident[:, :])
                    ins.then_inc(turned, 1)

                def turn(i, s, p1, p2, p3, last=False):
                    a, f, o = i - 1, i - 2, 1 - s
                    layer = i // SEQS
                    half_o, half_f = bass.ds((a // SEQS) % 2, 1), bass.ds((f // SEQS) % 2, 1)

                    def scores(g, t):
                        if not p2:
                            return
                        u = TPS * (GH * a + g) + t
                        if g == 0 and t == 0:
                            pe.wait_ge(qkT_ready, 8 * a + 8)
                        need(pe, exp_done, u - 1)
                        for ps_, m, heads, width in (((ps_s0, mask0, range(HG), P),) if t == 0 else
                                                     ((ps_s1, mask1, (0, 1), K1), (ps_s2, mask1, (2, 3), K1))):
                            k = len(heads)
                            nc.tensor.matmul(ps_[:, 0:k * width], identb[:, :], m[:, :].unsqueeze(1).to_broadcast([P, k, width]),
                                             start=True, stop=False)
                            for x, h in enumerate(heads):
                                pair, odd = divmod(HG * g + h, 2)
                                ins = nc.tensor.matmul(ps_[:, x * width:x * width + width],
                                                       qz[o][:, pair, odd, t * P:t * P + P],
                                                       kT[o][:, pair, t * (P - WIN):t * (P - WIN) + width],
                                                       start=False, stop=(x == k - 1))
                        ins.then_inc(scored, 1)

                    def turn_probs(g, t):
                        if not p2:
                            return
                        u = TPS * (GH * a + g) + t
                        pe.wait_ge(norm_done, u + 1)
                        need(pe, pt_ready, u)
                        for h in range(HG):
                            src = P1[g % 2][:, h, WIN:K1] if t else P0[g % 2][:, h, :]
                            ins = nc.tensor.transpose(ps_p[:, h * P:h * P + P], src, ident[:, :])
                        ins.then_inc(pt_turned, 1)

                    def weigh(g):
                        if not p2:
                            return
                        n = GH * a + g
                        pe.wait_ge(pt_ready, 2 * n + 2)
                        pe.wait_ge(bt_done, n + 1)
                        if g == 0:
                            pe.wait_ge(v_ready, 4 * a + 4)
                            need(pe, x_attn, a)
                        need(pe, ot_ready, n)
                        if g == 1 and p3:
                            pe.wait_ge(ffn_part, f + 1)
                        for h in range(HG):
                            head = HG * g + h
                            rows, c0 = slice(D * (h % 2), D * (h % 2) + D), (h // 2) * SEQ
                            nc.tensor.matmul(ps_o[rows, c0:c0 + K1], V[o][:, 0, head * D:head * D + D], PT0[g % 2][:, h, :],
                                             start=True, stop=False, skip_group_check=True)
                            ins = nc.tensor.matmul(ps_o[rows, c0 + P:c0 + SEQ], V[o][:, 1, head * D:head * D + D],
                                                   PT1[g % 2][:, h, :], start=False, stop=True, skip_group_check=True)
                        ins.then_inc(pv_done, 1)

                    def out_proj():
                        if not p2:
                            return
                        pe.wait_ge(ot_ready, GH * a + GH)
                        for t in range(TPS):
                            for j in range(PAIRS):
                                ins = nc.tensor.matmul(ps_o[:, t * P:t * P + P], oT[:, j, t * P:t * P + P],
                                                       Wo[:, half_o, j, :].rearrange("p a n -> p (a n)"),
                                                       start=(j == 0), stop=(j == PAIRS - 1))
                        ins.then_inc(wo_made, 1)

                    def project(j):
                        if not p1:
                            return
                        t, c = divmod(j, 6)
                        if j == 0:
                            pe.wait_ge(sT_ready, i + 1)
                            pe.wait_ge(wqkv_in, 16 * (layer + 1))
                        if j < 2:
                            need(pe, v_ready, 4 * i - 1 + j)
                        elif j in (2, 3):
                            pe.wait_ge(rot_done, 8 * i + j - 1)
                        elif j == 4:
                            pe.wait_ge(gate_ready, 2 * f + 2) if p3 else pe.wait_ge(rot_done, 8 * i + 3)
                        elif j == 5:
                            pe.wait_ge(lin_ready, 2 * f + 2) if p3 else pe.wait_ge(rot_done, 8 * i + 4)
                        elif j in (6, 7):
                            pe.wait_ge(v_ready, 4 * i + j - 5)
                        else:
                            pe.wait_ge(rot_done, 8 * i + j - 3)
                        nc.tensor.matmul(ps_w[j % 2][:, :], sT[:, t * P:t * P + P], Wqkv[:, c * CH:c * CH + CH],
                                         start=True, stop=True).then_inc(qkv_made, 1)

                    def turn_qk(j):
                        if not p1:
                            return
                        t, c = divmod(j, 6)
                        m = 8 * i + 4 * t + c
                        if c < 2:
                            pe.wait_ge(roped, m + 1)
                        else:
                            pe.wait_ge(scaled, 2 * (2 * i + t) + c - 1)
                        if j == 0:
                            pe.wait_ge(xnT_ready, f + 1) if p3 else pe.wait_ge(sT_ready, i + 1)
                        elif j == 2 and p3:
                            pe.wait_ge(hT_ready, 2 * f + 2)
                        else:
                            pe.wait_ge(qkT_ready, m)
                        for x in range(4):
                            ins = nc.tensor.transpose(ps_t[:, x * P:x * P + P], qk[:, c, x * P:x * P + P], ident[:, :])
                        ins.then_inc(qk_turned, 1)

                    def turn_normed():
                        if not p3:
                            return
                        pe.wait_ge(xn_ready, f + 1)
                        if p1:
                            pe.wait_ge(sT_ready, i + 1)
                        else:
                            pe.wait_ge(qkT_ready, 8 * ITEMS)
                            need(pe, hT_ready, 2 * f)
                        for t in range(TPS):
                            ins = nc.tensor.transpose(ps_t[:, t * P:t * P + P], xn[:, t, :], ident[:, :])
                        ins.then_inc(ft_made, 1)

                    def hidden(t, k):
                        if not p3:
                            return
                        if t == 0 and k == 0:
                            pe.wait_ge(xnT_ready, f + 1)
                            pe.wait_ge(later_in, LATER * (f // SEQS + 1))
                        if t == 0 and p1:
                            pe.wait_ge(rot_done, 8 * i + 3 + k)
                        elif t == 0:
                            pe.wait_ge(v_ready, 4 * ITEMS)
                        need(pe, lin_ready if k else gate_ready, 2 * f + t)
                        c0 = FF * (1 - k)
                        nc.tensor.matmul(ps_w[k][:, 0:FF], xnT[:, t * P:t * P + P],
                                         W1[:, half_f, c0:c0 + FF].rearrange("p a n -> p (a n)"),
                                         start=True, stop=True).then_inc(fw_made, 1)

                    def turn_hidden(t):
                        if not p3:
                            return
                        pe.wait_ge(h_ready, 2 * f + t + 1)
                        if t:
                            pe.wait_ge(hT_ready, 2 * f + 1)
                        elif p1:
                            pe.wait_ge(qkT_ready, 8 * i + 2)
                        else:
                            pe.wait_ge(xnT_ready, f + 1)
                        for k, rows in enumerate(FK):
                            ins = nc.tensor.transpose(ps_t[0:rows, k * P:k * P + P], hid[:, t, k * P:k * P + rows], ident[:, :])
                        ins.then_inc(ht_made, 1)

                    def ff_out():
                        if not p3:
                            return
                        pe.wait_ge(hT_ready, 2 * f + 2)
                        if p2:
                            pe.wait_ge(ot_ready, GH * a + 1)
                        else:
                            pe.wait_ge(x_attn, ITEMS)
                        for t in range(TPS):
                            for k, rows in enumerate(FK):
                                ins = nc.tensor.matmul(ps_o[:, t * P:t * P + P], hT[0:rows, t, k, :],
                                                       W2[0:rows, half_f, k, :].rearrange("p a n -> p (a n)"),
                                                       start=(k == 0), stop=(k == 2))
                        ins.then_inc(w2_made, 1)

                    scores(0, 0)
                    project(0)
                    scores(0, 1)
                    project(1)
                    project(2)
                    scores(1, 0)
                    project(3)
                    scores(1, 1)
                    turn_probs(0, 0)
                    turn_normed()
                    scores(2, 0)
                    turn_qk(0)
                    hidden(0, 0)
                    hidden(0, 1)
                    scores(2, 1)
                    hidden(1, 0)
                    turn_probs(0, 1)
                    turn_qk(1)
                    scores(3, 0)
                    hidden(1, 1)
                    project(4)
                    turn_hidden(0)
                    project(5)
                    project(6)
                    turn_probs(1, 0)
                    project(7)
                    weigh(0)
                    turn_probs(1, 1)
                    turn_hidden(1)
                    scores(3, 1)
                    project(8)
                    turn_qk(2)
                    turn_probs(2, 0)
                    ff_out()
                    project(9)
                    turn_qk(3)
                    turn_probs(2, 1)
                    weigh(1)
                    turn_qk(6)
                    turn_probs(3, 0)
                    weigh(2)
                    turn_probs(3, 1)
                    turn_qk(7)
                    project(10)
                    weigh(3)
                    turn_qk(8)
                    if p2:
                        pe.wait_ge(later_in, LATER * (a // SEQS + 1))
                    out_proj()
                    turn_qk(9)
                    project(11)
                    if p1 and not last:
                        turn_x(i + 1)

                turn_x(0)
                items(pe, turn)

            @block.scalar
            def _(act):
                def channels(i):
                    act.wait_ge(turned, i + 1)
                    need(act, qkv_made, 12 * i)
                    nc.scalar.copy(sT[:, :], ps_t[:, 0:SEQ]).then_inc(sT_ready, 1)

                def turn(i, s, p1, p2, p3, last=False):
                    a, f, o = i - 1, i - 2, 1 - s

                    def expo(g, t):
                        if not p2:
                            return
                        n, k = GH * a + g, g % 2
                        u = TPS * n + t
                        act.wait_ge(nm_ready, u + 1)
                        need(act, pt_turned, u - 3)
                        if t:
                            need(act, bt_done, n - 1)
                        for h in range(HG):
                            if t == 0:
                                src, dst = ps_s0[:, h * P:h * P + P], P0[k][:, h, :]
                            else:
                                x = (h % 2) * K1
                                src, dst = (ps_s2 if h >= 2 else ps_s1)[:, x:x + K1], P1[k][:, h, :]
                            ins = nc.scalar.activation(dst, src, ACT.Exp, bias=nbias[k][:, t, h:h + 1],
                                                       scale=sc8[o][:, t, HG * g + h:HG * g + h + 1],
                                                       accum_out=den[k][:, t, h:h + 1])
                        ins.then_inc(exp_done, 1)

                    def outputs(g):
                        if not p2:
                            return
                        n = GH * a + g
                        act.wait_ge(pv_done, n + 1)
                        if g == 0:
                            need(act, wo_made, a)
                        nc.scalar.copy(oT[:, 2 * g:2 * g + 2, :], ps_o[:, :].rearrange("p (j q) -> p j q", j=2)).then_inc(ot_ready, 1)

                    def squares(j):
                        if not p1:
                            return
                        t, c = divmod(j, 6)
                        m = 8 * i + 4 * t + c
                        act.wait_ge(qkv_made, 12 * i + j + 1)
                        need(act, n2_made, m - 1)
                        nc.scalar.activation(sq[c % 2][:, :], ps_w[j % 2][:, :], ACT.Square).then_inc(sq_done, 1)

                    def values(j):
                        if not p1:
                            return
                        t, c = divmod(j, 6)
                        act.wait_ge(qkv_made, 12 * i + j + 1)
                        need(act, pv_done, GH * (i - 1))
                        nc.scalar.copy(V[s][:, t, (c - 4) * CH:(c - 3) * CH], ps_w[j % 2][:, :]).then_inc(v_ready, 1)

                    def keep_qk(j):
                        if not p1:
                            return
                        t, c = divmod(j, 6)
                        m = 8 * i + 4 * t + c
                        act.wait_ge(qk_turned, m + 1)
                        if c == 0:
                            need(act, scored, TPS * GH * (i - 1))
                        src = ps_t[:, :].rearrange("p (j q) -> p j q", j=4)
                        pairs, cols = slice(4 * (c % 2), 4 * (c % 2) + 4), slice(t * P, t * P + P)
                        if c < 2:
                            nc.scalar.copy(qz[s][0:D, pairs, 0, cols], src[0:D])
                            ins = nc.scalar.copy(qz[s][D:P, pairs, 1, cols], src[D:P])
                        else:
                            ins = nc.scalar.copy(kT[s][:, pairs, cols], src)
                        ins.then_inc(qkT_ready, 1)

                    def ff_input():
                        if not p3:
                            return
                        act.wait_ge(ft_made, f + 1)
                        need(act, fw_made, 4 * f)
                        l = bass.ds(f // SEQS, 1)
                        nc.scalar.activation(xnT[:, :], ps_t[:, 0:SEQ], ACT.Identity, bias=offset[:, l], scale=gain[:, l]
                                             ).then_inc(xnT_ready, 1)

                    def gelu(t):
                        if not p3:
                            return
                        act.wait_ge(gate_ready, 2 * f + t + 1)
                        need(act, h_ready, 2 * f + t)
                        nc.scalar.activation(gated[:, :], gate[:, :], ACT.Gelu).then_inc(gelu_done, 1)

                    squares(0)
                    expo(0, 0)
                    squares(1)
                    squares(2)
                    expo(0, 1)
                    squares(3)
                    expo(1, 0)
                    ff_input()
                    expo(1, 1)
                    keep_qk(0)
                    expo(2, 0)
                    gelu(0)
                    keep_qk(1)
                    gelu(1)
                    values(4)
                    values(5)
                    squares(6)
                    expo(2, 1)
                    outputs(0)
                    squares(7)
                    expo(3, 0)
                    keep_qk(2)
                    squares(8)
                    expo(3, 1)
                    squares(9)
                    keep_qk(3)
                    outputs(1)
                    keep_qk(6)
                    outputs(2)
                    values(10)
                    keep_qk(7)
                    outputs(3)
                    keep_qk(8)
                    keep_qk(9)
                    if p1 and not last:
                        channels(i + 1)
                    values(11)

                channels(0)
                items(act, turn)

            @block.vector
            def _(dve):
                def turn(i, s, p1, p2, p3, last=False):
                    a, f, o = i - 1, i - 2, 1 - s
                    layer = bass.ds(min(i // SEQS, LAYERS - 1) if isinstance(i, int) else i // SEQS, 1)

                    def maxima(g, t):
                        if not p2:
                            return
                        n, k = GH * a + g, g % 2
                        u = TPS * n + t
                        dve.wait_ge(scored, u + 1)
                        if t == 0:
                            ins = nc.vector.tensor_reduce(nmax[k][:, 0, :], ps_s0[:, :].rearrange("p (h k) -> p h k", h=HG),
                                                          AX_X, ALU.max, negate=True)
                        else:
                            for x, src in ((0, ps_s1), (2, ps_s2)):
                                ins = nc.vector.tensor_reduce(nmax[k][:, 1, x:x + 2],
                                                              src[:, 0:2 * K1].rearrange("p (h k) -> p h k", h=2),
                                                              AX_X, ALU.max, negate=True)
                        ins.then_inc(maxed, 1)

                    def shift_of(g, t):
                        if not p2:
                            return
                        k = g % 2
                        u = TPS * (GH * a + g) + t
                        dve.wait_ge(maxed, u + 1)
                        need(dve, exp_done, u - 3)
                        if g == 0:
                            dve.wait_ge(sc_ready, 2 * a + t + 1)
                        nc.vector.tensor_tensor(nbias[k][:, t, :], nmax[k][:, t, :], sc8[o][:, t, HG * g:HG * g + HG],
                                                ALU.mult).then_inc(nm_ready, 1)

                    def invert(g, t):
                        if not p2:
                            return
                        k = g % 2
                        u = TPS * (GH * a + g) + t
                        dve.wait_ge(exp_done, u + 1)
                        nc.vector.reciprocal(den[k][:, t, :], den[k][:, t, :]).then_inc(inverted, 1)

                    def normalise(g, t):
                        if not p2:
                            return
                        k = g % 2
                        u = TPS * (GH * a + g) + t
                        dve.wait_ge(inverted, u + 1)
                        probs, width = (P1[k], K1) if t else (P0[k], P)
                        nc.vector.tensor_tensor(probs[:, :, :], probs[:, :, :],
                                                den[k][:, t, :].unsqueeze(2).to_broadcast([P, HG, width]), ALU.mult
                                                ).then_inc(norm_done, 1)

                    def turn_back(g):
                        if not p2:
                            return
                        n, k = GH * a + g, g % 2
                        dve.wait_ge(norm_done, TPS * n + 2)
                        need(dve, pv_done, n - 1)
                        nc.vector.transpose(PT0[k][P - WIN:P, :, P:K1], P1[k][0:WIN, :, 0:WIN]).then_inc(bt_done, 1)

                    def keep_probs(g, t):
                        if not p2:
                            return
                        n, k = GH * a + g, g % 2
                        dve.wait_ge(pt_turned, TPS * n + t + 1)
                        need(dve, pv_done, n - 1)
                        dst = PT1[k][:, :, :] if t else PT0[k][:, :, 0:P]
                        nc.vector.tensor_copy(dst, ps_p[:, :].rearrange("p (h q) -> p h q", h=HG)).then_inc(pt_ready, 1)

                    def add_attention():
                        if not p2:
                            return
                        dve.wait_ge(wo_made, a + 1)
                        rows = X[:, bass.ds((a % SEQS) * TPS, TPS), :]
                        nc.vector.tensor_tensor(rows, rows, ps_o[:, 0:SEQ].rearrange("p (t c) -> p t c", t=TPS),
                                                ALU.add).then_inc(x_attn, 1)

                    def rotate(j):
                        if not p1:
                            return
                        t, c = divmod(j, 6)
                        m, x = 8 * i + 4 * t + c, c // 2
                        k = c % 2
                        dve.wait_ge(sq_done, m + 1)
                        need(dve, roped, m - 1)
                        src = ps_w[j % 2][:, :].rearrange("p (h a e) -> p h a e", h=HC, a=2)
                        table = lambda v: v[x][:, layer, t, :].to_broadcast([P, HC, D])
                        nc.vector.tensor_tensor(t1[k][:, :].rearrange("p (h e) -> p h e", h=HC),
                                                ps_w[j % 2][:, :].rearrange("p (h e) -> p h e", h=HC), table(own), ALU.mult)
                        nc.vector.tensor_tensor(t2[k][:, :].rearrange("p (h a e) -> p h a e", h=HC, a=2), src[:, :, ::-1, :],
                                                table(cross).rearrange("p h (a e) -> p h a e", a=2), ALU.mult
                                                ).then_inc(rot_done, 1)

                    def sum_squares(j):
                        if not p1:
                            return
                        t, c = divmod(j, 6)
                        m = 8 * i + 4 * t + c
                        dve.wait_ge(sq_done, m + 1)
                        if c % 2 == 0:
                            need(dve, clamped, 2 * (2 * i + t) + c // 2 - 3)
                        nc.vector.tensor_reduce(n2[:, t, HC * c:HC * c + HC],
                                                sq[c % 2][:, :].rearrange("p (h e) -> p h e", h=HC),
                                                AX_X, ALU.add).then_inc(n2_made, 1)

                    def clamp(t, x):
                        if not p1:
                            return
                        n, heads = 2 * i + t, slice(H * x, H * x + H)
                        dve.wait_ge(n2_made, 8 * i + 4 * t + 2 * x + 2)
                        need(dve, powed, 2 * n + x - 3)
                        nc.vector.tensor_scalar(clampd[:, t, heads], n2[:, t, heads], 1e-24, None, ALU.max).then_inc(clamped, 1)

                    def q_factor(t):
                        if not p1:
                            return
                        dve.wait_ge(powed, 2 * (2 * i + t) + 1)
                        need(dve, exp_done, TPS * GH * (i - 1))
                        nc.vector.tensor_scalar(sc8[s][:, t, :], rn[:, t, 0:H], 8.0, None, ALU.mult).then_inc(sc_ready, 1)

                    def ff_stats():
                        if not p3:
                            return
                        dve.wait_ge(shifted2, SHIFT * (f + 1))
                        for t in range(TPS):
                            nc.vector.bn_stats(stats[:, t, :], xf[:, t, :]).then_inc(bn_done, 1)
                        dve.wait_ge(bn_done, TPS * (f + 1))
                        dve.sem_inc(dve_alone, 1)
                        for t in range(TPS):
                            nc.vector.bn_aggr(mv[:, t, :], stats[:, t, :]).then_inc(aggr_done, 1)
                        dve.wait_ge(aggr_done, TPS * (f + 1))
                        nc.vector.tensor_scalar(var[:, :], mv[:, :, 1], EPS, None, ALU.add).then_inc(var_ready, 1)

                    def ff_norm():
                        if not p3:
                            return
                        dve.wait_ge(rstd_ready, f + 1)
                        need(dve, ft_made, f)
                        for t in range(TPS):
                            ins = nc.vector.tensor_scalar(xn[:, t, :], xf[:, t, :], mv[:, t, 0:1], rstd[:, t:t + 1],
                                                          ALU.subtract, ALU.mult)
                        ins.then_inc(xn_ready, 1)

                    def bias_1(t, k):
                        if not p3:
                            return
                        n, hf = 2 * f + t, bass.ds((f // SEQS) % 2, 1)
                        if t == 0 and k == 0:
                            dve.wait_ge(later_in, LATER * (f // SEQS + 1))
                        dve.wait_ge(fw_made, 2 * n + k + 1)
                        bias = lambda c0: b1[:, hf, c0:c0 + FF].rearrange("p a n -> p (a n)")
                        if k == 0:
                            need(dve, gelu_done, n)
                            nc.vector.tensor_tensor(gate[:, :], ps_w[0][:, 0:FF], bias(FF), ALU.add).then_inc(gate_ready, 1)
                        else:
                            need(dve, h_ready, n)
                            nc.vector.tensor_tensor(lin[:, :], ps_w[1][:, 0:FF], bias(0), ALU.add).then_inc(lin_ready, 1)

                    def multiply(t):
                        if not p3:
                            return
                        n = 2 * f + t
                        dve.wait_ge(gelu_done, n + 1)
                        dve.wait_ge(lin_ready, n + 1)
                        need(dve, ht_made, n - 1)
                        nc.vector.tensor_tensor(hid[:, t, :], lin[:, :], gated[:, :], ALU.mult).then_inc(h_ready, 1)

                    def keep_hidden(t):
                        if not p3:
                            return
                        n = 2 * f + t
                        dve.wait_ge(ht_made, n + 1)
                        need(dve, w2_made, f)
                        nc.vector.tensor_copy(hT[:, t, 0:2, :], ps_t[:, 0:2 * P].rearrange("p (k q) -> p k q", k=2))
                        nc.vector.tensor_copy(hT[0:FK[2], t, 2, :], ps_t[0:FK[2], 2 * P:3 * P]).then_inc(hT_ready, 1)

                    def add_ff():
                        if not p3:
                            return
                        dve.wait_ge(w2_made, f + 1)
                        rows = X[:, bass.ds((f % SEQS) * TPS, TPS), :]
                        nc.vector.tensor_tensor(rows, rows, ps_o[:, 0:SEQ].rearrange("p (t c) -> p t c", t=TPS),
                                                ALU.add).then_inc(ffn_part, 1)
                        dve.wait_ge(ffn_part, f + 1)
                        nc.vector.tensor_tensor(rows, rows, b2[:, bass.ds((f // SEQS) % 2, 1), :].to_broadcast([P, TPS, P]),
                                                ALU.add).then_inc(x_ffn, 1)

                    maxima(0, 0)
                    shift_of(0, 0)
                    ff_stats()
                    rotate(0)
                    maxima(0, 1)
                    ff_norm()
                    sum_squares(0)
                    shift_of(0, 1)
                    rotate(1)
                    maxima(1, 0)
                    invert(0, 0)
                    sum_squares(1)
                    shift_of(1, 0)
                    normalise(0, 0)
                    rotate(2)
                    maxima(1, 1)
                    invert(0, 1)
                    invert(1, 0)
                    clamp(0, 0)
                    shift_of(1, 1)
                    rotate(3)
                    maxima(2, 0)
                    keep_probs(0, 0)
                    shift_of(2, 0)
                    bias_1(0, 0)
                    normalise(0, 1)
                    sum_squares(2)
                    invert(1, 1)
                    maxima(2, 1)
                    turn_back(0)
                    sum_squares(3)
                    bias_1(0, 1)
                    bias_1(1, 0)
                    invert(2, 0)
                    multiply(0)
                    keep_probs(0, 1)
                    bias_1(1, 1)
                    clamp(0, 1)
                    shift_of(2, 1)
                    maxima(3, 0)
                    normalise(1, 0)
                    normalise(1, 1)
                    normalise(2, 0)
                    keep_hidden(0)
                    keep_probs(1, 0)
                    shift_of(3, 0)
                    sum_squares(6)
                    multiply(1)
                    rotate(6)
                    keep_probs(1, 1)
                    invert(2, 1)
                    keep_hidden(1)
                    turn_back(1)
                    maxima(3, 1)
                    rotate(7)
                    shift_of(3, 1)
                    keep_probs(2, 0)
                    normalise(2, 1)
                    invert(3, 0)
                    add_ff()
                    sum_squares(7)
                    turn_back(2)
                    clamp(1, 0)
                    keep_probs(2, 1)
                    normalise(3, 0)
                    sum_squares(8)
                    invert(3, 1)
                    sum_squares(9)
                    keep_probs(3, 0)
                    clamp(1, 1)
                    normalise(3, 1)
                    rotate(8)
                    turn_back(3)
                    keep_probs(3, 1)
                    q_factor(0)
                    q_factor(1)
                    rotate(9)
                    add_attention()

                items(dve, turn)
                dve.wait_ge(x_ffn, ITEMS)

            @block.gpsimd
            def _(pool):
                def turn(i, s, p1, p2, p3, last=False):
                    f = i - 2

                    def add(j):
                        if not p1:
                            return
                        t, c = divmod(j, 6)
                        m, k = 8 * i + 4 * t + c, c % 2
                        pool.wait_ge(rot_done, m + 1)
                        need(pool, qk_turned, m - 3)
                        nc.gpsimd.tensor_tensor(qk[:, c, :], t1[k][:, :], t2[k][:, :], ALU.add).then_inc(roped, 1)

                    def norms(t, x):
                        if not p1:
                            return
                        n, heads = 2 * i + t, slice(H * x, H * x + H)
                        pool.wait_ge(clamped, 2 * n + x + 1)
                        if x == 0:
                            need(pool, sc_ready, n - 1)
                        else:
                            need(pool, scaled, 2 * n - 2)
                        nc.gpsimd.tensor_tensor(rn[:, t, heads], clampd[:, t, heads], half[:, heads], ALU.pow).then_inc(powed, 1)

                    def scale_k(j):
                        if not p1:
                            return
                        t, c = divmod(j, 6)
                        pool.wait_ge(powed, 2 * (2 * i + t) + 2)
                        pool.wait_ge(roped, 8 * i + 4 * t + c + 1)
                        v = qk[:, c, :].rearrange("p (h e) -> p h e", h=HC)
                        nc.gpsimd.tensor_tensor(v, v, rn[:, t, HC * c:HC * c + HC].unsqueeze(2).to_broadcast([P, HC, D]),
                                                ALU.mult).then_inc(scaled, 1)

                    def ff_rstd():
                        if not p3:
                            return
                        pool.wait_ge(var_ready, f + 1)
                        need(pool, xn_ready, f)
                        nc.gpsimd.tensor_tensor(rstd[:, :], var[:, :], half[:, 0:TPS], ALU.pow).then_inc(rstd_ready, 1)

                    ff_rstd()
                    add(0)
                    add(1)
                    norms(0, 0)
                    add(2)
                    add(3)
                    norms(0, 1)
                    scale_k(2)
                    add(6)
                    scale_k(3)
                    add(7)
                    norms(1, 0)
                    norms(1, 1)
                    add(8)
                    scale_k(8)
                    add(9)
                    scale_k(9)

                items(pool, turn)
        sem.clear()


def normalise_all(nc, X, store):
    with ExitStack() as ctx:
        mean = ctx.enter_context(nc.sbuf_tensor("n_mean", [P, TILES], F32))
        rstd = ctx.enter_context(nc.sbuf_tensor("n_rstd", [P, TILES], F32))
        stored = ctx.enter_context(nc.semaphore("n_stored"))
        normed = ctx.enter_context(nc.semaphore("n_normed"))
        layernorm_stats(nc, X, mean, rstd, "n")
        with nc.Block() as block:
            @block.sync
            def _(sp):
                sp.dma_start(store, X[:, :, :]).then_inc(stored, 16)

            @block.vector
            def _(dve):
                dve.wait_ge(stored, 16)
                with dve.Fori(0, TILES) as t:
                    row = X[:, bass.ds(t, 1), :].rearrange("p a c -> p (a c)")
                    nc.vector.tensor_scalar(row, row, mean[:, bass.ds(t, 1)], rstd[:, bass.ds(t, 1)],
                                            ALU.subtract, ALU.mult).then_inc(normed, 1)
                dve.wait_ge(normed, TILES)


def add_and_store(nc, X, store, out):
    PARTS = 4
    N = TILES // PARTS
    with ExitStack() as ctx:
        held = ctx.enter_context(nc.sbuf_tensor("f_held", [P, TILES, P], F32))
        back = [ctx.enter_context(nc.semaphore(f"f_back{i}")) for i in range(PARTS)]
        added = ctx.enter_context(nc.semaphore("f_added"))
        written = ctx.enter_context(nc.semaphore("f_written"))
        with nc.Block() as block:
            @block.sync
            def _(sp):
                for i in range(PARTS):
                    at = slice(i * N, i * N + N)
                    sp.dma_start(held[:, at, :], store[:, at, :]).then_inc(back[i], 16)
                for i in range(PARTS):
                    at = slice(i * N, i * N + N)
                    sp.wait_ge(added, i + 1)
                    sp.dma_start(out[:, at, :], X[:, at, :]).then_inc(written, 16)
                sp.wait_ge(written, 16 * PARTS)

            @block.vector
            def _(dve):
                for i in range(PARTS):
                    at = slice(i * N, i * N + N)
                    dve.wait_ge(back[i], 16)
                    nc.vector.tensor_tensor(X[:, at, :], X[:, at, :], held[:, at, :], ALU.add).then_inc(added, 1)


def mamba_moe_attention_local(nc, a):
    tiles = lambda v: v.rearrange("s (t p) c -> p (s t) c", p=P)
    with ExitStack() as ctx:
        X = ctx.enter_context(nc.sbuf_tensor("X", [P, TILES, P], F32))
        store = nc.dram_tensor("store", [P, TILES, P], F32).ap()
        x_in = ctx.enter_context(nc.semaphore("x_in"))
        ident = identity(nc, ctx)
        with nc.Block() as block:
            @block.sync
            def _(sp):
                sp.dma_start(X[:, :, :], tiles(a["x"])).then_inc(x_in, 16)
                sp.wait_ge(x_in, 16)
        selective_scan(nc, X, ident, a["in_w"], a["conv_w"], a["conv_b"], a["xp_w"], a["dt_w"], a["dt_b"],
                       a["a_log"], a["d_skip"], a["out_w"])
        expert_layer(nc, X, ident, a["gate_w"], a["e_w1"], a["e_b1"], a["e_w2"], a["e_b2"])
        full_attention(nc, X, ident, a["w_q"], a["b_q"], a["w_k"], a["b_k"], a["w_v"], a["b_v"], a["w_o"], a["b_o"],
                       a["table"])
        normalise_all(nc, X, store)
        local_layers(nc, X, ident, a["w_qkv"], a["q_scale"], a["k_scale"], a["l_wo"], a["ln_g"], a["ln_b"],
                     a["l_w1"], a["l_b1"], a["l_w2"], a["l_b2"], a["rotary"], a["masks"])
        add_and_store(nc, X, store, tiles(a["out"]))


def _rotary():
    import numpy as np
    dim, window, f = 64, 32, np.float32
    half = np.arange(0, dim, 2, dtype=f)
    inv_freq = (f(1.0) / f(10000.0) ** (half / f(dim))).astype(f)
    t = np.arange(SEQ, dtype=f)
    freqs = t[:, None] * inv_freq[None, :]
    freqs = np.concatenate([freqs, freqs], -1)
    base = (half + f(0.4 * dim)) / f(1.4 * dim)
    scale = base[None, :] ** ((t - SEQ // 2) / f(window // 2))[:, None]
    scale = np.concatenate([scale, scale], -1)
    sign = np.concatenate([-np.ones(dim // 2, f), np.ones(dim // 2, f)])
    cos, sin = np.cos(freqs), np.sin(freqs) * sign
    return np.stack([cos * scale, sin * scale, cos / scale, sin / scale], 1).astype(f)


def _masks():
    import numpy as np
    window, out = 32, []
    for tile, keys in ((0, np.arange(P)), (1, np.arange(P - window, 2 * P))):
        q, k = np.arange(P)[:, None] + P * tile, keys[None, :]
        sees = (k <= q) & (k >= q - window) & (k // window >= q // window - 1)
        out.append(np.where(sees, 0.0, -1e30))
    return np.concatenate(out, 1).astype(np.float32)


def kernel(**inputs):
    import numpy as _np
    import concourse.bacc as _bacc
    from concourse import mybir as _mybir
    from concourse.bass_utils import run_bass_kernel_spmd as _run

    given = {k: _np.asarray(v) for k, v in inputs.items()}
    turned = lambda name, *order: given[name].transpose(order)
    table = given["L1_attn_rel_table"]
    far = _np.broadcast_to(table[-1:], (2 * SEQ - 1 - table.shape[0], table.shape[1]))
    data = {
        "x": given["L0_attn_x"],
        "in_w": turned("L0_attn_in_proj_w", 0, 2, 1), "conv_w": given["L0_attn_conv_w"],
        "conv_b": given["L0_attn_conv_b"], "xp_w": turned("L0_attn_x_proj_w", 0, 2, 1),
        "dt_w": turned("L0_attn_dt_proj_w", 0, 2, 1), "dt_b": given["L0_attn_dt_proj_b"],
        "a_log": given["L0_attn_A_log"], "d_skip": given["L0_attn_D"], "out_w": turned("L0_attn_out_proj_w", 0, 2, 1),
        "gate_w": turned("L0_ffn_gate_w", 1, 0), "e_w1": turned("L0_ffn_w1", 0, 2, 1),
        "e_b1": turned("L0_ffn_b1", 1, 0), "e_w2": turned("L0_ffn_w2", 0, 2, 1), "e_b2": given["L0_ffn_b2"],
        "w_q": given["L1_attn_Wq"], "b_q": given["L1_attn_bq"], "w_k": given["L1_attn_Wk"], "b_k": given["L1_attn_bk"],
        "w_v": given["L1_attn_Wv"], "b_v": given["L1_attn_bv"], "w_o": given["L1_attn_Wo"], "b_o": given["L1_attn_bo"],
        "table": _np.concatenate([table, far], 0).T,
        "w_qkv": given["L1_ffn_Wqkv"], "q_scale": given["L1_ffn_q_scale"], "k_scale": given["L1_ffn_k_scale"],
        "l_wo": given["L1_ffn_Wo"], "ln_g": given["L1_ffn_ln_g"], "ln_b": given["L1_ffn_ln_b"],
        "l_w1": given["L1_ffn_W1"], "l_b1": given["L1_ffn_b1"], "l_w2": given["L1_ffn_W2"], "l_b2": given["L1_ffn_b2"],
        "rotary": _rotary(), "masks": _masks(),
    }
    nc = _bacc.Bacc("TRN2", target_bir_lowering=False, num_devices=1)
    arrays, tensors = {}, {}
    for name, v in data.items():
        v = _np.ascontiguousarray(v)
        arrays[f"in_{name}_dram"] = v
        tensors[name] = nc.dram_tensor(f"in_{name}_dram", v.shape, _mybir.dt.from_np(v.dtype), kind="ExternalInput").ap()
    tensors["out"] = nc.dram_tensor("out_0_dram", (SEQS, SEQ, P), F32, kind="ExternalOutput").ap()
    mamba_moe_attention_local(nc, tensors)
    r = _run(nc, [arrays], core_ids=[0])
    return r.results[0]["out_0_dram"]
```

```python
import concourse.bass as bass
from concourse import mybir
from contextlib import ExitStack

F32 = mybir.dt.float32
BF16 = mybir.dt.bfloat16
ALU = mybir.AluOpType
ACT = mybir.ActivationFunctionType
AX_X = mybir.AxisListType.X

P = 128
SEQS = 16
SEQ = 256
TILES = SEQS * SEQ // P
TPS = SEQ // P
EPS = 1e-5


def need(eng, sem, value):
    if isinstance(value, int) and value <= 0:
        return
    eng.wait_ge(sem, value)


class Steps:
    pass


class Semaphores:

    def __init__(self, nc, prefix):
        self.nc, self.prefix, self.all = nc, prefix, []

    def __call__(self, name):
        self.all.append(self.nc.alloc_semaphore(self.prefix + name))
        return self.all[-1]

    def clear(self):
        self.nc.clear_and_free_semaphores(self.all)
        self.nc.all_engine_barrier()


class Chain:

    def __init__(self, eng, sem):
        self.eng, self.sem, self.base, self.k, self.i, self.per = eng, sem, 0, 0, 0, 0

    def turn(self, i, per):
        if self.k and self.per == 0:
            self.base += self.k
        if self.per:
            assert self.k == self.per, (self.k, self.per)
        self.i, self.per, self.k = i, per, 0

    def end(self, turns):
        if self.per:
            assert self.k == self.per, (self.k, self.per)
        self.base += turns * self.per
        self.i, self.per, self.k = 0, 0, 0

    def now(self):
        return self.base + self.i * self.per + self.k

    def step(self, ins):
        ins.then_inc(self.sem, 1)
        self.k += 1

    def wait(self):
        self.eng.wait_ge(self.sem, self.now())

    def link(self, ins):
        self.step(ins)
        self.wait()


def identity(nc, ctx, name="ident"):
    ident = ctx.enter_context(nc.sbuf_tensor(name, [P, P], F32))
    zeroed = ctx.enter_context(nc.semaphore(name + "_zeroed"))
    with nc.Block() as block:
        @block.gpsimd
        def _(pool):
            nc.gpsimd.memset(ident[:, :], 0.0).then_inc(zeroed, 1)
            pool.wait_ge(zeroed, 1)
            nc.gpsimd.affine_select(out=ident[:, :], in_=ident[:, :], compare_op=ALU.not_equal, fill=1.0,
                                    base=0, pattern=[[-1, P]], channel_multiplier=1).then_inc(zeroed, 1)
            pool.wait_ge(zeroed, 2)
    return ident


def layernorm_stats(nc, X, mean, rstd, tag, beside=None):
    with ExitStack() as ctx:
        def sb(name, shape):
            return ctx.enter_context(nc.sbuf_tensor(f"{name}_{tag}", shape, F32))

        stats = sb("stats", [P, TILES, 6])
        spread = sb("spread", [P, TILES])
        var = sb("var", [P, TILES])
        half = sb("half", [P, TILES])
        sem = Semaphores(nc, tag + "_")
        stats_done, ln_steps, var_ready, half_set = sem("stats_done"), sem("ln_steps"), sem("var_ready"), sem("half_set")
        with nc.Block() as block:
            @block.vector
            def _(dve):
                with dve.Fori(0, TILES // 8) as t:
                    for k in range(8):
                        at = bass.ds(8 * t + k, 1)
                        nc.vector.bn_stats(stats[:, at, :], X[:, at, :]).then_inc(stats_done, 1)
                dve.wait_ge(stats_done, TILES)
                c = Chain(dve, ln_steps)
                me, qe, mo, qo = (stats[:, :, k] for k in (1, 2, 4, 5))
                nc.vector.tensor_tensor(mean[:, :], me, mo, ALU.add).then_inc(ln_steps, 1)
                nc.vector.tensor_tensor(spread[:, :], me, mo, ALU.subtract).then_inc(ln_steps, 1)
                nc.vector.tensor_tensor(var[:, :], qe, qo, ALU.add).then_inc(ln_steps, 1)
                c.k = 3
                c.wait()
                c.step(nc.vector.tensor_scalar(mean[:, :], mean[:, :], 0.5, None, ALU.mult))
                c.step(nc.vector.tensor_tensor(spread[:, :], spread[:, :], spread[:, :], ALU.mult))
                c.link(nc.vector.tensor_scalar(var[:, :], var[:, :], 1.0 / P, EPS, ALU.mult, ALU.add))
                c.wait()
                nc.vector.scalar_tensor_tensor(out=var[:, :], in0=spread[:, :], scalar=0.25, in1=var[:, :],
                                               op0=ALU.mult, op1=ALU.add).then_inc(var_ready, 1)
                dve.wait_ge(var_ready, 1)

            @block.gpsimd
            def _(pool):
                nc.gpsimd.memset(half[:, :], -0.5).then_inc(half_set, 1)
                if beside:
                    beside[1](pool)
                pool.wait_ge(half_set, 1)
                pool.wait_ge(var_ready, 1)
                nc.gpsimd.tensor_tensor(rstd[:, :], var[:, :], half[:, :], ALU.pow).then_inc(half_set, 1)
                pool.wait_ge(half_set, 2)

            if beside:
                block.sync(beside[0])
        sem.clear()


def selective_scan(nc, X, ident, in_w, conv_w, conv_b, xp_w, dt_w, dt_b, a_log, d_skip, out_w):
    H, DH, DI, N, K, R = 8, 16, 32, 16, 4, 8
    G, HG = 2, 4
    TOK = SEQS * SEQ
    NC_ = 4
    CHUNKS = N // NC_
    W = NC_ * SEQ
    with ExitStack() as ctx:
        def sb(name, shape):
            return ctx.enter_context(nc.sbuf_tensor("m_" + name, shape, F32))

        sem = Semaphores(nc, "m_")

        mean, rstd = sb("mean", [P, TILES]), sb("rstd", [P, TILES])
        Wu = sb("Wu", [P, G, P])
        Wz = sb("Wz", [P, G, P])
        xpw = sb("xpw", [P, G, R + 2 * N])
        Wdx = sb("Wdx", [P, G, HG * R])
        WBC = sb("WBC", [P, G, 2 * N, P])
        Wdt = sb("Wdt", [R * HG, G, P])
        Wo = sb("Wo", [P, G, HG * DH])
        convw, convb, dtb, dsk = sb("convw", [P, G, K]), sb("convb", [P, G]), sb("dtb", [P, G]), sb("dsk", [P, G])
        A = sb("A", [P, G, N])
        UC = sb("UC", [P, G, TOK])
        ZS = sb("ZS", [P, G, TOK])
        DELTA = sb("DELTA", [P, G, TOK])
        zeroed, loaded, a_ready = sem("zeroed"), sem("loaded"), sem("a_ready")
        a_ready_n, placed = sem("a_negated"), sem("placed")
        LOADS = 16 * (6 + 4 * H)

        def zero(pool):
            for w in (Wu[:, :, :], Wz[:, :, :], Wdt[:, :, :], Wo[:, :, :], Wdx[:, :, :], WBC[:, :, :, :]):
                nc.gpsimd.memset(w, 0.0).then_inc(zeroed, 1)

        def load(sp):
            n = 0
            for dst, src in ((convw[:, :, :], conv_w.rearrange("(g h) d k -> (h d) g k", g=G)),
                             (A[:, :, :], a_log.rearrange("(g h) d n -> (h d) g n", g=G)),
                             (xpw[:, :, :], xp_w.rearrange("(g h) d e -> (h d) g e", g=G))):
                sp.dma_start(dst, src).then_inc(loaded, 16)
                n += 1
            for dst, src in ((convb, conv_b), (dtb, dt_b), (dsk, d_skip)):
                with nc.allow_non_contiguous_dma(reason="small"):
                    sp.dma_start(dst[:, :], src.rearrange("(g h) d -> (h d) g", g=G)).then_inc(loaded, 16)
                n += 1
            sp.wait_ge(zeroed, 4)
            for h in range(H):
                g, hh = divmod(h, HG)
                rows, cols = slice(DH * h, DH * h + DH), slice(DI * hh, DI * hh + DI)
                for dst, src in ((Wu[rows, g, cols], in_w[h, :, 0:DI]), (Wz[rows, g, cols], in_w[h, :, DI:2 * DI]),
                                 (Wdt[R * hh:R * hh + R, g, cols], dt_w[h]),
                                 (Wo[cols, g, DH * hh:DH * hh + DH], out_w[h])):
                    with nc.allow_non_contiguous_dma(reason="small"):
                        sp.dma_start(dst, src).then_inc(loaded, 16)
                    n += 1
            assert 16 * n == LOADS
        layernorm_stats(nc, X, mean, rstd, "m", (load, zero))
        with nc.Block() as block:
            @block.vector
            def _(dve):
                dve.wait_ge(zeroed, 6)
                dve.wait_ge(loaded, LOADS)
                for h in range(H):
                    g, hh = divmod(h, HG)
                    rows = slice(DI * hh, DI * hh + DI)
                    nc.vector.tensor_copy(Wdx[rows, g, R * hh:R * hh + R], xpw[rows, g, 0:R]).then_inc(placed, 1)
                    nc.vector.tensor_copy(WBC[rows, g, :, rows], xpw[rows, g, R:].unsqueeze(2).to_broadcast(
                        [DI, 2 * N, DI])).then_inc(placed, 1)
                dve.wait_ge(placed, 2 * H)
                dve.wait_ge(a_ready, 1)
                nc.vector.tensor_scalar(A[:, :, :], A[:, :, :], -1.0, None, ALU.mult).then_inc(a_ready_n, 1)
                dve.wait_ge(a_ready_n, 1)

            @block.sync
            def _(sp):
                sp.wait_ge(loaded, LOADS)

            @block.scalar
            def _(act):
                act.wait_ge(loaded, LOADS)
                nc.scalar.activation(A[:, :, :], A[:, :, :], ACT.Exp).then_inc(a_ready, 1)

        with ExitStack() as inner:
            def isb(name, shape):
                return inner.enter_context(nc.sbuf_tensor("m1_" + name, shape, F32))

            def ips(name, cols):
                return inner.enter_context(nc.psum_tensor("m1_" + name, [P, cols], F32))

            xn = isb("xn", [P, TPS, P])
            xnT = isb("xnT", [P, SEQ])
            up = [isb(f"up{i}", [P, G, K - 1 + SEQ]) for i in range(2)]
            cv = [isb(f"cv{i}", [P, G, SEQ]) for i in range(2)]
            dts = isb("dts", [R * HG, G, SEQ])
            ps_x, ps_u, ps_z = ips("ps_x", 2 * SEQ), ips("ps_u", G * SEQ), ips("ps_z", G * SEQ)
            ps_d, ps_e = ips("ps_d", G * SEQ), ips("ps_e", G * SEQ)
            normed, turned, xnt_ready = sem("normed"), sem("turned"), sem("xnt_ready")
            projected, u_ready, z_used, conv_steps = sem("projected"), sem("u_ready"), sem("z_used"), sem("conv_steps")
            conv_ready, uc_ready, dt_made, dt_ready = sem("conv_ready"), sem("uc_ready"), sem("dt_made"), sem("dt_ready")
            raw_made, raw_ready, pads = sem("raw_made"), sem("raw_ready"), sem("pads")

            def sequences(eng, turn):
                turn(0, 0, True, False)
                turn(1, 1, False, False)
                with eng.Fori(0, SEQS // 2 - 2) as pair:
                    turn(2 * pair + 2, 0, False, False)
                    turn(2 * pair + 3, 1, False, False)
                turn(SEQS - 2, 0, False, False)
                turn(SEQS - 1, 1, False, True)

            with nc.Block() as block:
                @block.vector
                def _(dve):
                    for u in up:
                        nc.vector.memset(u[:, :, 0:K - 1], 0.0).then_inc(pads, 1)
                    dve.wait_ge(pads, 2)

                    def norm(b):
                        need(dve, turned, b)
                        for t in range(TPS):
                            at = bass.ds(b * TPS + t, 1)
                            nc.vector.tensor_scalar(xn[:, t, :], X[:, at, :].rearrange("p a c -> p (a c)"),
                                                    mean[:, at], rstd[:, at],
                                                    ALU.subtract, ALU.mult).then_inc(normed, 1)

                    def convolve(b, s):
                        dve.wait_ge(u_ready, b + 1)
                        need(dve, uc_ready, b - 1)
                        for k in reversed(range(K)):
                            for g in range(G):
                                tap = up[s][:, g, k:k + SEQ]
                                if k == K - 1:
                                    ins = nc.vector.tensor_scalar(cv[s][:, g, :], tap, convw[:, g, k:k + 1],
                                                                  convb[:, g:g + 1], ALU.mult, ALU.add)
                                else:
                                    ins = nc.vector.scalar_tensor_tensor(out=cv[s][:, g, :], in0=tap,
                                                                         scalar=convw[:, g, k:k + 1],
                                                                         in1=cv[s][:, g, :], op0=ALU.mult, op1=ALU.add)
                            if k:
                                ins.then_inc(conv_steps, 1)
                                dve.wait_ge(conv_steps, (K - 1) * b + K - k)
                            else:
                                ins.then_inc(conv_ready, 1)

                    def turn(b, s, first, last):
                        if not last:
                            norm(b + 1)
                        convolve(b, s)

                    norm(0)
                    sequences(dve, turn)

                @block.tensor
                def _(pe):
                    def transpose_x(b):
                        pe.wait_ge(normed, TPS * b + TPS)
                        need(pe, xnt_ready, b)
                        for t in range(TPS):
                            ins = nc.tensor.transpose(ps_x[:, t * P:t * P + P], xn[:, t, :], ident[:, :])
                        ins.then_inc(turned, 1)

                    def project(b):
                        pe.wait_ge(xnt_ready, b + 1)
                        need(pe, u_ready, b)
                        need(pe, z_used, b)
                        for dst, w in ((ps_u, Wu), (ps_z, Wz)):
                            for g in range(G):
                                ins = nc.tensor.matmul(dst[:, g * SEQ:g * SEQ + SEQ], w[:, g, :], xnT[:, :],
                                                       start=True, stop=True)
                        ins.then_inc(projected, 1)

                    def make_dt(b):
                        pe.wait_ge(uc_ready, b + 1)
                        need(pe, dt_ready, b)
                        for g in range(G):
                            ins = nc.tensor.matmul(ps_d[0:R * HG, g * SEQ:g * SEQ + SEQ], Wdx[:, g, :],
                                                   UC[:, g, bass.ds(b * SEQ, SEQ)], start=True, stop=True)
                        ins.then_inc(dt_made, 1)

                    def make_raw(b):
                        pe.wait_ge(dt_ready, b + 1)
                        need(pe, raw_ready, b)
                        for g in range(G):
                            ins = nc.tensor.matmul(ps_e[:, g * SEQ:g * SEQ + SEQ], Wdt[:, g, :], dts[:, g, :],
                                                   start=True, stop=True)
                        ins.then_inc(raw_made, 1)

                    def turn(b, s, first, last):
                        if not last:
                            transpose_x(b + 1)
                        if not first:
                            make_dt(b - 1)
                        if not last:
                            project(b + 1)
                        if not first:
                            make_raw(b - 1)

                    transpose_x(0)
                    project(0)
                    sequences(pe, turn)
                    make_dt(SEQS - 1)
                    make_raw(SEQS - 1)

                @block.scalar
                def _(act):
                    act.wait_ge(pads, 2)

                    def channels(b):
                        act.wait_ge(turned, b + 1)
                        need(act, projected, b)
                        nc.scalar.copy(xnT[:, :], ps_x[:, 0:SEQ]).then_inc(xnt_ready, 1)

                    def keep_u(b, s):
                        act.wait_ge(projected, b + 1)
                        need(act, conv_ready, b - 1)
                        nc.scalar.copy(up[s][:, :, K - 1:], ps_u[:, :].rearrange("p (g l) -> p g l", g=G)).then_inc(u_ready, 1)

                    def keep_z(b):
                        nc.scalar.activation(ZS[:, :, bass.ds(b * SEQ, SEQ)], ps_z[:, :].rearrange("p (g l) -> p g l", g=G),
                                             ACT.Silu).then_inc(z_used, 1)

                    def silu_u(b, s):
                        act.wait_ge(conv_ready, b + 1)
                        nc.scalar.activation(UC[:, :, bass.ds(b * SEQ, SEQ)], cv[s][:, :, :], ACT.Silu).then_inc(uc_ready, 1)

                    def keep_dt(b):
                        act.wait_ge(dt_made, b + 1)
                        need(act, raw_made, b)
                        nc.scalar.copy(dts[:, :, :], ps_d[0:R * HG, :].rearrange("p (g l) -> p g l", g=G)).then_inc(dt_ready, 1)

                    def keep_raw(b):
                        act.wait_ge(raw_made, b + 1)
                        for g in range(G):
                            ins = nc.scalar.activation(DELTA[:, g, bass.ds(b * SEQ, SEQ)], ps_e[:, g * SEQ:g * SEQ + SEQ],
                                                       ACT.Identity, bias=dtb[:, g:g + 1])
                        ins.then_inc(raw_ready, 1)

                    def turn(b, s, first, last):
                        if not last:
                            channels(b + 1)
                        if not first:
                            keep_dt(b - 1)
                        if not last:
                            keep_u(b + 1, 1 - s)
                            keep_z(b + 1)
                        if not first:
                            keep_raw(b - 1)
                        silu_u(b, s)

                    channels(0)
                    keep_u(0, 0)
                    keep_z(0)
                    sequences(act, turn)
                    keep_dt(SEQS - 1)
                    keep_raw(SEQS - 1)

        with ExitStack() as inner:
            PIECE = 2048
            PIECES = G * TOK // PIECE
            tail = [inner.enter_context(nc.sbuf_tensor(f"m2_tail{i}", [P, PIECE], F32)) for i in range(2)]
            flat = DELTA[:, :, :].rearrange("p g t -> p (g t)")
            abs_done, exp_done, ln_ready, sp_done = sem("abs_done"), sem("exp_done"), sem("ln_ready"), sem("sp_done")
            with nc.Block() as block:
                @block.scalar
                def _(act):
                    for i in range(PIECES):
                        at, v = slice(i * PIECE, (i + 1) * PIECE), tail[i % 2][:, :]
                        need(act, sp_done, i - 1)
                        nc.scalar.activation(v, flat[:, at], ACT.Abs).then_inc(abs_done, 1)
                        act.wait_ge(abs_done, i + 1)
                        nc.scalar.activation(v, v, ACT.Exp, scale=-1.0).then_inc(exp_done, 1)
                        act.wait_ge(exp_done, i + 1)
                        nc.scalar.activation(v, v, ACT.Ln, bias=1.0).then_inc(ln_ready, 1)

                @block.vector
                def _(dve):
                    for i in range(PIECES):
                        at, v = slice(i * PIECE, (i + 1) * PIECE), tail[i % 2][:, :]
                        dve.wait_ge(ln_ready, i + 1)
                        nc.vector.scalar_tensor_tensor(out=flat[:, at], in0=flat[:, at], scalar=0.0, in1=v,
                                                       op0=ALU.max, op1=ALU.add).then_inc(sp_done, 1)

        with ExitStack() as inner:
            def isb(name, shape):
                return inner.enter_context(nc.sbuf_tensor("m3_" + name, shape, F32))

            def ips(name, cols):
                return inner.enter_context(nc.psum_tensor("m3_" + name, [P, cols], F32))

            UNITS = G * CHUNKS
            POOL = 2
            dA = [isb(f"dA{i}", [P, NC_, SEQ]) for i in range(2)]
            dBu = [isb(f"dBu{i}", [P, NC_, SEQ]) for i in range(2)]
            hs = [isb(f"hs{i}", [P, NC_, SEQ]) for i in range(2)]
            hc = [isb(f"hc{i}", [P, NC_, SEQ]) for i in range(2)]
            du = isb("du", [P, SEQ])
            part = isb("part", [P, 2, SEQ])
            ysum = isb("ysum", [P, G, SEQ])
            yT = isb("yT", [P, G, SEQ])
            ps_B = [ips(f"ps_B{i}", W) for i in range(2)]
            ps_C = ips("ps_C", W)
            ps_o = ips("ps_o", TPS * P)
            dA_zero, B_ready, C_ready, dA_ready = sem("dA_zero"), sem("B_ready"), sem("C_ready"), sem("dA_ready")
            du_ready, dBu_done, scan_done, hc_ready = sem("du_ready"), sem("dBu_done"), sem("scan_done"), sem("hc_ready")
            pool_steps, y_partial, y_ready = sem("pool_steps"), sem("y_partial"), sem("y_ready")
            alone = sem("alone")
            y_steps, out_made, x_added = sem("y_steps"), sem("out_made"), sem("x_added")

            with nc.Block() as block:
                @block.tensor
                def _(pe):
                    def out_proj(b):
                        pe.wait_ge(y_ready, G * b + G)
                        need(pe, x_added, b)
                        for t in range(TPS):
                            for g in range(G):
                                o = t * P + g * HG * DH
                                ins = nc.tensor.matmul(ps_o[:, o:o + HG * DH], yT[:, g, t * P:t * P + P], Wo[:, g, :],
                                                       start=True, stop=True)
                        ins.then_inc(out_made, 1)

                    def repeat(ps, column, b, u, done):
                        g, c = divmod(u, CHUNKS)
                        for j in range(NC_):
                            ins = nc.tensor.matmul(ps[:, j * SEQ:j * SEQ + SEQ], WBC[:, g, column + NC_ * c + j, :],
                                                   UC[:, g, bass.ds(b * SEQ, SEQ)], start=True, stop=True)
                        ins.then_inc(done, 1)

                    def turn(b, first, last=False):
                        for u in range(UNITS):
                            n = UNITS * b + u
                            if u + 1 < UNITS or not last:
                                need(pe, dBu_done, n)
                                repeat(ps_B[(u + 1) % 2], 0, b + (u + 1) // UNITS, (u + 1) % UNITS, B_ready)
                            need(pe, hc_ready, n)
                            repeat(ps_C, N, b, u, C_ready)
                            if u == 1 and not first:
                                out_proj(b - 1)

                    repeat(ps_B[0], 0, 0, 0, B_ready)
                    turn(0, True)
                    turn(1, False)
                    with pe.Fori(2, SEQS - 1) as b:
                        turn(b, False)
                    turn(SEQS - 1, False, True)
                    out_proj(SEQS - 1)

                @block.scalar
                def _(act):
                    act.wait_ge(dA_zero, 2)

                    def turn(b):
                        rest = bass.ds(b * SEQ + 1, SEQ - 1)
                        for u in range(UNITS):
                            g, c = divmod(u, CHUNKS)
                            need(act, scan_done, UNITS * b + u - 1)
                            act.sem_inc(alone, 1)
                            for j in range(NC_):
                                s = NC_ * c + j
                                ins = nc.scalar.activation(dA[u % 2][:, j, 1:], DELTA[:, g, rest], ACT.Exp,
                                                           scale=A[:, g, s:s + 1])
                            ins.then_inc(dA_ready, 1)

                    turn(0)
                    with act.Fori(1, SEQS) as b:
                        turn(b)

                @block.vector
                def _(dve):
                    for i in range(2):
                        nc.vector.memset(dA[i][:, :, 0:1], 0.0).then_inc(dA_zero, 1)
                    dve.wait_ge(dA_zero, 2)
                    c2 = Chain(dve, y_steps)

                    def gate(b, g):
                        seq = bass.ds(b * SEQ, SEQ)
                        dve.wait_ge(y_partial, (CHUNKS - 1) * (G * b + g + 1))
                        need(dve, out_made, b)
                        c2.link(nc.vector.scalar_tensor_tensor(out=yT[:, g, :], in0=UC[:, g, seq], scalar=dsk[:, g:g + 1],
                                                               in1=ysum[:, g, :], op0=ALU.mult, op1=ALU.add))
                        nc.vector.tensor_tensor(yT[:, g, :], yT[:, g, :], ZS[:, g, seq], ALU.mult).then_inc(y_ready, 1)

                    def add_out(b):
                        dve.wait_ge(out_made, b + 1)
                        tiles = bass.ds(b * TPS, TPS)
                        nc.vector.tensor_tensor(X[:, tiles, :], X[:, tiles, :],
                                                ps_o[:, :].rearrange("p (t c) -> p t c", t=TPS), ALU.add).then_inc(x_added, 1)

                    def expand(b, u):
                        g, n, seq = u // CHUNKS, UNITS * b + u, bass.ds(b * SEQ, SEQ)
                        if u % CHUNKS == 0:
                            need(dve, dBu_done, n)
                            nc.vector.tensor_tensor(du[:, :], DELTA[:, g, seq], UC[:, g, seq], ALU.mult).then_inc(du_ready, 1)
                            dve.wait_ge(du_ready, G * b + g + 1)
                        dve.wait_ge(B_ready, n + 1)
                        need(dve, scan_done, n - 1)
                        nc.vector.tensor_tensor(dBu[u % 2][:, :, :], ps_B[u % 2][:, :].rearrange("p (j l) -> p j l", j=NC_),
                                                du[:, :].unsqueeze(1).to_broadcast([P, NC_, SEQ]),
                                                ALU.mult).then_inc(dBu_done, 1)

                    def turn(b, first, last=False):
                        for u in range(UNITS):
                            n, s = UNITS * b + u, u % 2
                            dve.wait_ge(dBu_done, n + 1)
                            dve.wait_ge(dA_ready, n + 1)
                            need(dve, hc_ready, n - 1)
                            nc.vector.tensor_tensor_scan(hs[s][:, :, :].rearrange("p j l -> p (j l)"),
                                                         dA[s][:, :, :].rearrange("p j l -> p (j l)"),
                                                         dBu[s][:, :, :].rearrange("p j l -> p (j l)"), 0.0,
                                                         ALU.mult, ALU.add).then_inc(scan_done, 1)
                            if u + 1 < UNITS:
                                expand(b, u + 1)
                            elif not last:
                                expand(b + 1, 0)
                            dve.wait_ge(scan_done, n + 1)
                            dve.wait_ge(C_ready, n + 1)
                            need(dve, pool_steps, POOL * (n - 1))
                            nc.vector.tensor_tensor(hc[s][:, :, :], ps_C[:, :].rearrange("p (j l) -> p j l", j=NC_),
                                                    hs[s][:, :, :], ALU.mult).then_inc(hc_ready, 1)
                            if u == CHUNKS:
                                gate(b, 0)
                            if u == 0 and not first:
                                gate(b - 1, 1)
                            if u == 2 and not first:
                                add_out(b - 1)

                    expand(0, 0)
                    c2.turn(0, 1)
                    turn(0, True)
                    c2.end(1)
                    c2.turn(0, 2)
                    turn(1, False)
                    c2.end(1)
                    with dve.Fori(2, SEQS - 1) as b:
                        c2.turn(b - 2, 2)
                        turn(b, False)
                    c2.end(SEQS - 3)
                    c2.turn(0, 2)
                    turn(SEQS - 1, False, True)
                    c2.end(1)
                    gate(SEQS - 1, 1)
                    add_out(SEQS - 1)
                    dve.wait_ge(x_added, SEQS)

                @block.gpsimd
                def _(pool):
                    def turn(b):
                        for u in range(UNITS):
                            g, c = divmod(u, CHUNKS)
                            n = UNITS * b + u
                            pool.wait_ge(hc_ready, n + 1)
                            if c == 0:
                                need(pool, y_ready, G * (b - 1) + g + 1 if not isinstance(b, int) or b else 0)
                            v = hc[u % 2]
                            nc.gpsimd.tensor_tensor(part[:, :, :], v[:, 0:2, :], v[:, 2:4, :], ALU.add).then_inc(pool_steps, 1)
                            pool.wait_ge(pool_steps, POOL * n + 1)
                            if c == 0:
                                nc.gpsimd.tensor_tensor(ysum[:, g, :], part[:, 0, :], part[:, 1, :], ALU.add).then_inc(pool_steps, 1)
                                pool.wait_ge(pool_steps, POOL * n + 2)
                            else:
                                nc.gpsimd.tensor_tensor(part[:, 0, :], part[:, 0, :], part[:, 1, :], ALU.add).then_inc(pool_steps, 1)
                                pool.wait_ge(pool_steps, POOL * n + 2)
                                ins = nc.gpsimd.tensor_tensor(ysum[:, g, :], ysum[:, g, :], part[:, 0, :], ALU.add)
                                ins.then_inc(y_partial, 1)
                                pool.wait_ge(y_partial, (CHUNKS - 1) * (G * b + g) + c)

                    turn(0)
                    with pool.Fori(1, SEQS) as b:
                        turn(b)
        sem.clear()


def expert_layer(nc, X, ident, gate_w, w1, b1, w2, b2):
    E = 8
    CAP = int(1.25 * SEQS * SEQ / E)
    TG = 4
    GROUPS = TILES // TG
    with ExitStack() as ctx:
        def sb(name, shape):
            return ctx.enter_context(nc.sbuf_tensor("e_" + name, shape, F32))

        def ps(name, cols):
            return ctx.enter_context(nc.psum_tensor("e_" + name, [P, cols], F32))

        sem = Semaphores(nc, "e_")

        mean, rstd = sb("mean", [P, TILES]), sb("rstd", [P, TILES])
        layernorm_stats(nc, X, mean, rstd, "e")
        W1, W2 = sb("W1", [P, E, P]), sb("W2", [P, E, P])
        B1, B2, Wg = sb("B1", [P, E]), sb("B2", [E, P]), sb("Wg", [P, E])
        XT = sb("XT", [P, SEQS, SEQ])
        xn = [sb(f"xn{i}", [P, TPS, P]) for i in range(2)]
        xw = [sb(f"xw{i}", [P, SEQ]) for i in range(2)]
        L = sb("L", [P, TILES, E])
        top, total = sb("top", [P, TILES]), sb("total", [P, TILES])
        above, level = sb("above", [P, TILES, E, E]), sb("level", [P, TILES, E, E])
        earlier = sb("earlier", [P, E, E])
        rank = sb("rank", [P, TILES, E])
        counts, keep, ones = sb("counts", [P, E]), sb("keep", [P, E]), sb("ones", [P, P])
        gw = sb("gw", [P, TG, E])
        gT = sb("gT", [E, TG * P])
        h = [sb(f"h{i}", [P, TG * P]) for i in range(2)]
        ps_x, ps_l, ps_c = ps("ps_x", 512), ps("ps_l", 512), ps("ps_c", 512)
        ps_h = [ps(f"ps_h{i}", 512) for i in range(2)]
        ps_y = [ps(f"ps_y{i}", 512) for i in range(2)]
        ps_b = ps("ps_b", 512)
        loaded, normed, turned, xw_ready, xt_ready = (sem(s) for s in ("loaded", "normed", "turned", "xw_ready", "xt_ready"))
        logits_made, logits_ready, pick, exp_done = (sem(s) for s in ("logits_made", "logits_ready", "pick", "exp_done"))
        counted, summed, consts = sem("counted"), sem("summed"), sem("consts")
        h_made, h_ready, y_made, y_added = sem("h_made"), sem("h_ready"), sem("y_made"), sem("y_added")
        gt_made, gt_ready, bias_made, bias_added = sem("gt_made"), sem("gt_ready"), sem("bias_made"), sem("bias_added")
        weighted, gw_ready = sem("weighted"), sem("gw_ready")

        ps_xn = (ps_x, ps_b)

        def sequences(eng, turn):
            turn(0, 0, False)
            turn(1, 1, False)
            with eng.Fori(0, SEQS // 2 - 2) as pair:
                turn(2 * pair + 2, 0, False)
                turn(2 * pair + 3, 1, False)
            turn(SEQS - 2, 0, False)
            turn(SEQS - 1, 1, True)

        with nc.Block() as block:
            @block.sync
            def _(sp):
                for dst, src in ((W1[:, :, :], w1.rearrange("e h f -> h e f")), (W2[:, :, :], w2.rearrange("e f g -> f e g")),
                                 (B1[:, :], b1), (B2[:, :], b2), (Wg[:, :], gate_w)):
                    sp.dma_start(dst, src).then_inc(loaded, 16)

            @block.gpsimd
            def _(pool):
                nc.gpsimd.memset(ones[:, :], 1.0).then_inc(consts, 1)
                nc.gpsimd.memset(earlier[:, :, :], 0.0).then_inc(consts, 1)
                pool.wait_ge(consts, 2)
                for e in range(1, E):
                    nc.gpsimd.memset(earlier[:, e, 0:e], 1.0).then_inc(consts, 1)

                def turn(b, s, last):
                    pool.wait_ge(xw_ready, b + 1)
                    nc.gpsimd.tensor_copy(XT[:, bass.ds(b, 1), :].rearrange("p a l -> p (a l)"), xw[s][:, :]).then_inc(xt_ready, 1)

                sequences(pool, turn)
                pool.wait_ge(weighted, 1)

                def group(r):
                    need(pool, gt_made, r)
                    nc.gpsimd.tensor_copy(gw[:, :, :], L[:, bass.ds(r * TG, TG), :]).then_inc(gw_ready, 1)

                group(0)
                with pool.Fori(1, GROUPS) as r:
                    group(r)

            @block.vector
            def _(dve):
                def norm(b, s):
                    need(dve, turned, b - 1)
                    for t in range(TPS):
                        at = bass.ds(b * TPS + t, 1)
                        nc.vector.tensor_scalar(xn[s][:, t, :], X[:, at, :].rearrange("p a c -> p (a c)"),
                                                mean[:, at], rstd[:, at], ALU.subtract, ALU.mult).then_inc(normed, 1)

                def turn(b, s, last):
                    if not last:
                        norm(b + 1, 1 - s)
                    dve.wait_ge(logits_made, b + 1)
                    nc.vector.tensor_copy(L[:, bass.ds(b * TPS, TPS), :],
                                          ps_l[:, 0:TPS * E].rearrange("p (t e) -> p t e", t=TPS)).then_inc(logits_ready, 1)

                norm(0, 0)
                sequences(dve, turn)
                dve.wait_ge(logits_ready, SEQS)
                dve.wait_ge(consts, 2 + E - 1)
                c = Chain(dve, pick)
                per_token = lambda v: v[:, :].unsqueeze(2).to_broadcast([P, TILES, E])
                c.link(nc.vector.tensor_reduce(top[:, :], L[:, :, :], AX_X, ALU.max))
                c.link(nc.vector.tensor_tensor(L[:, :, :], L[:, :, :], per_token(top), ALU.subtract))
                dve.wait_ge(exp_done, 1)
                c.link(nc.vector.tensor_reduce(total[:, :], L[:, :, :], AX_X, ALU.add))
                c.link(nc.vector.reciprocal(total[:, :], total[:, :]))
                c.link(nc.vector.tensor_tensor(L[:, :, :], L[:, :, :], per_token(total), ALU.mult))
                mine = L[:, :, :].unsqueeze(3).to_broadcast([P, TILES, E, E])
                other = L[:, :, :].unsqueeze(2).to_broadcast([P, TILES, E, E])
                c.step(nc.vector.tensor_tensor(above[:, :, :, :], other, mine, ALU.is_gt))
                c.link(nc.vector.tensor_tensor(level[:, :, :, :], other, mine, ALU.is_equal))
                c.link(nc.vector.tensor_tensor(
                    level[:, :, :, :].rearrange("p t e f -> p t (e f)"), level[:, :, :, :].rearrange("p t e f -> p t (e f)"),
                    earlier[:, :, :].rearrange("p e f -> p (e f)").unsqueeze(1).to_broadcast([P, TILES, E * E]), ALU.mult))
                c.link(nc.vector.tensor_tensor(above[:, :, :, :], above[:, :, :, :], level[:, :, :, :], ALU.add))
                c.link(nc.vector.tensor_reduce(rank[:, :, :], above[:, :, :, :], AX_X, ALU.add))
                c.link(nc.vector.tensor_scalar(rank[:, :, :], rank[:, :, :], 1.5, None, ALU.is_lt))
                nc.vector.tensor_reduce(counts[:, :], rank[:, :, :].rearrange("p t e -> p e t"), AX_X,
                                        ALU.add).then_inc(counted, 1)
                c.link(nc.vector.tensor_tensor(L[:, :, :], L[:, :, :], rank[:, :, :], ALU.mult))
                dve.wait_ge(summed, 1)
                c.link(nc.vector.tensor_scalar(keep[:, :], ps_c[:, 0:E], CAP + 0.5, None, ALU.is_lt))
                nc.vector.tensor_tensor(L[:, :, :], L[:, :, :], keep[:, :].unsqueeze(1).to_broadcast([P, TILES, E]),
                                        ALU.mult).then_inc(weighted, 1)
                dve.wait_ge(weighted, 1)

                def experts(r):
                    for e in range(E):
                        n = E * r + e
                        dve.wait_ge(y_made, n + 1)
                        if e:
                            dve.wait_ge(y_added, TG * n)
                        else:
                            need(dve, bias_added, r)
                        for t in range(TG):
                            row = X[:, bass.ds(r * TG + t, 1), :].rearrange("p a c -> p (a c)")
                            weight = L[:, bass.ds(r * TG + t, 1), e]
                            nc.vector.scalar_tensor_tensor(out=row, in0=ps_y[e % 2][:, t * P:t * P + P], scalar=weight,
                                                           in1=row, op0=ALU.mult, op1=ALU.add).then_inc(y_added, 1)
                    dve.wait_ge(bias_made, r + 1)
                    dve.wait_ge(y_added, TG * (E * r + E))
                    rows = X[:, bass.ds(r * TG, TG), :]
                    nc.vector.tensor_tensor(rows, rows, ps_b[:, :].rearrange("p (t c) -> p t c", t=TG),
                                            ALU.add).then_inc(bias_added, 1)

                experts(0)
                with dve.Fori(1, GROUPS) as r:
                    experts(r)
                dve.wait_ge(bias_added, GROUPS)

            @block.scalar
            def _(act):
                def turn(b, s, last):
                    act.wait_ge(turned, b + 1)
                    need(act, logits_made, b - 1)
                    need(act, xt_ready, b - 1)
                    nc.scalar.copy(xw[s][:, :], ps_xn[s][:, 0:SEQ]).then_inc(xw_ready, 1)

                sequences(act, turn)
                act.wait_ge(pick, 2)
                nc.scalar.activation(L[:, :, :], L[:, :, :], ACT.Exp).then_inc(exp_done, 1)
                act.wait_ge(loaded, 16 * 5)

                def experts(r):
                    for e in range(E):
                        n = E * r + e
                        act.wait_ge(h_made, n + 1)
                        need(act, y_made, n - 1)
                        nc.scalar.activation(h[e % 2][:, :], ps_h[e % 2][:, :], ACT.Silu, bias=B1[:, e:e + 1]).then_inc(h_ready, 1)
                    act.wait_ge(gt_made, r + 1)
                    need(act, bias_made, r)
                    nc.scalar.copy(gT[:, :], ps_x[0:E, :]).then_inc(gt_ready, 1)

                experts(0)
                with act.Fori(1, GROUPS) as r:
                    experts(r)

            @block.tensor
            def _(pe):
                pe.wait_ge(loaded, 16 * 5)

                def transpose_x(b, s):
                    pe.wait_ge(normed, TPS * b + TPS)
                    need(pe, xw_ready, b - 1)
                    for t in range(TPS):
                        ins = nc.tensor.transpose(ps_xn[s][:, t * P:t * P + P], xn[s][:, t, :], ident[:, :])
                    ins.then_inc(turned, 1)

                def turn(b, s, last):
                    if not last:
                        transpose_x(b + 1, 1 - s)
                    pe.wait_ge(xw_ready, b + 1)
                    need(pe, logits_ready, b)
                    for t in range(TPS):
                        ins = nc.tensor.matmul(ps_l[:, t * E:t * E + E], xw[s][:, t * P:t * P + P], Wg[:, :],
                                               start=True, stop=True)
                    ins.then_inc(logits_made, 1)

                transpose_x(0, 0)
                sequences(pe, turn)
                pe.wait_ge(counted, 1)
                nc.tensor.matmul(ps_c[:, 0:E], ones[:, :], counts[:, :], start=True, stop=True).then_inc(summed, 1)
                pe.wait_ge(xt_ready, SEQS)
                pe.wait_ge(weighted, 1)

                def first(r, e):
                    n = E * r + e
                    need(pe, h_ready, n - 1)
                    nc.tensor.matmul(ps_h[e % 2][:, :], W1[:, e, :],
                                     XT[:, bass.ds(r * (TG // TPS), TG // TPS), :].rearrange("p a l -> p (a l)"),
                                     start=True, stop=True).then_inc(h_made, 1)

                def second(r, e):
                    n = E * r + e
                    pe.wait_ge(h_ready, n + 1)
                    need(pe, y_added, TG * (n - 1))
                    for t in range(TG):
                        ins = nc.tensor.matmul(ps_y[e % 2][:, t * P:t * P + P], h[e % 2][:, t * P:t * P + P], W2[:, e, :],
                                               start=True, stop=True)
                    ins.then_inc(y_made, 1)

                def experts(r):
                    first(r, 0)
                    for e in range(E):
                        if e + 1 < E:
                            first(r, e + 1)
                        second(r, e)
                    pe.wait_ge(gw_ready, r + 1)
                    need(pe, gt_ready, r)
                    for t in range(TG):
                        ins = nc.tensor.transpose(ps_x[0:E, t * P:t * P + P],
                                                  gw[:, t, :], ident[:, :])
                    ins.then_inc(gt_made, 1)
                    pe.wait_ge(gt_ready, r + 1)
                    need(pe, bias_added, r)
                    for t in range(TG):
                        ins = nc.tensor.matmul(ps_b[:, t * P:t * P + P], gT[:, t * P:t * P + P], B2[:, :],
                                               start=True, stop=True)
                    ins.then_inc(bias_made, 1)

                experts(0)
                with pe.Fori(1, GROUPS) as r:
                    experts(r)
        sem.clear()


def full_attention(nc, X, ident, w_q, b_q, w_k, b_k, w_v, b_v, w_o, b_o, table):
    H, D = 16, 8
    SCALE = float(D) ** -0.5
    SPREAD = P + D
    SPAN = 2 * SEQ - 1
    RING = 4
    AHEAD = 5
    TURN, WEIGH = 3, 4
    with ExitStack() as ctx:
        def sb(name, shape):
            return ctx.enter_context(nc.sbuf_tensor("a_" + name, shape, F32))

        def ps(name, cols=512):
            return ctx.enter_context(nc.psum_tensor("a_" + name, [P, cols], F32))

        sem = Semaphores(nc, "a_")

        mean, rstd = sb("mean", [P, TILES]), sb("rstd", [P, TILES])
        layernorm_stats(nc, X, mean, rstd, "a")
        W = sb("W", [P, 4, P])
        bq, bk = sb("bq", [P, 1]), sb("bk", [P, 1])
        bv, bo = sb("bv", [P, P]), sb("bo", [P, P])
        hmask = sb("hmask", [P, H])
        near = sb("near", [P, H, SEQ])
        far = sb("far", [P, H])
        xn, xT, xTr = sb("xn", [P, TPS, P]), sb("xT", [P, SEQ]), sb("xTr", [P, SEQ])
        qT = [sb(f"qT{i}", [P, SEQ]) for i in range(2)]
        kT = [sb(f"kT{i}", [P, SEQ]) for i in range(2)]
        qz = [sb(f"qz{i}", [P, H, SEQ]) for i in range(2)]
        Vz = [sb(f"Vz{i}", [P, TPS, H * SPREAD]) for i in range(2)]
        nmax = [sb(f"nmax{i}", [P, TPS]) for i in range(RING)]
        den = [sb(f"den{i}", [P, TPS]) for i in range(RING)]
        prob = [sb(f"prob{i}", [P, TPS, SEQ]) for i in range(RING)]
        probT = [sb(f"probT{i}", [P, TPS, SEQ]) for i in range(RING)]
        oT = sb("oT", [P, SEQ])
        ps_x, ps_q = ps("ps_x"), ps("ps_q")
        ps_o = [ps(f"ps_o{i}", SEQ) for i in range(2)]
        ps_s = [ps(f"ps_s{i}") for i in range(2)]
        ps_t = [ps(f"ps_t{i}") for i in range(2)]
        loaded, masks, zeroed = sem("loaded"), sem("masks"), sem("zeroed")
        normed, turned, xt_ready, xtr_ready = sem("normed"), sem("turned"), sem("xt_ready"), sem("xtr_ready")
        qkv_made, q_ready, k_ready, qz_ready, v_ready = (sem(s) for s in ("qkv_made", "q_ready", "k_ready", "qz_ready", "v_ready"))
        scored, biased, maxed, nmax_ready, exp_done = (sem(s) for s in ("scored", "biased", "maxed", "nmax_ready", "exp_done"))
        inverted, prob_ready, prob_turned, probT_ready, pv_done = (
            sem(s) for s in ("inverted", "prob_ready", "prob_turned", "probT_ready", "pv_done"))
        oT_ready, out_made, out_added, x_ready = (sem(s) for s in ("oT_ready", "out_made", "out_added", "x_ready"))
        LOADS = 16 * 10

        def sequences(eng, turn, start, tail):
            start()
            turn(0, 0, True, False)
            turn(1, 1, False, False)
            with eng.Fori(0, SEQS // 2 - 2) as pair:
                turn(2 * pair + 2, 0, False, False)
                turn(2 * pair + 3, 1, False, False)
            turn(SEQS - 2, 0, False, False)
            turn(SEQS - 1, 1, False, True)
            tail()

        with nc.Block() as block:
            @block.sync
            def _(sp):
                for i, w in enumerate((w_q, w_k, w_v, w_o)):
                    sp.dma_start(W[:, i, :], w).then_inc(loaded, 16)
                for dst, src in ((bq, b_q), (bk, b_k)):
                    sp.dma_start(dst[:, :], src.rearrange("(c a) -> c a", a=1)).then_inc(loaded, 16)
                for dst, src in ((bv, b_v), (bo, b_o)):
                    sp.dma_start(dst[:, :], src.rearrange("(a c) -> a c", a=1).to_broadcast([P, P])).then_inc(loaded, 16)
                sp.dma_start(near[:, :, :], bass.AP(tensor=table.tensor, offset=0, ap=[[1, P], [SPAN, H], [1, SEQ]])
                             ).then_inc(loaded, 16)
                with nc.allow_non_contiguous_dma(reason="small"):
                    sp.dma_start(far[:, :], bass.AP(tensor=table.tensor, offset=SPAN - 1, ap=[[0, P], [SPAN, H]])
                                 ).then_inc(loaded, 16)

            @block.gpsimd
            def _(pool):
                for v in Vz:
                    nc.gpsimd.memset(v[:, :, :], 0.0).then_inc(zeroed, 1)

            @block.vector
            def _(dve):
                def norm(b):
                    need(dve, turned, b)
                    for t in range(TPS):
                        at = bass.ds(b * TPS + t, 1)
                        nc.vector.tensor_scalar(xn[:, t, :], X[:, at, :].rearrange("p a c -> p (a c)"),
                                                mean[:, at], rstd[:, at], ALU.subtract, ALU.mult).then_inc(normed, 1)

                def reverse(b):
                    dve.wait_ge(xt_ready, b + 1)
                    need(dve, qkv_made, b)
                    nc.vector.tensor_copy(xTr[:, :], xT[:, ::-1]).then_inc(xtr_ready, 1)

                def values(b, s, t):
                    dve.wait_ge(qkv_made, b + 1)
                    if isinstance(b, int) and b < 2:
                        dve.wait_ge(zeroed, 2)
                    need(dve, pv_done, H * (b - 1))
                    nc.vector.tensor_tensor(
                        Vz[s][:, t, :].rearrange("p (h k) -> p h k", h=H)[:, :, 0:D],
                        ps_x[:, SEQ + t * P:SEQ + t * P + P].rearrange("p (h d) -> p h d", h=H),
                        bv[:, :].rearrange("p (h d) -> p h d", h=H), ALU.add).then_inc(v_ready, 1)

                def queries(b, s, heads):
                    dve.wait_ge(q_ready, b + 1)
                    need(dve, scored, H * (b - 1))
                    for h in heads:
                        nc.vector.tensor_scalar(qz[s][:, h, :], qT[s][:, :], hmask[:, h:h + 1], SCALE,
                                                ALU.mult, ALU.mult).then_inc(qz_ready, 1)

                def shift(b, h):
                    n, i, r = H * b + h, h % 2, h % RING
                    dve.wait_ge(scored, n + 1)
                    nc.vector.tensor_tensor(ps_s[i][:, 0:SEQ], ps_s[i][:, 0:SEQ], near[:, h, :], ALU.add).then_inc(biased, 1)
                    dve.wait_ge(biased, n + 1)
                    need(dve, exp_done, n + 1 - RING)
                    nc.vector.tensor_reduce(nmax[r][:, :], ps_s[i][:, :].rearrange("p (t k) -> p t k", t=TPS), AX_X,
                                            ALU.max, negate=True).then_inc(maxed, 1)
                    dve.wait_ge(maxed, n + 1)
                    nc.vector.scalar_tensor_tensor(out=nmax[r][:, 1:2], in0=nmax[r][:, 1:2], scalar=far[:, h:h + 1],
                                                   in1=far[:, h:h + 1], op0=ALU.subtract, op1=ALU.add).then_inc(nmax_ready, 1)

                def scale(b, h):
                    n, r = H * b + h, h % RING
                    dve.wait_ge(exp_done, n + 1)
                    nc.vector.reciprocal(den[r][:, :], den[r][:, :]).then_inc(inverted, 1)
                    dve.wait_ge(inverted, n + 1)
                    for t in range(TPS):
                        ins = nc.vector.tensor_scalar(prob[r][:, t, :], prob[r][:, t, :], den[r][:, t:t + 1], None, ALU.mult)
                    ins.then_inc(prob_ready, 1)

                def add_out(b):
                    dve.wait_ge(out_made, b + 1)
                    rows = X[:, bass.ds(b * TPS, TPS), :]
                    nc.vector.tensor_tensor(rows, rows, ps_x[:, 0:SEQ].rearrange("p (t c) -> p t c", t=TPS),
                                            ALU.add).then_inc(out_added, 1)
                    dve.wait_ge(out_added, b + 1)
                    nc.vector.tensor_tensor(rows, rows, bo[:, :].unsqueeze(1).to_broadcast([P, TPS, P]),
                                            ALU.add).then_inc(x_ready, 1)

                def start():
                    nc.vector.tensor_reduce(hmask[:, :], ident[:, :].rearrange("p (h d) -> p h d", h=H), AX_X,
                                            ALU.add).then_inc(masks, 1)
                    dve.wait_ge(masks, 1)
                    dve.wait_ge(loaded, LOADS)
                    norm(0)
                    reverse(0)
                    for t in range(TPS):
                        values(0, 0, t)
                    queries(0, 0, range(AHEAD))

                def turn(b, s, first, last):
                    for h in range(H):
                        shift(b, h)
                        if h < H - AHEAD:
                            queries(b, s, (h + AHEAD,))
                        elif not last:
                            queries(b + 1, 1 - s, (h + AHEAD - H,))
                        if h:
                            scale(b, h - 1)
                        elif not first:
                            scale(b - 1, H - 1)
                        if h == WEIGH + 2 and not first:
                            add_out(b - 1)
                        if not last:
                            if h == 2:
                                norm(b + 1)
                            if h == 8:
                                reverse(b + 1)
                            if h in (9, 10):
                                values(b + 1, 1 - s, h - 9)

                def tail():
                    scale(SEQS - 1, H - 1)
                    add_out(SEQS - 1)
                    dve.wait_ge(x_ready, SEQS)

                sequences(dve, turn, start, tail)

            @block.scalar
            def _(act):
                def channels(b):
                    act.wait_ge(turned, b + 1)
                    need(act, qkv_made, b)
                    need(act, xtr_ready, b)
                    nc.scalar.copy(xT[:, :], ps_x[:, 0:SEQ]).then_inc(xt_ready, 1)

                def keys(b, s):
                    act.wait_ge(qkv_made, b + 1)
                    need(act, qz_ready, H * (b - 1))
                    nc.scalar.activation(qT[s][:, :], ps_q[:, 0:SEQ], ACT.Identity, bias=bq[:, :]).then_inc(q_ready, 1)
                    need(act, scored, H * (b - 1))
                    nc.scalar.activation(kT[s][:, :], ps_q[:, SEQ:2 * SEQ], ACT.Identity, bias=bk[:, :]).then_inc(k_ready, 1)

                def expo(b, h):
                    n, i, r = H * b + h, h % 2, h % RING
                    act.wait_ge(nmax_ready, n + 1)
                    need(act, prob_turned, n + 1 - RING)
                    for t in range(TPS):
                        ins = nc.scalar.activation(prob[r][:, t, :], ps_s[i][:, t * SEQ:t * SEQ + SEQ], ACT.Exp,
                                                   bias=nmax[r][:, t:t + 1], accum_out=den[r][:, t:t + 1])
                    ins.then_inc(exp_done, 1)

                def evacuate(b, h):
                    n, i, r = H * b + h, h % 2, h % RING
                    act.wait_ge(prob_turned, n + 1)
                    need(act, pv_done, n + 1 - RING)
                    nc.scalar.copy(probT[r][:, :, :], ps_t[i][:, :].rearrange("p (k q) -> p k q", k=TPS)).then_inc(probT_ready, 1)

                def outputs(b, s):
                    act.wait_ge(pv_done, H * b + H)
                    need(act, out_made, b)
                    nc.scalar.copy(oT[:, :], ps_o[s][:, :]).then_inc(oT_ready, 1)

                def start():
                    act.wait_ge(loaded, LOADS)
                    channels(0)
                    keys(0, 0)

                def turn(b, s, first, last):
                    for h in range(H):
                        if h >= TURN:
                            evacuate(b, h - TURN)
                        elif not first:
                            evacuate(b - 1, H - TURN + h)
                        expo(b, h)
                        if h == WEIGH and not first:
                            outputs(b - 1, 1 - s)
                        if not last:
                            if h == 8:
                                channels(b + 1)
                            if h == 9:
                                keys(b + 1, 1 - s)

                def tail():
                    for h in range(H - TURN, H):
                        evacuate(SEQS - 1, h)
                    outputs(SEQS - 1, 1)

                sequences(act, turn, start, tail)

            @block.tensor
            def _(pe):
                def transpose_x(b):
                    pe.wait_ge(normed, TPS * b + TPS)
                    need(pe, xt_ready, b)
                    need(pe, out_added, b - 1)
                    for t in range(TPS):
                        ins = nc.tensor.transpose(ps_x[:, t * P:t * P + P], xn[:, t, :], ident[:, :])
                    ins.then_inc(turned, 1)

                def project(b):
                    pe.wait_ge(xt_ready, b + 1)
                    pe.wait_ge(xtr_ready, b + 1)
                    need(pe, k_ready, b)
                    nc.tensor.matmul(ps_q[:, 0:SEQ], W[:, 0, :], xT[:, :], start=True, stop=True)
                    nc.tensor.matmul(ps_q[:, SEQ:2 * SEQ], W[:, 1, :], xTr[:, :], start=True, stop=True)
                    for t in range(TPS):
                        ins = nc.tensor.matmul(ps_x[:, SEQ + t * P:SEQ + t * P + P], xTr[:, t * P:t * P + P], W[:, 2, :],
                                               start=True, stop=True)
                    ins.then_inc(qkv_made, 1)

                def score(b, s, h):
                    n, i = H * b + h, h % 2
                    pe.wait_ge(qz_ready, n + 1)
                    if h == 0:
                        pe.wait_ge(k_ready, b + 1)
                    need(pe, exp_done, n - 1)
                    for t in range(TPS):
                        ins = nc.tensor.matmul(ps_s[i][:, t * SEQ:t * SEQ + SEQ], qz[s][:, h, t * P:t * P + P], kT[s][:, :],
                                               start=True, stop=True)
                    ins.then_inc(scored, 1)

                def turn_probs(b, h):
                    n, i, r = H * b + h, h % 2, h % RING
                    pe.wait_ge(prob_ready, n + 1)
                    need(pe, probT_ready, n - 1)
                    for k in range(TPS):
                        for t in range(TPS):
                            ins = nc.tensor.transpose(ps_t[i][:, k * SEQ + t * P:k * SEQ + t * P + P],
                                                      prob[r][:, t, k * P:k * P + P], ident[:, :])
                    ins.then_inc(prob_turned, 1)

                def weigh(b, s, h):
                    n, r = H * b + h, h % RING
                    pe.wait_ge(probT_ready, n + 1)
                    if h == 0:
                        pe.wait_ge(v_ready, TPS * b + TPS)
                        need(pe, oT_ready, b - 1)
                    for k in range(TPS):
                        ins = nc.tensor.matmul(ps_o[s][:, :], Vz[s][:, k, h * P:h * P + P], probT[r][:, k, :],
                                               start=(h == 0 and k == 0), stop=(h == H - 1 and k == TPS - 1))
                    ins.then_inc(pv_done, 1)

                def out_proj(b, known):
                    pe.wait_ge(oT_ready, b + 1)
                    pe.wait_ge(v_ready, TPS * known)
                    for t in range(TPS):
                        ins = nc.tensor.matmul(ps_x[:, t * P:t * P + P], oT[:, t * P:t * P + P], W[:, 3, :],
                                               start=True, stop=True)
                    ins.then_inc(out_made, 1)

                def start():
                    pe.wait_ge(loaded, LOADS)
                    transpose_x(0)
                    project(0)

                def turn(b, s, first, last):
                    for h in range(H):
                        score(b, s, h)
                        if h >= TURN:
                            turn_probs(b, h - TURN)
                        elif not first:
                            turn_probs(b - 1, H - TURN + h)
                        if h >= WEIGH:
                            weigh(b, s, h - WEIGH)
                        elif not first:
                            weigh(b - 1, 1 - s, H - WEIGH + h)
                        if h == WEIGH + 1 and not first:
                            out_proj(b - 1, b + 1)
                        if not last:
                            if h == 7:
                                transpose_x(b + 1)
                            if h == 9:
                                project(b + 1)

                def tail():
                    for x in range(WEIGH):
                        if x < TURN:
                            turn_probs(SEQS - 1, H - TURN + x)
                        weigh(SEQS - 1, 1, H - WEIGH + x)
                    out_proj(SEQS - 1, SEQS)

                sequences(pe, turn, start, tail)
        sem.clear()


def local_layers(nc, X, ident, w_qkv, q_scale, k_scale, w_o, ln_g, ln_b, w_1, b_1, w_2, b_2, rotary, masks):
    LAYERS, H, D, WIN = 6, 16, 64, 32
    INNER = H * D
    FF = w_2.shape[1]
    ITEMS = LAYERS * SEQS
    PAIRS = H // 2
    CH = 512
    HC = CH // D
    GH, HG = 4, H // 4
    K1 = P + WIN
    FK = [P, P, FF - 2 * P]
    with ExitStack() as ctx:
        def sb(name, shape, dt=F32):
            return ctx.enter_context(nc.sbuf_tensor("l_" + name, shape, dt))

        def ps(name, cols=512):
            return ctx.enter_context(nc.psum_tensor("l_" + name, [P, cols], F32))

        sem = Semaphores(nc, "l_")

        Wqkv = sb("Wqkv", [P, 3 * INNER])
        Wo = sb("Wo", [P, 2, PAIRS, P])
        W1 = sb("W1", [P, 2, 2 * FF])
        W2 = sb("W2", [P, 2, 3, P])
        b1 = sb("b1", [P, 2, 2 * FF])
        b2 = sb("b2", [P, 2, P])
        gain, offset = sb("gain", [P, LAYERS]), sb("offset", [P, LAYERS])
        own = [sb(f"own{x}", [P, LAYERS, TPS, D]) for x in "qk"]
        cross = [sb(f"cross{x}", [P, LAYERS, TPS, D]) for x in "qk"]
        mask0, mask1 = sb("mask0", [P, P], BF16), sb("mask1", [P, K1], BF16)
        identb = sb("identb", [P, P], BF16)
        xs, sT = sb("xs", [P, TPS, P]), sb("sT", [P, SEQ])
        sq = [sb(f"sq{i}", [P, CH]) for i in range(2)]
        t1 = [sb(f"t1_{i}", [P, CH]) for i in range(2)]
        t2 = [sb(f"t2_{i}", [P, CH]) for i in range(2)]
        n2, clampd, rn = sb("n2", [P, TPS, 2 * H]), sb("clampd", [P, TPS, 2 * H]), sb("rn", [P, TPS, 2 * H])
        half = sb("half", [P, 2 * H])
        qk = sb("qk", [P, 4, CH])
        qz = [sb(f"qz{i}", [P, PAIRS, 2, SEQ]) for i in range(2)]
        kT = [sb(f"kT{i}", [P, PAIRS, SEQ]) for i in range(2)]
        V = [sb(f"V{i}", [P, TPS, INNER]) for i in range(2)]
        sc8 = [sb(f"sc8_{i}", [P, TPS, H]) for i in range(2)]
        nmax = [sb(f"nmax{i}", [P, TPS, HG]) for i in range(2)]
        nbias = [sb(f"nbias{i}", [P, TPS, HG]) for i in range(2)]
        den = [sb(f"den{i}", [P, TPS, HG]) for i in range(2)]
        P0 = [sb(f"P0_{i}", [P, HG, P]) for i in range(2)]
        P1 = [sb(f"P1_{i}", [P, HG, K1]) for i in range(2)]
        PT0 = [sb(f"PT0_{i}", [P, HG, K1]) for i in range(2)]
        PT1 = [sb(f"PT1_{i}", [P, HG, P]) for i in range(2)]
        oT = sb("oT", [P, PAIRS, SEQ])
        xf, stats, mv = sb("xf", [P, TPS, P]), sb("stats", [P, TPS, 6]), sb("mv", [P, TPS, 2])
        var, rstd = sb("var", [P, TPS]), sb("rstd", [P, TPS])
        xn, xnT = sb("xn", [P, TPS, P]), sb("xnT", [P, SEQ])
        gate, gated, lin = sb("gate", [P, FF]), sb("gated", [P, FF]), sb("lin", [P, FF])
        hid = sb("hid", [P, TPS, FF])
        hT = sb("hT", [P, TPS, 3, P])
        ps_w = [ps(f"ps_w{i}") for i in range(2)]
        ps_t, ps_p, ps_o = ps("ps_t"), ps("ps_p"), ps("ps_o")
        ps_s0, ps_s1, ps_s2 = ps("ps_s0"), ps("ps_s1"), ps("ps_s2")

        names = ("setup consts zeroed scales_in qscales wqkv_in later_in shifted turned sT_ready qkv_made sq_done rot_done n2_made clamped "
                 "powed roped scaled qk_turned qkT_ready sc_ready v_ready scored maxed nm_ready exp_done inverted "
                 "norm_done bt_done pt_turned pt0_ready pt1_ready pv_done ot_ready wo_made x_attn shifted2 bn_done var_ready "
                 "rstd_ready xn_ready ft_made xnT_ready fw_made gate_ready gelu_done lin_ready h_ready ht_made "
                 "hT_ready w2_made ffn_part x_ffn aggr_done small_done").split()
        S = {n: sem(n) for n in names}
        (setup, consts, zeroed, scales_in, qscales, wqkv_in, later_in, shifted, turned, sT_ready, qkv_made, sq_done, rot_done, n2_made,
         clamped, powed, roped, scaled, qk_turned, qkT_ready, sc_ready, v_ready, scored, maxed, nm_ready, exp_done,
         inverted, norm_done, bt_done, pt_turned, pt0_ready, pt1_ready, pv_done, ot_ready, wo_made, x_attn, shifted2, bn_done,
         var_ready, rstd_ready, xn_ready, ft_made, xnT_ready, fw_made, gate_ready, gelu_done, lin_ready, h_ready,
         ht_made, hT_ready, w2_made, ffn_part, x_ffn, aggr_done, small_done) = (S[n] for n in names)
        sp_alone, dve_alone = sem("sp_alone"), sem("dve_alone")
        LATER = 16 * 6
        SHIFT = 16 * 3
        MISC = 16 * 10

        with ExitStack() as inner:
            base = inner.enter_context(nc.sbuf_tensor("l_base", [P, TPS, 4, D], F32))
            scale = inner.enter_context(nc.sbuf_tensor("l_scale", [P, 2, LAYERS, D], F32))
            maskf = inner.enter_context(nc.sbuf_tensor("l_maskf", [P, P + K1], F32))
            with nc.Block() as block:
                @block.sync
                def _(sp):
                    n = 0
                    for dst, src in (
                            (base[:, :, :, :], rotary.rearrange("(t p) k e -> p t k e", p=P)),
                            (scale[:, 0, :, :], q_scale.rearrange("(a l) e -> a l e", a=1).to_broadcast([P, LAYERS, D])),
                            (scale[:, 1, :, :], k_scale.rearrange("(a l) e -> a l e", a=1).to_broadcast([P, LAYERS, D])),
                            (maskf[:, :], masks)):
                        sp.dma_start(dst, src).then_inc(setup, 16)
                        n += 1
                    with nc.allow_non_contiguous_dma(reason="small"):
                        sp.dma_start(gain[:, :], ln_g.rearrange("l c -> c l")).then_inc(setup, 16)
                        sp.dma_start(offset[:, :], ln_b.rearrange("l c -> c l")).then_inc(setup, 16)
                    sp.wait_ge(setup, 16 * (n + 2))

                @block.vector
                def _(dve):
                    dve.wait_ge(setup, 16 * 6)
                    for x in range(2):
                        for t in range(TPS):
                            fac = lambda k: base[:, t, 2 * x + k, :].unsqueeze(1).to_broadcast([P, LAYERS, D])
                            nc.vector.tensor_tensor(own[x][:, :, t, :], scale[:, x, :, :], fac(0), ALU.mult).then_inc(qscales, 1)
                            for hf in range(2):
                                lo, hi = slice(hf * D // 2, (hf + 1) * D // 2), slice((1 - hf) * D // 2, (2 - hf) * D // 2)
                                nc.vector.tensor_tensor(cross[x][:, :, t, lo], scale[:, x, :, hi], fac(1)[:, :, lo],
                                                        ALU.mult).then_inc(qscales, 1)
                    nc.vector.tensor_copy(mask0[:, :], maskf[:, 0:P]).then_inc(qscales, 1)
                    nc.vector.tensor_copy(mask1[:, :], maskf[:, P:]).then_inc(qscales, 1)
                    nc.vector.tensor_copy(identb[:, :], ident[:, :]).then_inc(qscales, 1)
                    nc.vector.memset(xs[0:1, 0, D:], 0.0).then_inc(qscales, 1)
                    nc.vector.memset(xf[0:1, 0, D:], 0.0).then_inc(qscales, 1)
                    dve.wait_ge(qscales, 6 * TPS + 5)

                @block.gpsimd
                def _(pool):
                    nc.gpsimd.memset(half[:, :], -0.5).then_inc(zeroed, 1)
                    for i in range(2):
                        nc.gpsimd.memset(qz[i][:, :, :, :], 0.0).then_inc(zeroed, 1)
                        nc.gpsimd.memset(PT0[i][:, :, :], 0.0).then_inc(zeroed, 1)
                    pool.wait_ge(zeroed, 5)

        def items(eng, steps, turn):
            def at(i):
                return steps(i, i % 2, 0 <= i < ITEMS, 1 <= i <= ITEMS, 2 <= i < ITEMS + 2)

            for i in range(-1, 3):
                turn(at(i), at(i + 1))
            with eng.Fori(0, ITEMS // 2 - 2) as pair:
                three = [steps(2 * pair + 3 + x, (x + 1) % 2, True, True, True) for x in range(3)]
                turn(three[0], three[1])
                turn(three[1], three[2])
            for i in range(ITEMS - 1, ITEMS + 2):
                turn(at(i), at(i + 1))

        with nc.Block() as block:
            @block.sync
            def _(sp):
                def load_qkv(l):
                    need(sp, qkv_made, 12 * SEQS * l)
                    sp.dma_start(Wqkv[:, :], w_qkv[bass.ds(l, 1), :, :].rearrange("a c n -> c (a n)")).then_inc(wqkv_in, 16)

                def load_later(l):
                    need(sp, x_ffn, SEQS * (l - 1))
                    sp.sem_inc(sp_alone, 1)
                    h = bass.ds(l % 2, 1)
                    at = bass.ds(l, 1)
                    sp.dma_start(Wo[:, h, :, :].rearrange("p a j n -> p (a j) n"),
                                 w_o[at, :, :].rearrange("a (j p) n -> p (a j) n", p=P)).then_inc(later_in, 16)
                    sp.dma_start(W1[:, h, :].rearrange("p a n -> p (a n)"),
                                 w_1[at, :, :].rearrange("a c n -> c (a n)")).then_inc(later_in, 16)
                    sp.dma_start(W2[:, h, 0:2, :].rearrange("p a k n -> p (a k) n"),
                                 w_2[at, 0:2 * P, :].rearrange("a (k p) n -> p (a k) n", p=P)).then_inc(later_in, 16)
                    sp.dma_start(W2[0:FK[2], h, 2, :].rearrange("p a n -> p (a n)"),
                                 w_2[at, 2 * P:FF, :].rearrange("a p n -> p (a n)")).then_inc(later_in, 16)
                    sp.dma_start(b1[:, h, :].rearrange("p a n -> p (a n)"),
                                 b_1[at, :].to_broadcast([P, 2 * FF])).then_inc(later_in, 16)
                    sp.dma_start(b2[:, h, :].rearrange("p a n -> p (a n)"),
                                 b_2[at, :].to_broadcast([P, P])).then_inc(later_in, 16)

                def shift(dst, b, done):
                    t = bass.ds(b * TPS, TPS)
                    sp.dma_start(dst[:, :, 0:D], X[:, t, 0:D]).then_inc(done, 16)
                    sp.dma_start(dst[1:P, :, D:], X[0:P - 1, t, D:]).then_inc(done, 16)
                    sp.dma_start(dst[0:1, 1, D:], X[P - 1:P, bass.ds(b * TPS, 1), D:].rearrange("p a c -> p (a c)")
                                 ).then_inc(done, 16)

                def item(i, b, ahead, first=False, layer=None):
                    if not first:
                        sp.wait_ge(x_ffn, i - SEQS + 1)
                        sp.sem_inc(sp_alone, 1)
                    need(sp, turned, i)
                    shift(xs, b, shifted)
                    if layer is not None:
                        load_qkv(layer)
                    if ahead:
                        later(i - 2, (b + SEQS - 2) % SEQS)

                def later(f, b):
                    sp.wait_ge(x_attn, f + 1)
                    sp.sem_inc(sp_alone, 1)
                    need(sp, xn_ready, f)
                    shift(xf, b, shifted2)

                load_qkv(0)
                load_later(0)
                item(0, 0, False, True)
                item(1, 1, False, True)
                item(2, 2, True, True)
                item(3, 3, True, True)
                load_later(1)
                with sp.Fori(4, SEQS) as b:
                    item(b, b, True, True)
                with sp.Fori(1, LAYERS - 1) as l:
                    item(l * SEQS, 0, True, layer=l)
                    with sp.Fori(1, 4) as b:
                        item(l * SEQS + b, b, True)
                    load_later(l + 1)
                    with sp.Fori(4, SEQS) as b:
                        item(l * SEQS + b, b, True)
                item((LAYERS - 1) * SEQS, 0, True, layer=LAYERS - 1)
                with sp.Fori(1, SEQS) as b:
                    item((LAYERS - 1) * SEQS + b, b, True)
                later(ITEMS - 2, SEQS - 2)
                later(ITEMS - 1, SEQS - 1)

            @block.tensor
            def _(pe):
                def steps(i, s, p1, p2, p3):
                    a, f, o = i - 1, i - 2, 1 - s
                    layer = i // SEQS
                    half_o, half_f = bass.ds((a // SEQS) % 2, 1), bass.ds((f // SEQS) % 2, 1)

                    def scores(g, t):
                        if not p2:
                            return
                        u = TPS * (GH * a + g) + t
                        if g == 0 and t == 0:
                            pe.wait_ge(qkT_ready, 8 * a + 8)
                        need(pe, exp_done, u - 1)
                        for ps_, m, heads, width in (((ps_s0, mask0, range(HG), P),) if t == 0 else
                                                     ((ps_s1, mask1, (0, 1), K1), (ps_s2, mask1, (2, 3), K1))):
                            k = len(heads)
                            nc.tensor.matmul(ps_[:, 0:k * width], identb[:, :], m[:, :].unsqueeze(1).to_broadcast([P, k, width]),
                                             start=True, stop=False)
                            for x, h in enumerate(heads):
                                pair, odd = divmod(HG * g + h, 2)
                                ins = nc.tensor.matmul(ps_[:, x * width:x * width + width],
                                                       qz[o][:, pair, odd, t * P:t * P + P],
                                                       kT[o][:, pair, t * (P - WIN):t * (P - WIN) + width],
                                                       start=False, stop=(x == k - 1))
                        ins.then_inc(scored, 1)

                    def turn_probs(g, t):
                        if not p2:
                            return
                        u = TPS * (GH * a + g) + t
                        pe.wait_ge(norm_done, u + 1)
                        if t:
                            pe.wait_ge(pt0_ready, GH * a + g + 1)
                        else:
                            need(pe, pt1_ready, GH * a + g)
                        for h in range(HG):
                            src = P1[g % 2][:, h, WIN:K1] if t else P0[g % 2][:, h, :]
                            ins = nc.tensor.transpose(ps_p[:, h * P:h * P + P], src, ident[:, :])
                        ins.then_inc(pt_turned, 1)

                    def weigh(g):
                        if not p2:
                            return
                        n = GH * a + g
                        pe.wait_ge(pt0_ready, n + 1)
                        pe.wait_ge(pt1_ready, n + 1)
                        pe.wait_ge(bt_done, n + 1)
                        if g == 0:
                            pe.wait_ge(v_ready, 4 * a + 4)
                            need(pe, x_attn, a)
                        need(pe, ot_ready, n)
                        if g == 2 and p3:
                            pe.wait_ge(ffn_part, f + 1)
                        for h in range(HG):
                            head = HG * g + h
                            rows, c0 = slice(D * (h % 2), D * (h % 2) + D), (h // 2) * SEQ
                            nc.tensor.matmul(ps_o[rows, c0:c0 + K1], V[o][:, 0, head * D:head * D + D], PT0[g % 2][:, h, :],
                                             start=True, stop=False, skip_group_check=True)
                            ins = nc.tensor.matmul(ps_o[rows, c0 + P:c0 + SEQ], V[o][:, 1, head * D:head * D + D],
                                                   PT1[g % 2][:, h, :], start=False, stop=True, skip_group_check=True)
                        ins.then_inc(pv_done, 1)

                    def out_proj():
                        if not p2:
                            return
                        pe.wait_ge(later_in, LATER * (a // SEQS + 1))
                        pe.wait_ge(ot_ready, GH * a + GH)
                        for t in range(TPS):
                            for j in range(PAIRS):
                                ins = nc.tensor.matmul(ps_o[:, t * P:t * P + P], oT[:, j, t * P:t * P + P],
                                                       Wo[:, half_o, j, :].rearrange("p a n -> p (a n)"),
                                                       start=(j == 0), stop=(j == PAIRS - 1))
                        ins.then_inc(wo_made, 1)

                    def turn_x():
                        if not p1:
                            return
                        pe.wait_ge(shifted, SHIFT * (i + 1))
                        need(pe, qkT_ready, 8 * i)
                        for t in range(TPS):
                            ins = nc.tensor.transpose(ps_t[:, t * P:t * P + P], xs[:, t, :], ident[:, :])
                        ins.then_inc(turned, 1)

                    def project(j):
                        if not p1:
                            return
                        t, c = divmod(j, 6)
                        if j == 0:
                            pe.wait_ge(sT_ready, i + 1)
                            pe.wait_ge(wqkv_in, 16 * (layer + 1))
                        if j < 2:
                            need(pe, v_ready, 4 * i - 1 + j)
                        elif j in (2, 3):
                            pe.wait_ge(rot_done, 8 * i + j - 1)
                        elif j in (4, 5):
                            pe.wait_ge((gate_ready, lin_ready)[j - 4], 2 * f + 1) if p3 else pe.wait_ge(rot_done, 8 * i + j - 1)
                        elif j in (6, 7):
                            pe.wait_ge((gate_ready, lin_ready)[j - 6], 2 * f + 2) if p3 else pe.wait_ge(v_ready, 4 * i + j - 5)
                        else:
                            pe.wait_ge(rot_done, 8 * i + j - 3)
                        nc.tensor.matmul(ps_w[j % 2][:, :], sT[:, t * P:t * P + P], Wqkv[:, c * CH:c * CH + CH],
                                         start=True, stop=True).then_inc(qkv_made, 1)

                    def turn_qk(j):
                        if not p1:
                            return
                        t, c = divmod(j, 6)
                        m = 8 * i + 4 * t + c
                        if c < 2:
                            pe.wait_ge(roped, m + 1)
                        else:
                            pe.wait_ge(scaled, 2 * (2 * i + t) + c - 1)
                        if j == 0:
                            pe.wait_ge(xnT_ready, f + 1) if p3 else pe.wait_ge(sT_ready, i + 1)
                        elif j in (2, 7) and p3:
                            pe.wait_ge(hT_ready, 2 * f + (1 if j == 2 else 2))
                        else:
                            pe.wait_ge(qkT_ready, m)
                        for x in range(4):
                            ins = nc.tensor.transpose(ps_t[:, x * P:x * P + P], qk[:, c, x * P:x * P + P], ident[:, :])
                        ins.then_inc(qk_turned, 1)

                    def turn_normed():
                        if not p3:
                            return
                        pe.wait_ge(xn_ready, f + 1)
                        if p1:
                            pe.wait_ge(sT_ready, i + 1)
                        else:
                            pe.wait_ge(qkT_ready, 8 * ITEMS)
                            need(pe, hT_ready, 2 * f)
                        for t in range(TPS):
                            ins = nc.tensor.transpose(ps_t[:, t * P:t * P + P], xn[:, t, :], ident[:, :])
                        ins.then_inc(ft_made, 1)

                    def hidden(t, k):
                        if not p3:
                            return
                        if t == 0 and k == 0:
                            pe.wait_ge(xnT_ready, f + 1)
                            pe.wait_ge(later_in, LATER * (f // SEQS + 1))
                        if p1:
                            pe.wait_ge(v_ready, 4 * i + 1 + k) if t else pe.wait_ge(rot_done, 8 * i + 3 + k)
                        else:
                            pe.wait_ge(v_ready, 4 * ITEMS)
                        need(pe, lin_ready if k else gate_ready, 2 * f + t)
                        c0 = FF * (1 - k)
                        nc.tensor.matmul(ps_w[k][:, 0:FF], xnT[:, t * P:t * P + P],
                                         W1[:, half_f, c0:c0 + FF].rearrange("p a n -> p (a n)"),
                                         start=True, stop=True).then_inc(fw_made, 1)

                    def turn_hidden(t):
                        if not p3:
                            return
                        pe.wait_ge(h_ready, 2 * f + t + 1)
                        if p1:
                            pe.wait_ge(qkT_ready, 8 * i + (5 if t else 2))
                        else:
                            pe.wait_ge(hT_ready, 2 * f + 1) if t else pe.wait_ge(xnT_ready, f + 1)
                        for k, rows in enumerate(FK):
                            ins = nc.tensor.transpose(ps_t[0:rows, k * P:k * P + P], hid[:, t, k * P:k * P + rows], ident[:, :])
                        ins.then_inc(ht_made, 1)

                    def ff_out():
                        if not p3:
                            return
                        pe.wait_ge(hT_ready, 2 * f + 2)
                        if p2:
                            pe.wait_ge(ot_ready, GH * a + 2)
                        else:
                            pe.wait_ge(x_attn, ITEMS)
                        for t in range(TPS):
                            for k, rows in enumerate(FK):
                                ins = nc.tensor.matmul(ps_o[:, t * P:t * P + P], hT[0:rows, t, k, :],
                                                       W2[0:rows, half_f, k, :].rearrange("p a n -> p (a n)"),
                                                       start=(k == 0), stop=(k == 2))
                        ins.then_inc(w2_made, 1)

                    step = Steps()
                    step.project, step.scores, step.turn_normed, step.turn_probs = project, scores, turn_normed, turn_probs
                    step.hidden, step.turn_qk, step.weigh, step.turn_hidden = hidden, turn_qk, weigh, turn_hidden
                    step.ff_out, step.turn_x, step.out_proj = ff_out, turn_x, out_proj
                    return step

                def turn(now, new):
                    now.project(3)
                    now.scores(2, 1)
                    now.turn_normed()
                    now.turn_probs(1, 0)
                    now.hidden(0, 0)
                    now.hidden(0, 1)
                    now.project(4)
                    now.turn_qk(0)
                    now.project(5)
                    now.hidden(1, 0)
                    now.hidden(1, 1)
                    now.project(6)
                    now.turn_qk(1)
                    now.project(7)
                    now.weigh(0)
                    now.turn_hidden(0)
                    now.turn_probs(1, 1)
                    now.project(8)
                    now.scores(3, 0)
                    now.turn_qk(2)
                    now.project(9)
                    now.turn_qk(3)
                    now.scores(3, 1)
                    now.turn_qk(6)
                    now.turn_probs(2, 0)
                    now.weigh(1)
                    now.turn_hidden(1)
                    now.project(10)
                    now.turn_probs(2, 1)
                    now.turn_qk(7)
                    now.ff_out()
                    now.project(11)
                    now.turn_qk(8)
                    now.turn_probs(3, 0)
                    now.weigh(2)
                    now.turn_qk(9)
                    now.turn_probs(3, 1)
                    new.scores(0, 0)
                    new.turn_x()
                    new.scores(0, 1)
                    new.project(0)
                    now.weigh(3)
                    new.scores(1, 0)
                    now.out_proj()
                    new.turn_probs(0, 0)
                    new.scores(1, 1)
                    new.project(1)
                    new.project(2)
                    new.turn_probs(0, 1)
                    new.scores(2, 0)

                items(pe, steps, turn)

            @block.scalar
            def _(act):
                def steps(i, s, p1, p2, p3):
                    a, f, o = i - 1, i - 2, 1 - s

                    def expo(g, t):
                        if not p2:
                            return
                        n, k = GH * a + g, g % 2
                        u = TPS * n + t
                        act.wait_ge(nm_ready, u + 1)
                        need(act, pt_turned, u - 3)
                        if t:
                            need(act, bt_done, n - 1)
                        for h in range(HG):
                            if t == 0:
                                src, dst = ps_s0[:, h * P:h * P + P], P0[k][:, h, :]
                            else:
                                x = (h % 2) * K1
                                src, dst = (ps_s2 if h >= 2 else ps_s1)[:, x:x + K1], P1[k][:, h, :]
                            ins = nc.scalar.activation(dst, src, ACT.Exp, bias=nbias[k][:, t, h:h + 1],
                                                       scale=sc8[o][:, t, HG * g + h:HG * g + h + 1],
                                                       accum_out=den[k][:, t, h:h + 1])
                        ins.then_inc(exp_done, 1)

                    def keep_probs_1(g):
                        if not p2:
                            return
                        n, k = GH * a + g, g % 2
                        act.wait_ge(pt_turned, TPS * n + 2)
                        need(act, pv_done, n - 1)
                        nc.scalar.copy(PT1[k][:, :, :], ps_p[:, :].rearrange("p (h q) -> p h q", h=HG)
                                       ).then_inc(pt1_ready, 1)

                    def outputs(g):
                        if not p2:
                            return
                        n = GH * a + g
                        act.wait_ge(pv_done, n + 1)
                        if g == 0:
                            need(act, wo_made, a)
                        nc.scalar.copy(oT[:, 2 * g:2 * g + 2, :], ps_o[:, :].rearrange("p (j q) -> p j q", j=2)).then_inc(ot_ready, 1)

                    def channels():
                        if not p1:
                            return
                        act.wait_ge(turned, i + 1)
                        need(act, qkv_made, 12 * i)
                        nc.scalar.copy(sT[:, :], ps_t[:, 0:SEQ]).then_inc(sT_ready, 1)

                    def squares(j):
                        if not p1:
                            return
                        t, c = divmod(j, 6)
                        m = 8 * i + 4 * t + c
                        act.wait_ge(qkv_made, 12 * i + j + 1)
                        need(act, n2_made, m - 1)
                        nc.scalar.activation(sq[c % 2][:, :], ps_w[j % 2][:, :], ACT.Square).then_inc(sq_done, 1)

                    def values(j):
                        if not p1:
                            return
                        t, c = divmod(j, 6)
                        act.wait_ge(qkv_made, 12 * i + j + 1)
                        need(act, pv_done, GH * (i - 1))
                        nc.scalar.copy(V[s][:, t, (c - 4) * CH:(c - 3) * CH], ps_w[j % 2][:, :]).then_inc(v_ready, 1)

                    def keep_qk(j):
                        if not p1:
                            return
                        t, c = divmod(j, 6)
                        m = 8 * i + 4 * t + c
                        act.wait_ge(qk_turned, m + 1)
                        if c == 0:
                            need(act, scored, TPS * GH * (i - 1))
                        src = ps_t[:, :].rearrange("p (j q) -> p j q", j=4)
                        pairs, cols = slice(4 * (c % 2), 4 * (c % 2) + 4), slice(t * P, t * P + P)
                        if c < 2:
                            nc.scalar.copy(qz[s][0:D, pairs, 0, cols], src[0:D])
                            ins = nc.scalar.copy(qz[s][D:P, pairs, 1, cols], src[D:P])
                        else:
                            ins = nc.scalar.copy(kT[s][:, pairs, cols], src)
                        ins.then_inc(qkT_ready, 1)

                    def ff_input():
                        if not p3:
                            return
                        act.wait_ge(ft_made, f + 1)
                        need(act, fw_made, 4 * f)
                        l = bass.ds(f // SEQS, 1)
                        nc.scalar.activation(xnT[:, :], ps_t[:, 0:SEQ], ACT.Identity, bias=offset[:, l], scale=gain[:, l]
                                             ).then_inc(xnT_ready, 1)

                    def gelu(t):
                        if not p3:
                            return
                        act.wait_ge(gate_ready, 2 * f + t + 1)
                        need(act, h_ready, 2 * f + t)
                        nc.scalar.activation(gated[:, :], gate[:, :], ACT.Gelu).then_inc(gelu_done, 1)

                    step = Steps()
                    step.squares, step.keep_probs_1, step.ff_input, step.expo = squares, keep_probs_1, ff_input, expo
                    step.gelu, step.values, step.keep_qk, step.outputs = gelu, values, keep_qk, outputs
                    step.channels = channels
                    return step

                def turn(now, new):
                    now.squares(3)
                    now.keep_probs_1(0)
                    now.ff_input()
                    now.expo(2, 0)
                    now.gelu(0)
                    now.values(4)
                    now.values(5)
                    now.keep_qk(0)
                    now.gelu(1)
                    now.squares(6)
                    now.keep_qk(1)
                    now.squares(7)
                    now.expo(2, 1)
                    now.squares(8)
                    now.keep_qk(2)
                    now.outputs(0)
                    now.squares(9)
                    now.keep_qk(3)
                    now.keep_probs_1(1)
                    now.keep_qk(6)
                    now.expo(3, 0)
                    now.outputs(1)
                    now.keep_probs_1(2)
                    now.keep_qk(7)
                    now.expo(3, 1)
                    now.keep_qk(8)
                    now.keep_qk(9)
                    now.outputs(2)
                    now.values(10)
                    now.keep_probs_1(3)
                    new.channels()
                    now.values(11)
                    new.expo(0, 0)
                    new.squares(0)
                    now.outputs(3)
                    new.expo(0, 1)
                    new.expo(1, 0)
                    new.squares(1)
                    new.expo(1, 1)
                    new.squares(2)

                items(act, steps, turn)

            @block.vector
            def _(dve):
                def steps(i, s, p1, p2, p3):
                    a, f, o = i - 1, i - 2, 1 - s
                    layer = bass.ds(min(i // SEQS, LAYERS - 1) if isinstance(i, int) else i // SEQS, 1)

                    def maxima(g, t):
                        if not p2:
                            return
                        n, k = GH * a + g, g % 2
                        u = TPS * n + t
                        dve.wait_ge(scored, u + 1)
                        if t == 0:
                            ins = nc.vector.tensor_reduce(nmax[k][:, 0, :], ps_s0[:, :].rearrange("p (h k) -> p h k", h=HG),
                                                          AX_X, ALU.max, negate=True)
                        else:
                            for x, src in ((0, ps_s1), (2, ps_s2)):
                                ins = nc.vector.tensor_reduce(nmax[k][:, 1, x:x + 2],
                                                              src[:, 0:2 * K1].rearrange("p (h k) -> p h k", h=2),
                                                              AX_X, ALU.max, negate=True)
                        ins.then_inc(maxed, 1)

                    def shift_of(g, t):
                        if not p2:
                            return
                        k = g % 2
                        u = TPS * (GH * a + g) + t
                        dve.wait_ge(maxed, u + 1)
                        need(dve, exp_done, u - 3)
                        if g == 0:
                            dve.wait_ge(sc_ready, 2 * a + t + 1)
                        nc.vector.tensor_tensor(nbias[k][:, t, :], nmax[k][:, t, :], sc8[o][:, t, HG * g:HG * g + HG],
                                                ALU.mult).then_inc(nm_ready, 1)

                    def invert(g, t):
                        if not p2:
                            return
                        k = g % 2
                        u = TPS * (GH * a + g) + t
                        dve.wait_ge(exp_done, u + 1)
                        nc.vector.reciprocal(den[k][:, t, :], den[k][:, t, :]).then_inc(inverted, 1)

                    def normalise(g, t):
                        if not p2:
                            return
                        k = g % 2
                        u = TPS * (GH * a + g) + t
                        dve.wait_ge(inverted, u + 1)
                        probs, width = (P1[k], K1) if t else (P0[k], P)
                        nc.vector.tensor_tensor(probs[:, :, :], probs[:, :, :],
                                                den[k][:, t, :].unsqueeze(2).to_broadcast([P, HG, width]), ALU.mult
                                                ).then_inc(norm_done, 1)

                    def turn_back(g):
                        if not p2:
                            return
                        n, k = GH * a + g, g % 2
                        dve.wait_ge(norm_done, TPS * n + 2)
                        need(dve, pv_done, n - 1)
                        nc.vector.transpose(PT0[k][P - WIN:P, :, P:K1], P1[k][0:WIN, :, 0:WIN]).then_inc(bt_done, 1)

                    def keep_probs_0(g):
                        if not p2:
                            return
                        n, k = GH * a + g, g % 2
                        dve.wait_ge(pt_turned, TPS * n + 1)
                        need(dve, pv_done, n - 1)
                        nc.vector.tensor_copy(PT0[k][:, :, 0:P], ps_p[:, :].rearrange("p (h q) -> p h q", h=HG)
                                              ).then_inc(pt0_ready, 1)

                    def add_attention():
                        if not p2:
                            return
                        dve.wait_ge(wo_made, a + 1)
                        rows = X[:, bass.ds((a % SEQS) * TPS, TPS), :]
                        nc.vector.tensor_tensor(rows, rows, ps_o[:, 0:SEQ].rearrange("p (t c) -> p t c", t=TPS),
                                                ALU.add).then_inc(x_attn, 1)

                    def rotate(j):
                        if not p1:
                            return
                        t, c = divmod(j, 6)
                        m, x = 8 * i + 4 * t + c, c // 2
                        k = c % 2
                        dve.wait_ge(sq_done, m + 1)
                        need(dve, roped, m - 1)
                        src = ps_w[j % 2][:, :].rearrange("p (h a e) -> p h a e", h=HC, a=2)
                        table = lambda v: v[x][:, layer, t, :].to_broadcast([P, HC, D])
                        nc.vector.tensor_tensor(t1[k][:, :].rearrange("p (h e) -> p h e", h=HC),
                                                ps_w[j % 2][:, :].rearrange("p (h e) -> p h e", h=HC), table(own), ALU.mult)
                        nc.vector.tensor_tensor(t2[k][:, :].rearrange("p (h a e) -> p h a e", h=HC, a=2), src[:, :, ::-1, :],
                                                table(cross).rearrange("p h (a e) -> p h a e", a=2), ALU.mult
                                                ).then_inc(rot_done, 1)

                    def sum_squares(j):
                        if not p1:
                            return
                        t, c = divmod(j, 6)
                        m = 8 * i + 4 * t + c
                        dve.wait_ge(sq_done, m + 1)
                        if c % 2 == 0:
                            need(dve, clamped, 2 * (2 * i + t) + c // 2 - 3)
                        nc.vector.tensor_reduce(n2[:, t, HC * c:HC * c + HC],
                                                sq[c % 2][:, :].rearrange("p (h e) -> p h e", h=HC),
                                                AX_X, ALU.add).then_inc(n2_made, 1)

                    def clamp(t, x):
                        if not p1:
                            return
                        n, heads = 2 * i + t, slice(H * x, H * x + H)
                        dve.wait_ge(n2_made, 8 * i + 4 * t + 2 * x + 2)
                        need(dve, powed, 2 * n + x - 3)
                        nc.vector.tensor_scalar(clampd[:, t, heads], n2[:, t, heads], 1e-24, None, ALU.max).then_inc(clamped, 1)

                    def q_factor(t):
                        if not p1:
                            return
                        dve.wait_ge(powed, 2 * (2 * i + t) + 1)
                        need(dve, exp_done, TPS * GH * (i - 1))
                        nc.vector.tensor_scalar(sc8[s][:, t, :], rn[:, t, 0:H], 8.0, None, ALU.mult).then_inc(sc_ready, 1)

                    def ff_stats():
                        if not p3:
                            return
                        dve.wait_ge(shifted2, SHIFT * (f + 1))
                        for t in range(TPS):
                            nc.vector.bn_stats(stats[:, t, :], xf[:, t, :]).then_inc(bn_done, 1)
                        dve.wait_ge(bn_done, TPS * (f + 1))
                        dve.sem_inc(dve_alone, 1)
                        for t in range(TPS):
                            nc.vector.bn_aggr(mv[:, t, :], stats[:, t, :]).then_inc(aggr_done, 1)
                        dve.wait_ge(aggr_done, TPS * (f + 1))
                        nc.vector.tensor_scalar(var[:, :], mv[:, :, 1], EPS, None, ALU.add).then_inc(var_ready, 1)

                    def ff_norm():
                        if not p3:
                            return
                        dve.wait_ge(rstd_ready, f + 1)
                        need(dve, ft_made, f)
                        for t in range(TPS):
                            ins = nc.vector.tensor_scalar(xn[:, t, :], xf[:, t, :], mv[:, t, 0:1], rstd[:, t:t + 1],
                                                          ALU.subtract, ALU.mult)
                        ins.then_inc(xn_ready, 1)

                    def bias_1(t, k):
                        if not p3:
                            return
                        n, hf = 2 * f + t, bass.ds((f // SEQS) % 2, 1)
                        if t == 0 and k == 0:
                            dve.wait_ge(later_in, LATER * (f // SEQS + 1))
                        dve.wait_ge(fw_made, 2 * n + k + 1)
                        bias = lambda c0: b1[:, hf, c0:c0 + FF].rearrange("p a n -> p (a n)")
                        if k == 0:
                            need(dve, gelu_done, n)
                            nc.vector.tensor_tensor(gate[:, :], ps_w[0][:, 0:FF], bias(FF), ALU.add).then_inc(gate_ready, 1)
                        else:
                            need(dve, h_ready, n)
                            nc.vector.tensor_tensor(lin[:, :], ps_w[1][:, 0:FF], bias(0), ALU.add).then_inc(lin_ready, 1)

                    def multiply(t):
                        if not p3:
                            return
                        n = 2 * f + t
                        dve.wait_ge(gelu_done, n + 1)
                        dve.wait_ge(lin_ready, n + 1)
                        need(dve, ht_made, n - 1)
                        nc.vector.tensor_tensor(hid[:, t, :], lin[:, :], gated[:, :], ALU.mult).then_inc(h_ready, 1)

                    def keep_hidden(t):
                        if not p3:
                            return
                        n = 2 * f + t
                        dve.wait_ge(ht_made, n + 1)
                        need(dve, w2_made, f)
                        nc.vector.tensor_copy(hT[:, t, 0:2, :], ps_t[:, 0:2 * P].rearrange("p (k q) -> p k q", k=2))
                        nc.vector.tensor_copy(hT[0:FK[2], t, 2, :], ps_t[0:FK[2], 2 * P:3 * P]).then_inc(hT_ready, 1)

                    def add_ff():
                        if not p3:
                            return
                        dve.wait_ge(w2_made, f + 1)
                        rows = X[:, bass.ds((f % SEQS) * TPS, TPS), :]
                        nc.vector.tensor_tensor(rows, rows, ps_o[:, 0:SEQ].rearrange("p (t c) -> p t c", t=TPS),
                                                ALU.add).then_inc(ffn_part, 1)
                        dve.wait_ge(ffn_part, f + 1)
                        nc.vector.tensor_tensor(rows, rows, b2[:, bass.ds((f // SEQS) % 2, 1), :].to_broadcast([P, TPS, P]),
                                                ALU.add).then_inc(x_ffn, 1)

                    step = Steps()
                    step.maxima, step.ff_norm, step.shift_of, step.clamp = maxima, ff_norm, shift_of, clamp
                    step.rotate, step.bias_1, step.sum_squares, step.invert = rotate, bias_1, sum_squares, invert
                    step.keep_probs_0, step.multiply, step.normalise, step.keep_hidden = keep_probs_0, multiply, normalise, keep_hidden
                    step.q_factor, step.turn_back, step.add_ff, step.add_attention = q_factor, turn_back, add_ff, add_attention
                    step.ff_stats = ff_stats
                    return step

                def turn(now, new):
                    now.maxima(2, 0)
                    now.ff_norm()
                    now.shift_of(2, 0)
                    now.clamp(0, 0)
                    now.rotate(2)
                    now.rotate(3)
                    now.bias_1(0, 0)
                    now.sum_squares(2)
                    now.invert(1, 1)
                    now.bias_1(0, 1)
                    now.sum_squares(3)
                    now.maxima(2, 1)
                    now.clamp(0, 1)
                    now.keep_probs_0(1)
                    now.multiply(0)
                    now.bias_1(1, 0)
                    now.invert(2, 0)
                    now.normalise(1, 1)
                    now.bias_1(1, 1)
                    now.normalise(2, 0)
                    now.shift_of(2, 1)
                    now.rotate(6)
                    now.sum_squares(6)
                    now.sum_squares(7)
                    now.keep_hidden(0)
                    now.clamp(1, 0)
                    now.rotate(7)
                    now.maxima(3, 0)
                    now.invert(2, 1)
                    now.q_factor(0)
                    now.sum_squares(8)
                    now.shift_of(3, 0)
                    now.normalise(2, 1)
                    now.sum_squares(9)
                    now.clamp(1, 1)
                    now.turn_back(1)
                    now.multiply(1)
                    now.rotate(8)
                    now.keep_probs_0(2)
                    now.keep_hidden(1)
                    now.rotate(9)
                    now.invert(3, 0)
                    now.maxima(3, 1)
                    now.shift_of(3, 1)
                    now.turn_back(2)
                    now.normalise(3, 0)
                    now.add_ff()
                    now.keep_probs_0(3)
                    now.invert(3, 1)
                    now.normalise(3, 1)
                    new.maxima(0, 0)
                    new.shift_of(0, 0)
                    now.turn_back(3)
                    now.q_factor(1)
                    new.maxima(0, 1)
                    new.shift_of(0, 1)
                    new.invert(0, 0)
                    new.sum_squares(0)
                    new.maxima(1, 0)
                    new.rotate(0)
                    new.shift_of(1, 0)
                    new.invert(0, 1)
                    new.normalise(0, 0)
                    new.normalise(0, 1)
                    now.add_attention()
                    new.keep_probs_0(0)
                    new.invert(1, 0)
                    new.normalise(1, 0)
                    new.turn_back(0)
                    new.maxima(1, 1)
                    new.shift_of(1, 1)
                    new.rotate(1)
                    new.ff_stats()
                    new.sum_squares(1)

                items(dve, steps, turn)
                dve.wait_ge(x_ffn, ITEMS)

            @block.gpsimd
            def _(pool):
                def steps(i, s, p1, p2, p3):
                    f = i - 2

                    def add(j):
                        if not p1:
                            return
                        t, c = divmod(j, 6)
                        m, k = 8 * i + 4 * t + c, c % 2
                        pool.wait_ge(rot_done, m + 1)
                        need(pool, qk_turned, m - 3)
                        nc.gpsimd.tensor_tensor(qk[:, c, :], t1[k][:, :], t2[k][:, :], ALU.add).then_inc(roped, 1)

                    def norms(t, x):
                        if not p1:
                            return
                        n, heads = 2 * i + t, slice(H * x, H * x + H)
                        pool.wait_ge(clamped, 2 * n + x + 1)
                        if x == 0:
                            need(pool, sc_ready, n - 1)
                        else:
                            need(pool, scaled, 2 * n - 2)
                        nc.gpsimd.tensor_tensor(rn[:, t, heads], clampd[:, t, heads], half[:, heads], ALU.pow).then_inc(powed, 1)

                    def scale_k(j):
                        if not p1:
                            return
                        t, c = divmod(j, 6)
                        pool.wait_ge(powed, 2 * (2 * i + t) + 2)
                        pool.wait_ge(roped, 8 * i + 4 * t + c + 1)
                        v = qk[:, c, :].rearrange("p (h e) -> p h e", h=HC)
                        nc.gpsimd.tensor_tensor(v, v, rn[:, t, HC * c:HC * c + HC].unsqueeze(2).to_broadcast([P, HC, D]),
                                                ALU.mult).then_inc(scaled, 1)

                    def ff_rstd():
                        if not p3:
                            return
                        pool.wait_ge(var_ready, f + 1)
                        need(pool, xn_ready, f)
                        nc.gpsimd.tensor_tensor(rstd[:, :], var[:, :], half[:, 0:TPS], ALU.pow).then_inc(rstd_ready, 1)

                    step = Steps()
                    step.norms, step.add, step.scale_k, step.ff_rstd = norms, add, scale_k, ff_rstd
                    return step

                def turn(now, new):
                    now.norms(0, 0)
                    now.add(2)
                    now.add(3)
                    now.norms(0, 1)
                    now.scale_k(2)
                    now.scale_k(3)
                    now.add(6)
                    now.norms(1, 0)
                    now.add(7)
                    now.norms(1, 1)
                    now.add(8)
                    now.scale_k(8)
                    now.add(9)
                    now.scale_k(9)
                    new.add(0)
                    new.ff_rstd()
                    new.add(1)

                items(pool, steps, turn)
        sem.clear()


def normalise_all(nc, X, store):
    with ExitStack() as ctx:
        mean = ctx.enter_context(nc.sbuf_tensor("n_mean", [P, TILES], F32))
        rstd = ctx.enter_context(nc.sbuf_tensor("n_rstd", [P, TILES], F32))
        stored = ctx.enter_context(nc.semaphore("n_stored"))
        normed = ctx.enter_context(nc.semaphore("n_normed"))
        layernorm_stats(nc, X, mean, rstd, "n")
        with nc.Block() as block:
            @block.sync
            def _(sp):
                sp.dma_start(store, X[:, :, :]).then_inc(stored, 16)

            @block.vector
            def _(dve):
                dve.wait_ge(stored, 16)
                with dve.Fori(0, TILES // 8) as r:
                    for k in range(8):
                        t = bass.ds(8 * r + k, 1)
                        row = X[:, t, :].rearrange("p a c -> p (a c)")
                        nc.vector.tensor_scalar(row, row, mean[:, t], rstd[:, t],
                                                ALU.subtract, ALU.mult).then_inc(normed, 1)
                dve.wait_ge(normed, TILES)


def add_and_store(nc, X, store, out):
    PARTS = 4
    N = TILES // PARTS
    with ExitStack() as ctx:
        held = ctx.enter_context(nc.sbuf_tensor("f_held", [P, TILES, P], F32))
        back = [ctx.enter_context(nc.semaphore(f"f_back{i}")) for i in range(PARTS)]
        added = ctx.enter_context(nc.semaphore("f_added"))
        written = ctx.enter_context(nc.semaphore("f_written"))
        with nc.Block() as block:
            @block.sync
            def _(sp):
                for i in range(PARTS):
                    at = slice(i * N, i * N + N)
                    sp.dma_start(held[:, at, :], store[:, at, :]).then_inc(back[i], 16)
                for i in range(PARTS):
                    at = slice(i * N, i * N + N)
                    sp.wait_ge(added, i + 1)
                    sp.dma_start(out[:, at, :], X[:, at, :]).then_inc(written, 16)
                sp.wait_ge(written, 16 * PARTS)

            @block.vector
            def _(dve):
                for i in range(PARTS):
                    at = slice(i * N, i * N + N)
                    dve.wait_ge(back[i], 16)
                    nc.vector.tensor_tensor(X[:, at, :], X[:, at, :], held[:, at, :], ALU.add).then_inc(added, 1)


def mamba_moe_attention_local(nc, a):
    tiles = lambda v: v.rearrange("s (t p) c -> p (s t) c", p=P)
    with ExitStack() as ctx:
        X = ctx.enter_context(nc.sbuf_tensor("X", [P, TILES, P], F32))
        store = nc.dram_tensor("store", [P, TILES, P], F32).ap()
        x_in = ctx.enter_context(nc.semaphore("x_in"))
        ident = identity(nc, ctx)
        with nc.Block() as block:
            @block.sync
            def _(sp):
                sp.dma_start(X[:, :, :], tiles(a["x"])).then_inc(x_in, 16)
                sp.wait_ge(x_in, 16)
        selective_scan(nc, X, ident, a["in_w"], a["conv_w"], a["conv_b"], a["xp_w"], a["dt_w"], a["dt_b"],
                       a["a_log"], a["d_skip"], a["out_w"])
        expert_layer(nc, X, ident, a["gate_w"], a["e_w1"], a["e_b1"], a["e_w2"], a["e_b2"])
        full_attention(nc, X, ident, a["w_q"], a["b_q"], a["w_k"], a["b_k"], a["w_v"], a["b_v"], a["w_o"], a["b_o"],
                       a["table"])
        normalise_all(nc, X, store)
        local_layers(nc, X, ident, a["w_qkv"], a["q_scale"], a["k_scale"], a["l_wo"], a["ln_g"], a["ln_b"],
                     a["l_w1"], a["l_b1"], a["l_w2"], a["l_b2"], a["rotary"], a["masks"])
        add_and_store(nc, X, store, tiles(a["out"]))


def _rotary():
    import numpy as np
    dim, window, f = 64, 32, np.float32
    half = np.arange(0, dim, 2, dtype=f)
    inv_freq = (f(1.0) / f(10000.0) ** (half / f(dim))).astype(f)
    t = np.arange(SEQ, dtype=f)
    freqs = t[:, None] * inv_freq[None, :]
    freqs = np.concatenate([freqs, freqs], -1)
    base = (half + f(0.4 * dim)) / f(1.4 * dim)
    scale = base[None, :] ** ((t - SEQ // 2) / f(window // 2))[:, None]
    scale = np.concatenate([scale, scale], -1)
    sign = np.concatenate([-np.ones(dim // 2, f), np.ones(dim // 2, f)])
    cos, sin = np.cos(freqs), np.sin(freqs) * sign
    return np.stack([cos * scale, sin * scale, cos / scale, sin / scale], 1).astype(f)


def _masks():
    import numpy as np
    window, out = 32, []
    for tile, keys in ((0, np.arange(P)), (1, np.arange(P - window, 2 * P))):
        q, k = np.arange(P)[:, None] + P * tile, keys[None, :]
        sees = (k <= q) & (k >= q - window) & (k // window >= q // window - 1)
        out.append(np.where(sees, 0.0, -1e30))
    return np.concatenate(out, 1).astype(np.float32)


def kernel(**inputs):
    import numpy as _np
    import concourse.bacc as _bacc
    from concourse import mybir as _mybir
    from concourse.bass_utils import run_bass_kernel_spmd as _run

    given = {k: _np.asarray(v) for k, v in inputs.items()}
    turned = lambda name, *order: given[name].transpose(order)
    table = given["L1_attn_rel_table"]
    far = _np.broadcast_to(table[-1:], (2 * SEQ - 1 - table.shape[0], table.shape[1]))
    data = {
        "x": given["L0_attn_x"],
        "in_w": turned("L0_attn_in_proj_w", 0, 2, 1), "conv_w": given["L0_attn_conv_w"],
        "conv_b": given["L0_attn_conv_b"], "xp_w": turned("L0_attn_x_proj_w", 0, 2, 1),
        "dt_w": turned("L0_attn_dt_proj_w", 0, 2, 1), "dt_b": given["L0_attn_dt_proj_b"],
        "a_log": given["L0_attn_A_log"], "d_skip": given["L0_attn_D"], "out_w": turned("L0_attn_out_proj_w", 0, 2, 1),
        "gate_w": turned("L0_ffn_gate_w", 1, 0), "e_w1": turned("L0_ffn_w1", 0, 2, 1),
        "e_b1": turned("L0_ffn_b1", 1, 0), "e_w2": turned("L0_ffn_w2", 0, 2, 1), "e_b2": given["L0_ffn_b2"],
        "w_q": given["L1_attn_Wq"], "b_q": given["L1_attn_bq"], "w_k": given["L1_attn_Wk"], "b_k": given["L1_attn_bk"],
        "w_v": given["L1_attn_Wv"], "b_v": given["L1_attn_bv"], "w_o": given["L1_attn_Wo"], "b_o": given["L1_attn_bo"],
        "table": _np.concatenate([table, far], 0).T,
        "w_qkv": given["L1_ffn_Wqkv"], "q_scale": given["L1_ffn_q_scale"], "k_scale": given["L1_ffn_k_scale"],
        "l_wo": given["L1_ffn_Wo"], "ln_g": given["L1_ffn_ln_g"], "ln_b": given["L1_ffn_ln_b"],
        "l_w1": given["L1_ffn_W1"], "l_b1": given["L1_ffn_b1"], "l_w2": given["L1_ffn_W2"], "l_b2": given["L1_ffn_b2"],
        "rotary": _rotary(), "masks": _masks(),
    }
    nc = _bacc.Bacc("TRN2", target_bir_lowering=False, num_devices=1)
    arrays, tensors = {}, {}
    for name, v in data.items():
        v = _np.ascontiguousarray(v)
        arrays[f"in_{name}_dram"] = v
        tensors[name] = nc.dram_tensor(f"in_{name}_dram", v.shape, _mybir.dt.from_np(v.dtype), kind="ExternalInput").ap()
    tensors["out"] = nc.dram_tensor("out_0_dram", (SEQS, SEQ, P), F32, kind="ExternalOutput").ap()
    mamba_moe_attention_local(nc, tensors)
    r = _run(nc, [arrays], core_ids=[0])
    return r.results[0]["out_0_dram"]
```
